# Optimizing a Trainium2 kernel written in Bass

```python
import numpy as np
import jax
import jax.numpy as jnp

def _softmax(x, axis=-1):
    return jax.nn.softmax(x, axis=axis)

def _gelu(x):
    return jax.nn.gelu(x, approximate=True)

def _silu(x):
    return jax.nn.silu(x)

def _sigmoid(x):
    return jax.nn.sigmoid(x)

def _layernorm(x, axis=-1, eps=1e-05):
    m = jnp.mean(x, axis=axis, keepdims=True)
    v = jnp.var(x, axis=axis, keepdims=True)
    return (x - m) / jnp.sqrt(v + eps)

def _scatter_add(tgt, idx, src, axis=0):
    return tgt.at[idx].add(src)

def _segment_sum(src, seg, n):
    return jax.ops.segment_sum(src, seg, n)
kernel_name = 'mk_early_fusion_d1_tok_img768_r4_62c36d'

def setup_inputs(seed: int=0):
    np.random.seed(seed)
    _w = jnp.asarray

    def _rec_inputs():
        import jax
        import jax.numpy as jnp
        _rk = jax.random.key(seed)
        x = -7.10856e-05 + 0.999911 * jax.random.normal(jax.random.fold_in(_rk, 1), (4, 32, 128, 128), jnp.float32)
        txt = -0.00271877 + 0.451779 * jax.random.normal(jax.random.fold_in(_rk, 2), (4, 128, 192), jnp.float32)
        return (x, txt)
    x, txt = _rec_inputs()

    def _L0_tok_setup():
        import jax, jax.numpy as jnp
        import numpy as np
        B, C, H, W = (8, 32, 128, 128)
        P = 8
        D = 128
        NH, DH = (8, 64)
        M = 512
        L = 2
        DOUT = 192
        INNER = NH * DH

        def _ln(x, g, b, eps=1e-05):
            mu = x.mean(-1, keepdims=True)
            xc = x - mu
            var = (xc * xc).mean(-1, keepdims=True)
            return xc * jax.lax.rsqrt(var + eps) * g + b

        def _forward(im, conv_w, conv_b, ln1_g, ln1_b, qkv_w, out_w, out_b, ln2_g, ln2_b, ff1_w, ff1_b, ff2_w, ff2_b, lnf_g, lnf_b, head_w, head_b):
            b, c, h, w = im.shape
            hp, wp = (h // P, w // P)
            patches = im.reshape(b, c, hp, P, wp, P)
            x = jnp.einsum('bchpwq,dcpq->bhwd', patches, conv_w)
            x = x.reshape(b, hp * wp, -1) + conv_b
            n = hp * wp
            scale = DH ** (-0.5)
            for i in range(ln1_g.shape[0]):
                y = _ln(x, ln1_g[i], ln1_b[i])
                qkv = y @ qkv_w[i]
                q, k, v = jnp.split(qkv, 3, axis=-1)
                to_heads = lambda t: t.reshape(b, n, NH, DH).transpose(0, 2, 1, 3)
                q, k, v = (to_heads(q), to_heads(k), to_heads(v))
                q = jax.nn.softmax(q, axis=-1) * scale
                k = jax.nn.softmax(k, axis=-2)
                ctx = jnp.einsum('bhnd,bhne->bhde', k, v)
                att = jnp.einsum('bhnd,bhde->bhne', q, ctx)
                att = att.transpose(0, 2, 1, 3).reshape(b, n, INNER)
                x = x + att @ out_w[i] + out_b[i]
                y = _ln(x, ln2_g[i], ln2_b[i])
                hdn = jax.nn.gelu(y @ ff1_w[i] + ff1_b[i], approximate=False)
                x = x + hdn @ ff2_w[i] + ff2_b[i]
            return _ln(x, lnf_g, lnf_b) @ head_w + head_b
        key = jax.random.key(seed)
        ks = iter(jax.random.split(key, 32))
        g = lambda shape, s=0.02: (jax.random.normal(next(ks), shape) * s).astype(jnp.float32)
        inp = {'im': jax.random.normal(next(ks), (B, C, H, W), dtype=jnp.float32), 'conv_w': g((D, C, P, P)), 'conv_b': jnp.zeros((D,), jnp.float32), 'ln1_g': jnp.ones((L, D), jnp.float32), 'ln1_b': jnp.zeros((L, D), jnp.float32), 'qkv_w': g((L, D, 3 * INNER)), 'out_w': g((L, INNER, D)), 'out_b': jnp.zeros((L, D), jnp.float32), 'ln2_g': jnp.ones((L, D), jnp.float32), 'ln2_b': jnp.zeros((L, D), jnp.float32), 'ff1_w': g((L, D, M)), 'ff1_b': jnp.zeros((L, M), jnp.float32), 'ff2_w': g((L, M, D)), 'ff2_b': jnp.zeros((L, D), jnp.float32), 'lnf_g': jnp.ones((D,), jnp.float32), 'lnf_b': jnp.zeros((D,), jnp.float32), 'head_w': g((D, DOUT)), 'head_b': jnp.zeros((DOUT,), jnp.float32)}
        return inp
    _L0_tok_all = _L0_tok_setup()
    _L0_tok_in = {k: v for k, v in _L0_tok_all.items() if k in ('conv_w', 'conv_b', 'ln1_g', 'ln1_b', 'qkv_w', 'out_w', 'out_b', 'ln2_g', 'ln2_b', 'ff1_w', 'ff1_b', 'ff2_w', 'ff2_b', 'lnf_g', 'lnf_b', 'head_w', 'head_b')}
    del _L0_tok_all

    def _L0_attn_setup():
        import jax, jax.numpy as jnp
        import numpy as np
        B, S, H, NH = (1, 512, 192, 12)
        HD = H // NH
        key = jax.random.key(seed)
        k0, k1, k2, k3 = jax.random.split(key, 4)
        BN = B * S
        return {'hidden_states': jax.random.normal(k0, (B, S, H), dtype=jnp.float32), 'g': jax.random.uniform(k1, (BN, BN), dtype=jnp.float32), 'attention_mask': jnp.zeros((B, S), dtype=jnp.float32), 'Wq': jax.random.normal(k2, (H, H), dtype=jnp.float32) * 0.02, 'bq': jnp.zeros((H,), dtype=jnp.float32), 'Wv': jax.random.normal(k3, (H, H), dtype=jnp.float32) * 0.02, 'bv': jnp.zeros((H,), dtype=jnp.float32)}
    _L0_attn_all = _L0_attn_setup()
    _L0_attn_in = {k: v for k, v in _L0_attn_all.items() if k in ('g', 'attention_mask', 'Wq', 'bq', 'Wv', 'bv')}
    del _L0_attn_all

    def _L0_ffn_setup():
        import jax, jax.numpy as jnp
        import numpy as np
        E = 16
        K = 4
        H = 192
        I = 384
        LIMIT = 7.0
        ALPHA = 1.702
        EPS = 1e-05

        def rmsnorm(x, scale):
            xf = x.astype(jnp.float32)
            inv = jax.lax.rsqrt(jnp.mean(xf * xf, axis=-1, keepdims=True) + EPS)
            return (xf * inv).astype(x.dtype) * scale

        def swiglu(x, limit=LIMIT, alpha=ALPHA):
            x_glu = x[..., ::2]
            x_lin = x[..., 1::2]
            x_glu = jnp.minimum(x_glu, limit)
            x_lin = jnp.clip(x_lin, -limit, limit)
            return x_glu * jax.nn.sigmoid(alpha * x_glu) * (x_lin + 1.0)
        key = jax.random.key(seed)
        ks = jax.random.split(key, 7)
        s = 0.02
        return {'x': jax.random.normal(ks[0], (2, 256, H), dtype=jnp.float32), 'norm_scale': jnp.ones((H,), dtype=jnp.float32), 'gate_w': jax.random.normal(ks[1], (E, H), dtype=jnp.float32) * s, 'gate_b': jnp.zeros((E,), dtype=jnp.float32), 'mlp1_w': jax.random.normal(ks[2], (E, 2 * I, H), dtype=jnp.float32) * s, 'mlp1_b': jax.random.normal(ks[3], (E, 2 * I), dtype=jnp.float32) * s, 'mlp2_w': jax.random.normal(ks[4], (E, H, I), dtype=jnp.float32) * s, 'mlp2_b': jax.random.normal(ks[5], (E, H), dtype=jnp.float32) * s}
    _L0_ffn_all = _L0_ffn_setup()
    _L0_ffn_in = {k: v for k, v in _L0_ffn_all.items() if k in ('norm_scale', 'gate_w', 'gate_b', 'mlp1_w', 'mlp1_b', 'mlp2_w', 'mlp2_b')}
    del _L0_ffn_all
    return {'x': x, 'txt': txt, 'L0_tok_conv_w': _L0_tok_in['conv_w'], 'L0_tok_conv_b': _L0_tok_in['conv_b'], 'L0_tok_ln1_g': _L0_tok_in['ln1_g'], 'L0_tok_ln1_b': _L0_tok_in['ln1_b'], 'L0_tok_qkv_w': _L0_tok_in['qkv_w'], 'L0_tok_out_w': _L0_tok_in['out_w'], 'L0_tok_out_b': _L0_tok_in['out_b'], 'L0_tok_ln2_g': _L0_tok_in['ln2_g'], 'L0_tok_ln2_b': _L0_tok_in['ln2_b'], 'L0_tok_ff1_w': _L0_tok_in['ff1_w'], 'L0_tok_ff1_b': _L0_tok_in['ff1_b'], 'L0_tok_ff2_w': _L0_tok_in['ff2_w'], 'L0_tok_ff2_b': _L0_tok_in['ff2_b'], 'L0_tok_lnf_g': _L0_tok_in['lnf_g'], 'L0_tok_lnf_b': _L0_tok_in['lnf_b'], 'L0_tok_head_w': _L0_tok_in['head_w'], 'L0_tok_head_b': _L0_tok_in['head_b'], 'L0_attn_g': _L0_attn_in['g'], 'L0_attn_attention_mask': _L0_attn_in['attention_mask'], 'L0_attn_Wq': _L0_attn_in['Wq'], 'L0_attn_bq': _L0_attn_in['bq'], 'L0_attn_Wv': _L0_attn_in['Wv'], 'L0_attn_bv': _L0_attn_in['bv'], 'L0_ffn_norm_scale': _L0_ffn_in['norm_scale'], 'L0_ffn_gate_w': _L0_ffn_in['gate_w'], 'L0_ffn_gate_b': _L0_ffn_in['gate_b'], 'L0_ffn_mlp1_w': _L0_ffn_in['mlp1_w'], 'L0_ffn_mlp1_b': _L0_ffn_in['mlp1_b'], 'L0_ffn_mlp2_w': _L0_ffn_in['mlp2_w'], 'L0_ffn_mlp2_b': _L0_ffn_in['mlp2_b']}

def reference(x, txt, L0_tok_conv_w, L0_tok_conv_b, L0_tok_ln1_g, L0_tok_ln1_b, L0_tok_qkv_w, L0_tok_out_w, L0_tok_out_b, L0_tok_ln2_g, L0_tok_ln2_b, L0_tok_ff1_w, L0_tok_ff1_b, L0_tok_ff2_w, L0_tok_ff2_b, L0_tok_lnf_g, L0_tok_lnf_b, L0_tok_head_w, L0_tok_head_b, L0_attn_g, L0_attn_attention_mask, L0_attn_Wq, L0_attn_bq, L0_attn_Wv, L0_attn_bv, L0_ffn_norm_scale, L0_ffn_gate_w, L0_ffn_gate_b, L0_ffn_mlp1_w, L0_ffn_mlp1_b, L0_ffn_mlp2_w, L0_ffn_mlp2_b):
    import jax
    import jax.numpy as jnp

    def _L0_tok_ref(im, conv_w, conv_b, ln1_g, ln1_b, qkv_w, out_w, out_b, ln2_g, ln2_b, ff1_w, ff1_b, ff2_w, ff2_b, lnf_g, lnf_b, head_w, head_b):
        import jax, jax.numpy as jnp
        import numpy as np
        B, C, H, W = (8, 32, 128, 128)
        P = 8
        D = 128
        NH, DH = (8, 64)
        M = 512
        L = 2
        DOUT = 192
        INNER = NH * DH

        def _ln(x, g, b, eps=1e-05):
            mu = x.mean(-1, keepdims=True)
            xc = x - mu
            var = (xc * xc).mean(-1, keepdims=True)
            return xc * jax.lax.rsqrt(var + eps) * g + b

        def _forward(im, conv_w, conv_b, ln1_g, ln1_b, qkv_w, out_w, out_b, ln2_g, ln2_b, ff1_w, ff1_b, ff2_w, ff2_b, lnf_g, lnf_b, head_w, head_b):
            b, c, h, w = im.shape
            hp, wp = (h // P, w // P)
            patches = im.reshape(b, c, hp, P, wp, P)
            x = jnp.einsum('bchpwq,dcpq->bhwd', patches, conv_w)
            x = x.reshape(b, hp * wp, -1) + conv_b
            n = hp * wp
            scale = DH ** (-0.5)
            for i in range(ln1_g.shape[0]):
                y = _ln(x, ln1_g[i], ln1_b[i])
                qkv = y @ qkv_w[i]
                q, k, v = jnp.split(qkv, 3, axis=-1)
                to_heads = lambda t: t.reshape(b, n, NH, DH).transpose(0, 2, 1, 3)
                q, k, v = (to_heads(q), to_heads(k), to_heads(v))
                q = jax.nn.softmax(q, axis=-1) * scale
                k = jax.nn.softmax(k, axis=-2)
                ctx = jnp.einsum('bhnd,bhne->bhde', k, v)
                att = jnp.einsum('bhnd,bhde->bhne', q, ctx)
                att = att.transpose(0, 2, 1, 3).reshape(b, n, INNER)
                x = x + att @ out_w[i] + out_b[i]
                y = _ln(x, ln2_g[i], ln2_b[i])
                hdn = jax.nn.gelu(y @ ff1_w[i] + ff1_b[i], approximate=False)
                x = x + hdn @ ff2_w[i] + ff2_b[i]
            return _ln(x, lnf_g, lnf_b) @ head_w + head_b
        return _forward(im, conv_w, conv_b, ln1_g, ln1_b, qkv_w, out_w, out_b, ln2_g, ln2_b, ff1_w, ff1_b, ff2_w, ff2_b, lnf_g, lnf_b, head_w, head_b)

    def _L0_attn_ref(hidden_states, g, attention_mask, Wq, bq, Wv, bv):
        import jax, jax.numpy as jnp
        import numpy as np
        B, S, H, NH = (1, 512, 192, 12)
        HD = H // NH
        hs = jnp.swapaxes(hidden_states, 0, 1)
        s, b, h = hs.shape
        BN = s * b
        q = hs @ Wq.T + bq
        v = hs @ Wv.T + bv
        q = jnp.swapaxes(q.reshape(s, b, NH, HD), 0, 1).reshape(NH, BN, HD)
        q = q / jnp.maximum(jnp.linalg.norm(q, axis=2, keepdims=True), 1e-12)
        v = jnp.swapaxes(v.reshape(s, b, NH, HD), 0, 1).reshape(BN, NH, HD)
        bool_mask = (attention_mask >= 0).reshape(-1, 1).astype(g.dtype)
        _g_masked = g * (bool_mask @ bool_mask.T)
        AB = jnp.einsum('hnd,hmd->hnm', q, q)
        AA = jnp.sum(q * q, axis=-1, keepdims=True)
        sim = -(AA - 2.0 * AB + jnp.swapaxes(AA, -1, -2)) * HD ** (-0.5)
        attn = jax.nn.softmax(sim, axis=-1)
        out = jnp.einsum('hnm,hmd->hnd', attn, jnp.swapaxes(v, 0, 1))
        out = out.reshape(b, s, NH, HD).reshape(b, s, h)
        return out

    def _L0_ffn_ref(x, norm_scale, gate_w, gate_b, mlp1_w, mlp1_b, mlp2_w, mlp2_b):
        import jax, jax.numpy as jnp
        import numpy as np
        E = 16
        K = 4
        H = 192
        I = 384
        LIMIT = 7.0
        ALPHA = 1.702
        EPS = 1e-05

        def rmsnorm(x, scale):
            xf = x.astype(jnp.float32)
            inv = jax.lax.rsqrt(jnp.mean(xf * xf, axis=-1, keepdims=True) + EPS)
            return (xf * inv).astype(x.dtype) * scale

        def swiglu(x, limit=LIMIT, alpha=ALPHA):
            x_glu = x[..., ::2]
            x_lin = x[..., 1::2]
            x_glu = jnp.minimum(x_glu, limit)
            x_lin = jnp.clip(x_lin, -limit, limit)
            return x_glu * jax.nn.sigmoid(alpha * x_glu) * (x_lin + 1.0)
        B, T, _ = x.shape
        t = rmsnorm(x, norm_scale)
        g = jnp.einsum('bth,eh->bte', t, gate_w) + gate_b
        top_vals, top_idx = jax.lax.top_k(g, K)
        route_w = jax.nn.softmax(top_vals, axis=-1)
        t_flat = t.reshape(B * T, H)
        idx_flat = top_idx.reshape(B * T, K)
        w_flat = route_w.reshape(B * T, K)
        onehot = jax.nn.one_hot(idx_flat, E, dtype=t_flat.dtype)
        comb = jnp.einsum('nke,nk->ne', onehot, w_flat)
        h = jnp.einsum('nh,ech->nec', t_flat, mlp1_w) + mlp1_b
        a = swiglu(h)
        y = jnp.einsum('nec,ehc->neh', a, mlp2_w) + mlp2_b
        out_flat = jnp.einsum('neh,ne->nh', y, comb)
        return x + out_flat.reshape(B, T, H)
    h = _L0_tok_ref(x, L0_tok_conv_w, L0_tok_conv_b, L0_tok_ln1_g, L0_tok_ln1_b, L0_tok_qkv_w, L0_tok_out_w, L0_tok_out_b, L0_tok_ln2_g, L0_tok_ln2_b, L0_tok_ff1_w, L0_tok_ff1_b, L0_tok_ff2_w, L0_tok_ff2_b, L0_tok_lnf_g, L0_tok_lnf_b, L0_tok_head_w, L0_tok_head_b)
    h = jnp.concatenate([h, txt], axis=1)
    h = h + _L0_attn_ref(_layernorm(h, axis=-1), L0_attn_g, L0_attn_attention_mask, L0_attn_Wq, L0_attn_bq, L0_attn_Wv, L0_attn_bv)
    h = h + _L0_ffn_ref(_layernorm(h, axis=-1), L0_ffn_norm_scale, L0_ffn_gate_w, L0_ffn_gate_b, L0_ffn_mlp1_w, L0_ffn_mlp1_b, L0_ffn_mlp2_w, L0_ffn_mlp2_b)
    return h

_drawn_inputs = setup_inputs


def setup_inputs(seed=0):
    import zlib

    import numpy as np

    out = dict(_drawn_inputs(seed))
    spreads = {'L0_tok_conv_b': (0.0, 0.1),
     'L0_tok_ln1_g': (1.0, 0.6),
     'L0_tok_ln1_b': (0.0, 0.8),
     'L0_tok_out_b': (0.0, 0.1),
     'L0_tok_ln2_g': (1.0, 0.6),
     'L0_tok_ln2_b': (0.0, 0.8),
     'L0_tok_ff1_b': (0.0, 0.328),
     'L0_tok_ff2_b': (0.0, 0.1),
     'L0_tok_lnf_g': (1.0, 0.2),
     'L0_tok_lnf_b': (0.0, 0.1),
     'L0_tok_head_b': (0.0, 0.1),
     'L0_attn_bq': (0.0, 2.0),
     'L0_attn_bv': (0.0, 0.1),
     'L0_ffn_norm_scale': (1.0, 0.6),
     'L0_ffn_gate_b': (0.0, 0.547)}
    factors = {'L0_tok_qkv_w': 8.0,
     'L0_tok_out_w': 8.0,
     'L0_attn_Wq': 64.0,
     'L0_ffn_gate_w': 2.715,
     'L0_ffn_mlp1_b': 24.711,
     'L0_ffn_mlp2_b': 7.488}
    for name, (base, spread) in spreads.items():
        noise = np.random.default_rng([zlib.crc32(name.encode()), seed]).standard_normal(out[name].shape)
        drawn = base * np.exp(spread * noise) if base else spread * noise
        out[name] = jnp.asarray(drawn.astype(out[name].dtype))
    for name, factor in factors.items():
        out[name] = (out[name] * factor).astype(out[name].dtype)
    return out
```

```python
import concourse.bass as bass
from concourse import mybir
from contextlib import ExitStack

P = 128
NB, NPIX, D, KT = 4, 256, 128, 16
NT_IMG = NB * NPIX // P
LAYERS, INNER, HD, MLP = 2, 512, 64, 512
NPAIR = INNER // P
C, NH, DH = 192, 12, 16
NT = 12
KEYB = 12
QS = 1536
CB = C - P
QG = 4
QW = QS // QG
STK = 68
E, TOPK, FF = 16, 4, 384
BUCKET = QS + P
SPARE = E * BUCKET
MT = 64
NSPARE = MT - TOPK * NT
TOK_ACC = NT_IMG * 2 + LAYERS * (3 * NT_IMG + NB)


def fusion_kernel(nc, patches, conv_w, cols, rows, qkv_w, out_w, ff1_w, ff2_w, head_w, txt,
                  wqv_a, wqv_b, gate_a, gate_b, nscale, w1_a, w1_b, w2, b2, out, xs, ys):
    f32, f16, i32, u32 = mybir.dt.float32, mybir.dt.float16, mybir.dt.int32, mybir.dt.uint32
    ALU, ACT, AX = mybir.AluOpType, mybir.ActivationFunctionType, mybir.AxisListType
    ctx = ExitStack()
    with ctx:
        def sb(name, shape, dt=f32):
            return ctx.enter_context(nc.sbuf_tensor(name, shape, dt))

        def sem(name):
            return ctx.enter_context(nc.semaphore(name))

        ps = ctx.enter_context(nc.psum_tensor("ps", [P, 8 * 512], f32))

        def bank(i):
            return ps[:, i * 512:(i + 1) * 512]

        big = sb("big", [P, E * 2 * 768 + E * 3 * C])
        at = [0]

        def carve(n):
            at[0] += n
            return big[:, at[0] - n:at[0]]

        patch_sb = [carve(KT * NPIX).rearrange("p (k n) -> p k n", k=KT) for _ in range(NB)]
        convw_sb = carve(KT * D).rearrange("p (k d) -> p k d", k=KT)
        qkvw_sb = carve(LAYERS * 3 * INNER).rearrange("p (l n) -> p l n", l=LAYERS)
        outw_sb = carve(LAYERS * NPAIR * D).rearrange("p (l k d) -> p l k d", l=LAYERS, k=NPAIR)
        ff1w_sb = carve(LAYERS * MLP).rearrange("p (l n) -> p l n", l=LAYERS)
        ff2w_sb = carve(LAYERS * 4 * D).rearrange("p (l k d) -> p l k d", l=LAYERS, k=4)
        k_tok = carve(NT_IMG * INNER).rearrange("p (t n) -> p t n", t=NT_IMG)
        mlp_hid = carve(4 * NT_IMG * P).rearrange("p (h n) -> p h n", h=4)
        yT = carve(NT_IMG * P)
        q_tok, v_tok, kT, qT = [big[:, i * KT * NPIX:(i + 1) * KT * NPIX] for i in range(4)]
        q_tok = q_tok.rearrange("p (t n) -> p t n", t=NT_IMG)
        v_tok = v_tok.rearrange("p (t n) -> p t n", t=NT_IMG)
        kT = kT.rearrange("p (h n) -> p h n", h=NPAIR)
        qT = qT.rearrange("p (h n) -> p h n", h=NPAIR)
        w1a_sb = big[:, 0:E * 768]
        w1b_sb = big[:, E * 768:2 * E * 768]
        w2_sb = big[:, 2 * E * 768:]

        mid = sb("mid", [P, 8448 + NH * STK])
        probs = [mid[:, i * QS:(i + 1) * QS] for i in range(3)]
        ab = mid[:, 3 * QS:5 * QS].bitcast(f16)
        keysT = [ab[0:STK, (2 * i) * QS:(2 * i + 1) * QS] for i in range(2)]
        qrysT = [ab[0:STK, (2 * i + 1) * QS:(2 * i + 2) * QS] for i in range(2)]
        vhead = [mid[:, 5 * QS + i * KEYB * 32:5 * QS + (i + 1) * KEYB * 32]
                 .rearrange("p (k d) -> p k d", k=KEYB) for i in range(2)]
        stk = mid[:, 5 * QS + 2 * KEYB * 32:5 * QS + 2 * KEYB * 32 + NH * STK].bitcast(f16)
        key_tok = stk[:, 0:NH * STK].rearrange("p (h c) -> p h c", h=NH)
        qry_tok = stk[:, NH * STK:2 * NH * STK].rearrange("p (h c) -> p h c", h=NH)
        x_res = mid[:, 0:1024].rearrange("p (t d) -> p t d", t=NT_IMG)
        x_nrm = mid[:, 1024:2048].rearrange("p (t d) -> p t d", t=NT_IMG)
        ctx_bd = mid[:, 2048:4096].rearrange("p (b k d) -> p b k d", b=NB, k=NPAIR)
        ctx_w = mid[:, 4096:6144].rearrange("p (b k d) -> p b k d", b=NB, k=NPAIR)
        wqva_sb = mid[:, 6144:6528]
        wqvb_sb = mid[0:CB + 1, 6528:6912]
        hnT = [mid[:, 6912 + 256 * i:7168 + 256 * i] for i in range(2)]
        h_nrm = [mid[:, 7424 + 192 * i:7616 + 192 * i] for i in range(2)]
        rows_sb = mid[0:1, 7808:7808 + 5 * D + C]
        headw_sb = mid[:, 8640:8640 + C]
        done_e = mid[0:1, 0:MT * E].rearrange("p (j e) -> p j e", j=MT)
        done_t = mid[0:1, MT * E:2 * MT * E].rearrange("p (j e) -> p j e", j=MT)
        over = mid[:, 2 * MT * E:2 * MT * E + E * NT].rearrange("p (e t) -> p e t", e=E)
        ej, sj, rowj, tmpj = [mid[0:1, 2304 + MT * i:2304 + MT * (i + 1)] for i in range(4)]
        choice = mid[:, 6272:6272 + NT * TOPK * E].rearrange("p (n e) -> p n e", e=E)
        xt = [mid[:, i * C:(i + 1) * C] for i in range(2)]
        xtT = [mid[:, 384 + i * 256:640 + i * 256] for i in range(2)]
        glu = [mid[:, 896 + i * FF:1280 + i * FF] for i in range(2)]
        lin = [mid[:, 1664 + i * FF:2048 + i * FF] for i in range(2)]
        sig = [mid[:, 2432 + i * FF:2816 + i * FF] for i in range(2)]
        prod = [mid[:, 3200 + i * FF:3584 + i * FF] for i in range(2)]
        actv = [mid[:, 3968 + i * FF:4352 + i * FF] for i in range(2)]
        actT = [mid[:, 4736 + i * FF:5120 + i * FF] for i in range(2)]
        yt = [mid[:, 5504 + i * C:5696 + i * C] for i in range(2)]
        b2t = [mid[0:1, 5888 + i * C:6080 + i * C] for i in range(2)]
        gath = [mid[:, 6272 + i * 768:7040 + i * 768].rearrange("p (k c) -> p k c", k=TOPK) for i in range(3)]

        h_res = sb("h_res", [P, NT, C])
        qv = sb("qv", [P, NT, 2 * C])
        cols_sb = sb("cols_sb", [P, 18])
        ident = sb("ident", [P, P])
        ident16 = sb("ident16", [P, P], f16)
        ones = sb("ones", [P, P])
        tri = sb("tri", [P, P])
        zero_rows = sb("zero_rows", [P, C])
        gatea_sb = sb("gatea_sb", [P, E])
        gateb_sb = sb("gateb_sb", [CB + 1, E])
        nscale_sb = sb("nscale_sb", [P, C])
        iota_e = sb("iota_e", [P, E])
        iota_j = sb("iota_j", [P, MT])
        bucket0 = sb("bucket0", [P, E])
        edges = sb("edges", [P, NT])
        phalf = sb("phalf", [P, NT])
        nhalf = sb("nhalf", [P, NT])
        stat = sb("stat", [P, 2, 6])
        mv = sb("mv", [P, 2, 2])
        vps = sb("vps", [P, 2])
        rstd = sb("rstd", [P, 2])
        sq = sb("sq", [P, C])
        qn = sb("qn", [P, C])
        cnt, tiles_e, ends = [qn[:, 16 * i:16 * i + 16] for i in range(3)]
        shift = qn[:, 128:144]
        wgt = qn[:, 144:192].rearrange("p (t k) -> p t k", t=NT)
        wexp = qn[:, 48:96].rearrange("p (t k) -> p t k", t=NT)
        wsum, wrec = qn[:, 96:108], qn[:, 112:124]
        ss = sb("ss", [P, NH])
        nrm = sb("nrm", [P, NH])
        nrmc = sb("nrmc", [P, NH])
        rn = sb("rn", [P, NH])
        aa = sb("aa", [P, NH])
        o_acc = sb("o_acc", [P, QW])
        knmax, ksum, krec, krec8 = [o_acc[:, 16 * i:16 * i + 16].rearrange("p (h b) -> p h b", h=NPAIR) for i in range(4)]
        qmax, qsum, qrec = [o_acc[:, 64 * i:64 * i + 64].rearrange("p (t h) -> p t h", t=NT_IMG) for i in range(1, 4)]
        o_rec = sb("o_rec", [P, 3, QG])
        o_nrm = sb("o_nrm", [P, C])
        ej_i, row_i = [o_nrm[0:1, MT * i:MT * (i + 1)].bitcast(i32) for i in range(2)]
        pad0_i = o_nrm[0:1, 2 * MT:2 * MT + E].bitcast(i32)
        ln = sb("ln", [P, C])
        ms = sb("ms", [P, 1])
        mse = sb("mse", [P, 1])
        rms = sb("rms", [P, 1])
        t_row = sb("t_row", [P, C])
        slot_u = sb("slot_u", [P, TOPK], u32)
        bank_mark = sb("bank_mark", [P, 1])
        tT = sb("tT", [P, 2 * P])
        logit = sb("logit", [P, E])
        top_i = sb("top_i", [P, 8], u32)
        top_f = sb("top_f", [P, TOPK])
        onehot = sb("onehot", [P, TOPK, E])
        mask = sb("mask", [P, E])
        seen = sb("seen", [P, E])
        slot_e = sb("slot_e", [P, E])
        slot_oh = sb("slot_oh", [P, TOPK, E])
        slot_f = sb("slot_f", [P, TOPK])
        slot_all = sb("slot_all", [P, NT, TOPK])
        top_all = sb("top_all", [P, NT, TOPK])
        ys_row = sb("ys_row", [P, NT, TOPK], u32)
        top_v = sb("top_v", [P, NT, TOPK])
        top8 = sb("top8", [P, 8])

        patch_in = [sem(f"patch_in{b}") for b in range(NB)]
        convw_in, rows_in, tokw_in = sem("convw_in"), sem("rows_in"), sem("tokw_in")
        small_in = sem("small_in")
        consts_ready = sem("consts_ready")
        pool_step = sem("pool_step")
        dve_step = sem("dve_step")
        acc_ready, acc_taken = sem("acc_ready"), sem("acc_taken")
        act_ready, act_taken = sem("act_ready"), sem("act_taken")
        kt_ready, kt_taken = sem("kt_ready"), sem("kt_taken")
        kmax_ready = sem("kmax_ready")
        trq_ready, trq_taken = sem("trq_ready"), sem("trq_taken")
        trk_ready, trk_taken = sem("trk_ready"), sem("trk_taken")
        ctxw_ready, ctxw_taken = sem("ctxw_ready"), sem("ctxw_taken")
        mv_ready, rstd_ready = sem("mv_ready"), sem("rstd_ready")
        y_ready = sem("y_ready")
        qexp_ready, qrec_ready, qnorm_ready = sem("qexp_ready"), sem("qrec_ready"), sem("qnorm_ready")
        w_in = sem("w_in")
        scores_ready, probs_ready, probs_used = sem("scores_ready"), sem("probs_ready"), sem("probs_used")
        stack_ready, tr_ready, tr_taken = sem("stack_ready"), sem("tr_ready"), sem("tr_taken")
        vhead_ready = sem("vhead_ready")
        ss_ready, nrm_ready = sem("ss_ready"), sem("nrm_ready")
        oacc_ready = sem("oacc_ready")
        onrm_ready, h_ready = sem("onrm_ready"), sem("h_ready")
        lmv_ready, lrstd_ready = sem("lmv_ready"), sem("lrstd_ready")
        ms_ready, rms_ready = sem("ms_ready"), sem("rms_ready")
        t_ready, mask_ready, slots_ready, rows_out = (sem("t_ready"), sem("mask_ready"), sem("slots_ready"),
                                                      sem("rows_out"))
        base_ready = sem("base_ready")
        plan_ready = sem("plan_ready")
        cnt_ready = sem("cnt_ready")
        pads_out = sem("pads_out")
        x_in, x_read = [sem("x_in0"), sem("x_in1")], sem("x_read")
        b2_in, xT_ones = [sem("b2_in0"), sem("b2_in1")], sem("xT_ones")
        xT_ready = sem("xT_ready")
        h_done, glu_ready, lin_ready, sig_ready = sem("h_done"), sem("glu_ready"), sem("lin_ready"), sem("sig_ready")
        prod_ready, actv_ready = sem("prod_ready"), sem("actv_ready")
        aT_psum, aT_ready = sem("aT_psum"), sem("aT_ready")
        y_psum, y_sb = sem("y_psum"), sem("y_sb")
        y_out = [sem("y_out0"), sem("y_out1")]
        wexp_ready, place_ready = sem("wexp_ready"), sem("place_ready")
        wmax_ready = sem("wmax_ready")
        g_in = [sem(f"g_in{i}") for i in range(3)]
        g_used = sem("g_used")
        final_out = sem("final_out")

        NCONST = 18
        TR7 = 7

        def tr_base(r):
            return r * TR7 + 6

        def held_wait(eng, s, value):
            if not isinstance(value, int):
                value = eng.snap(value)
                eng.wait_ge(consts_ready, NCONST)
            eng.wait_ge(s, value)

        class Chain:
            def __init__(self, eng, s):
                self.eng, self.sem, self.base, self.n = eng, s, 0, 0

            def __call__(self, ins, held=False):
                self.n += 1
                ins.then_inc(self.sem, 1)
                (held_wait if held else type(self.eng).wait_ge)(self.eng, self.sem, self.base + self.n)

            def rebase(self, base):
                self.base, self.n = base, 0

        DVE_STEPS = 19
        POOL_STEPS = 2

        block = ctx.enter_context(nc.Block())

        @block.sync
        def _(sp):
            sp.dma_start(convw_sb, conv_w).then_inc(convw_in, 16)
            sp.dma_start(rows_sb, rows).then_inc(rows_in, 16)
            sp.dma_start(patch_sb[0], patches[0]).then_inc(patch_in[0], 16)
            sp.dma_start(cols_sb[:], cols).then_inc(small_in, 16)
            for b in range(1, NB):
                sp.dma_start(patch_sb[b], patches[b]).then_inc(patch_in[b], 16)
            for dst, src in ((qkvw_sb, qkv_w), (outw_sb, out_w), (ff1w_sb, ff1_w), (ff2w_sb, ff2_w),
                             (headw_sb, head_w)):
                sp.dma_start(dst, src).then_inc(tokw_in, 16)
            for dst, src in ((wqva_sb, wqv_a), (wqvb_sb, wqv_b), (gatea_sb[:], gate_a), (gateb_sb[:], gate_b),
                             (nscale_sb[:], nscale.broadcast_to([P, C]))):
                sp.dma_start(dst, src).then_inc(small_in, 16)
            for b in range(NB):
                sp.dma_start(h_res[:, 3 * b + 2, :], txt[b]).then_inc(small_in, 16)
            sp.wait_ge(acc_taken, TOK_ACC)
            for e in range(0, E, 4):
                sp.dma_start(w1a_sb[:, e * 768:(e + 4) * 768], w1_a[:, e * 768:(e + 4) * 768]).then_inc(w_in, 16)
                sp.dma_start(w1b_sb[0:CB + 1, e * 768:(e + 4) * 768], w1_b[:, e * 768:(e + 4) * 768]).then_inc(w_in, 16)
                sp.dma_start(w2_sb[:, e * 3 * C:(e + 4) * 3 * C], w2[:, e * 3 * C:(e + 4) * 3 * C]).then_inc(w_in, 16)
            sp.wait_ge(cnt_ready, 1)
            for e in range(E):
                first = sp.value_load(pad0_i[0:1, e:e + 1], min_val=0, max_val=SPARE - P)
                sp.dma_start(xs[bass.ds(first, P), :], zero_rows[:]).then_inc(pads_out, 16)
            sp.wait_ge(pads_out, 16 * E)
            sp.wait_ge(rows_out, 16 * (TOPK * NT + 1))
            sp.wait_ge(plan_ready, 1)

            def load_rows(j, r, free=True):
                if free:
                    sp.wait_ge(x_read, j - 1)
                row = sp.value_load(row_i[0:1, bass.ds(j, 1)], min_val=0, max_val=SPARE + (NSPARE - 1) * P)
                sp.dma_start(xt[r], xs[bass.ds(row, P), :]).then_inc(x_in[r], 16)

            def load_bias(j, r, free=True):
                if free:
                    sp.wait_ge(y_psum, j - 1)
                ex = sp.value_load(ej_i[0:1, bass.ds(j, 1)], min_val=0, max_val=E - 1)
                sp.dma_start(b2t[r], b2[bass.ds(ex, 1), :]).then_inc(b2_in[r], 16)

            load_rows(0, 0, False)
            load_rows(1, 1, False)
            load_bias(0, 0, False)
            load_rows(2, 0)
            load_bias(1, 1, False)
            load_rows(3, 1)
            with sp.Fori(1, MT // 2 - 1) as i:
                for r in (0, 1):
                    load_bias(i * 2 + r, r)
                    load_rows(i * 2 + (2 + r), r)
            for r in (0, 1):
                load_bias(MT - 2 + r, r)

        @block.gpsimd
        def _(pool):
            step = Chain(pool, pool_step)
            nc.gpsimd.memset(ident[:], 0.0).then_inc(consts_ready, 1)
            nc.gpsimd.memset(ident16[:], 0.0).then_inc(consts_ready, 1)
            nc.gpsimd.memset(ones[:], 1.0).then_inc(consts_ready, 1)
            pool.wait_ge(consts_ready, 3)
            nc.gpsimd.affine_select(out=ident[:], in_=ident[:], compare_op=ALU.not_equal, fill=1.0, base=0,
                                    pattern=[[-1, P]], channel_multiplier=1).then_inc(consts_ready, 1)
            nc.gpsimd.affine_select(out=ident16[:], in_=ident16[:], compare_op=ALU.not_equal, fill=1.0, base=0,
                                    pattern=[[-1, P]], channel_multiplier=1).then_inc(consts_ready, 1)
            nc.gpsimd.affine_select(out=tri[:], in_=ones[:], compare_op=ALU.is_gt, fill=0.0, base=0,
                                    pattern=[[1, P]], channel_multiplier=-1).then_inc(consts_ready, 1)
            nc.gpsimd.memset(zero_rows[:], 0.0).then_inc(consts_ready, 1)
            nc.gpsimd.memset(phalf[:], 0.5).then_inc(consts_ready, 1)
            nc.gpsimd.memset(nhalf[:], -0.5).then_inc(consts_ready, 1)
            nc.gpsimd.memset(mid[:, 2048:4096], 0.0).then_inc(consts_ready, 1)
            nc.gpsimd.memset(seen[:], 0.0).then_inc(consts_ready, 1)
            for dst, pat in ((iota_e, [[1, E]]), (iota_j, [[1, MT]]), (bucket0, [[BUCKET, E]]), (edges, [[P, NT]])):
                nc.gpsimd.iota(dst[:], pattern=pat, base=0, channel_multiplier=0,
                               allow_small_or_imprecise_dtypes=True).then_inc(consts_ready, 1)
            for i, dst in enumerate((hnT[0], hnT[1], tT)):
                pool.wait_ge(consts_ready, NCONST - 3 + i)
                nc.gpsimd.memset(dst[CB:CB + 1, P:2 * P], 1.0).then_inc(consts_ready, 1)
            pool.wait_ge(consts_ready, NCONST)
            pool.dma_start(xs[SPARE:SPARE + NSPARE * P, :].rearrange("(t p) c -> p t c", p=P),
                           zero_rows[:].unsqueeze(1).broadcast_to([P, NSPARE, C])).then_inc(rows_out, 16)

            def ln_rstd(i, n):
                pool.wait_ge(mv_ready, i + 1)
                step(nc.gpsimd.tensor_scalar(vps[:, 0:n], mv[:, 0:n, 1], 1e-5, None, ALU.add))
                nc.gpsimd.tensor_tensor(rstd[:, 0:n], vps[:, 0:n], nhalf[:, 0:n], ALU.pow).then_inc(rstd_ready, 1)

            for i in range(NB):
                ln_rstd(i, 2)
            for l in range(LAYERS):
                for t in range(NT_IMG):
                    pool.wait_ge(qrec_ready, NT_IMG * l + t + 1)
                    v = q_tok[:, t, :].rearrange("p (h d) -> p h d", h=8)
                    nc.gpsimd.tensor_tensor(v, v, qrec[:, t, :].unsqueeze(2).broadcast_to([P, 8, HD]),
                                            ALU.mult).then_inc(qnorm_ready, 1)
                for i in range(2 * NB):
                    ln_rstd(NB + 2 * NB * l + i, 2)
            for t in range(NT):
                ln_rstd(NB * (1 + 2 * LAYERS) + t, 1)

            pool.wait_ge(acc_taken, TOK_ACC + NT)
            nc.gpsimd.memset(key_tok[:, :, 66:68], -0.5).then_inc(consts_ready, 1)
            nc.gpsimd.memset(qry_tok[:, :, 64:66], -0.5).then_inc(consts_ready, 1)
            for r in range(2):
                step(nc.gpsimd.memset(vhead[r][:, :, 16:32], 0.0))
                step(nc.gpsimd.memset(vhead[r][:, :, 16:17], 1.0))

            def head_v(n, r):
                nc.gpsimd.tensor_copy(vhead[r][:, :, 0:DH], qv[:, :, bass.ds(n * DH + C, DH)]).then_inc(vhead_ready, 1)

            def norm_root(n):
                pool.wait_ge(ss_ready, n + 1)
                nc.gpsimd.tensor_tensor(nrm[:], ss[:], phalf[:, 0:NH], ALU.pow).then_inc(nrm_ready, 1)

            def route(r, par):
                pool.wait_ge(onrm_ready, r + 1)
                hr = h_res[:, bass.ds(r, 1), :].rearrange("p a c -> p (a c)")
                nc.gpsimd.tensor_tensor(hr, hr, o_nrm[:], ALU.add).then_inc(h_ready, 1)

            def route2(r, par):
                hr = h_res[:, bass.ds(r, 1), :].rearrange("p a c -> p (a c)")
                held_wait(pool, lmv_ready, r + 1)
                step(nc.gpsimd.tensor_scalar(vps[:, 0:1], mv[:, 0, 1:2], 1e-5, None, ALU.add))
                nc.gpsimd.tensor_tensor(rstd[:, 0:1], vps[:, 0:1], nhalf[:, 0:1], ALU.pow).then_inc(lrstd_ready, 1)
                held_wait(pool, ms_ready, r + 1)
                step(nc.gpsimd.tensor_scalar(mse[:], ms[:], 1.0 / C, 1e-5, ALU.mult, ALU.add))
                nc.gpsimd.tensor_tensor(rms[:], mse[:], nhalf[:, 0:1], ALU.pow).then_inc(rms_ready, 1)
                nc.gpsimd.tensor_tensor(hr, hr, ln[:], ALU.add).then_inc(base_ready, 1)
                held_wait(pool, slots_ready, r + 1)
                for k in range(TOPK):
                    nc.gpsimd.indirect_dma_start(
                        xs[:, :], bass.IndirectOffsetOnAxis(ap=slot_u[:, k:k + 1], axis=0),
                        t_row[:], None).then_inc(rows_out, 16)

            def pool_head(n, r, par, first, last):
                if not first:
                    route(r, 1 - par)
                if not last:
                    norm_root(n + 1)
                    if not first:
                        pool.wait_ge(oacc_ready, n)
                    head_v(n + 1, 1 - par)
                if not first:
                    route2(r, 1 - par)

            norm_root(0)
            head_v(0, 0)
            pool_head(0, None, 0, True, False)
            before = step.n
            with pool.Fori(0, 5) as i:
                for p in (0, 1):
                    step.rebase(i * (2 * POOL_STEPS) + (before + POOL_STEPS * p))
                    pool_head(i * 2 + (1 + p), i * 2 + p, 1 - p, False, False)
                    assert step.n == POOL_STEPS, step.n
            step.rebase(before + 10 * POOL_STEPS)
            pool_head(NT - 1, NT - 2, 1, False, True)
            route(NT - 1, 1)
            route2(NT - 1, 1)

            def expert(j, r):
                pool.wait_ge(sig_ready, j + 1)
                pool.wait_ge(prod_ready, j + 1)
                nc.gpsimd.tensor_tensor(actv[r], prod[r], sig[r], ALU.mult).then_inc(actv_ready, 1)

            with pool.Fori(0, MT // 2) as i:
                for r in (0, 1):
                    expert(i * 2 + r, r)

            pool.wait_ge(place_ready, 1)
            for r in (0, 1):
                pool.wait_ge(y_out[r], 16 * (MT // 2))
            for t in range(NT):
                if t >= 3:
                    pool.wait_ge(g_used, t - 2)
                for k in range(TOPK):
                    nc.gpsimd.indirect_dma_start(
                        gath[t % 3][:, k, :], None, ys[:, :],
                        bass.IndirectOffsetOnAxis(ap=ys_row[:, t, k:k + 1], axis=0)).then_inc(g_in[t % 3], 16)

        @block.tensor
        def _(pe):
            acc, acts, kts = [0], [0], [0]

            def acc_job():
                if acc[0] >= 2:
                    pe.wait_ge(acc_taken, acc[0] - 1)
                acc[0] += 1
                return bank((acc[0] - 1) % 2)

            def act_job():
                if acts[0] >= 2:
                    pe.wait_ge(act_taken, acts[0] - 1)
                acts[0] += 1
                return bank(2 + (acts[0] - 1) % 2)

            def rows_bias(dst, off, n):
                nc.tensor.matmul(dst, ones[0:1, :], rows_sb[0:1, off:off + n], start=True, stop=False)

            pe.wait_ge(consts_ready, NCONST)
            pe.wait_ge(convw_in, 16)
            pe.wait_ge(rows_in, 16)
            for t in range(NT_IMG):
                if t % 2 == 0:
                    pe.wait_ge(patch_in[t // 2], 16)
                o = acc_job()[:, 0:D]
                rows_bias(o, 0, D)
                for k in range(KT):
                    last = nc.tensor.matmul(o, patch_sb[t // 2][:, k, (t % 2) * P:(t % 2) * P + P], convw_sb[:, k, :],
                                            start=False, stop=(k == KT - 1))
                last.then_inc(acc_ready, 1)
            pe.wait_ge(tokw_in, 16 * 5)
            pe.wait_ge(small_in, 16 * 10)

            def ln_transpose(i, b):
                pe.wait_ge(y_ready, NB * i + b + 1)
                o = act_job()
                for s in range(2):
                    last = nc.tensor.transpose(o[:, s * P:(s + 1) * P], x_nrm[:, 2 * b + s, :], ident[:])
                last.then_inc(act_ready, 1)

            for l in range(LAYERS):
                for b in range(NB):
                    ln_transpose(2 * l, b)
                    yb = yT[:, b * NPIX:(b + 1) * NPIX]
                    pe.wait_ge(act_taken, acts[0])
                    for hp in range(2):
                        if kts[0] >= 2:
                            pe.wait_ge(kt_taken, kts[0] - 1)
                        o = bank(4 + kts[0] % 2)
                        kts[0] += 1
                        for s in range(2):
                            h = 2 * hp + s
                            last = nc.tensor.matmul(o[:, s * NPIX:(s + 1) * NPIX],
                                                    qkvw_sb[:, l, INNER + h * P:INNER + (h + 1) * P], yb,
                                                    start=True, stop=True)
                        last.then_inc(kt_ready, 1)
                    for t in (2 * b, 2 * b + 1):
                        o = act_job()
                        nc.tensor.matmul(o, yT[:, t * P:(t + 1) * P], qkvw_sb[:, l, 2 * INNER:3 * INNER],
                                         start=True, stop=True).then_inc(act_ready, 1)
                        o = acc_job()
                        nc.tensor.matmul(o, yT[:, t * P:(t + 1) * P], qkvw_sb[:, l, 0:INNER],
                                         start=True, stop=True).then_inc(acc_ready, 1)
                for b in range(NB):
                    pe.wait_ge(kt_taken, 2 * NB * l + 2 * b + 2)
                    for t in (2 * b, 2 * b + 1):
                        pe.wait_ge(trk_taken, NT_IMG * l + t)
                        if l and t == 0:
                            pe.wait_ge(ctxw_taken, NB * l)
                        for h in range(NPAIR):
                            last = nc.tensor.transpose(bank(7)[:, h * P:(h + 1) * P], kT[:, h, t * P:(t + 1) * P], ident[:])
                        last.then_inc(trk_ready, 1)
                        pe.wait_ge(qnorm_ready, NT_IMG * l + t + 1)
                        pe.wait_ge(trq_taken, NT_IMG * l + t)
                        for h in range(NPAIR):
                            last = nc.tensor.transpose(bank(6)[:, h * P:(h + 1) * P], q_tok[:, t, h * P:(h + 1) * P], ident[:])
                        last.then_inc(trq_ready, 1)
                    pe.wait_ge(trk_taken, NT_IMG * l + 2 * b + 2)
                    pe.wait_ge(act_taken, acts[0])
                    o = acc_job()
                    for h in range(NPAIR):
                        for s in range(2):
                            last = nc.tensor.matmul(o[:, h * P:(h + 1) * P], v_tok[:, 2 * b + s, h * P:(h + 1) * P],
                                                    k_tok[:, 2 * b + s, h * P:(h + 1) * P], start=(s == 0), stop=(s == 1))
                    last.then_inc(acc_ready, 1)
                ctx_jobs = acc[0]

                def ctx_times_w(b):
                    pe.wait_ge(acc_taken, ctx_jobs - NB + b + 1)
                    pe.wait_ge(trk_taken, NT_IMG * (l + 1))
                    pe.wait_ge(ctxw_taken, NB * l + b)
                    for h in range(NPAIR):
                        last = nc.tensor.matmul(bank(7)[:, h * P:(h + 1) * P], ctx_bd[:, b, h, :], outw_sb[:, l, h, :],
                                                start=True, stop=True)
                    last.then_inc(ctxw_ready, 1)

                ctx_times_w(0)
                for b in range(NB):
                    if b + 1 < NB:
                        ctx_times_w(b + 1)
                    pe.wait_ge(ctxw_taken, NB * l + b + 1)
                    for t in (2 * b, 2 * b + 1):
                        pe.wait_ge(trq_taken, NT_IMG * l + t + 1)
                        o = acc_job()[:, 0:D]
                        rows_bias(o, D * (1 + l), D)
                        for h in range(NPAIR):
                            last = nc.tensor.matmul(o, qT[:, h, t * P:(t + 1) * P], ctx_w[:, b, h, :],
                                                    start=False, stop=(h == NPAIR - 1))
                        last.then_inc(acc_ready, 1)

                def ff2(b, hidden):
                    pe.wait_ge(act_taken, hidden)
                    for t in (2 * b, 2 * b + 1):
                        o = acc_job()[:, 0:D]
                        rows_bias(o, D * (3 + l), D)
                        for h in range(4):
                            last = nc.tensor.matmul(o, mlp_hid[:, h, t * P:(t + 1) * P], ff2w_sb[:, l, h, :],
                                                    start=False, stop=(h == 3))
                        last.then_inc(acc_ready, 1)

                for b in range(NB):
                    ln_transpose(2 * l + 1, b)
                    if b:
                        ff2(b - 1, acts[0] - 1)
                    pe.wait_ge(act_taken, acts[0])
                    for hp in range(2):
                        o = act_job()
                        for s in range(2):
                            h = 2 * hp + s
                            last = nc.tensor.matmul(o[:, s * NPIX:(s + 1) * NPIX], ff1w_sb[:, l, h * P:(h + 1) * P],
                                                    yT[:, b * NPIX:(b + 1) * NPIX], start=True, stop=True)
                        last.then_inc(act_ready, 1)
                ff2(NB - 1, acts[0])

            for b in range(NB):
                ln_transpose(2 * LAYERS, b)
                pe.wait_ge(act_taken, acts[0])
                for t in (2 * b, 2 * b + 1):
                    o = acc_job()[:, 0:C]
                    rows_bias(o, 5 * D, C)
                    nc.tensor.matmul(o, yT[:, t * P:(t + 1) * P], headw_sb, start=False, stop=True).then_inc(acc_ready, 1)
            assert acc[0] == TOK_ACC, acc[0]

            def h_transpose(t):
                pe.wait_ge(y_ready, NB * (2 * LAYERS + 1) + t + 1)
                o = act_job()
                nc.tensor.transpose(o[:, 0:P], h_nrm[t % 2][:, 0:P], ident[:])
                nc.tensor.transpose(o[0:CB, P:2 * P], h_nrm[t % 2][:, P:C], ident[:]).then_inc(act_ready, 1)

            h_transpose(0)
            for t in range(NT):
                if t + 1 < NT:
                    h_transpose(t + 1)
                pe.wait_ge(act_taken, acts[0] - (t + 1 < NT))
                o = acc_job()[:, 0:2 * C]
                nc.tensor.matmul(o, hnT[t % 2][:, 0:P], wqva_sb, start=True, stop=False)
                nc.tensor.matmul(o, hnT[t % 2][0:CB + 1, P:2 * P], wqvb_sb, start=False, stop=True).then_inc(acc_ready, 1)

            b7 = bank(7)
            b7h = bank(7).bitcast(f16)
            SETS = [ps[:, 0:QS], ps[:, QS:2 * QS]]
            oacc = bank(6)

            def stacks(g, n, job):
                pe.wait_ge(tr_taken, job)
                if g == 0:
                    pe.wait_ge(stack_ready, n + 1)
                for s in range(8):
                    k = 8 * g + s
                    src = key_tok[:, k, :] if k < NH else qry_tok[:, k - NH, :]
                    last = nc.tensor.transpose(b7h[0:STK, s * P:(s + 1) * P], src, ident16[:])
                last.then_inc(tr_ready, 1)

            def scores(n_par, kb, s):
                if s is not None:
                    pe.wait_ge(probs_ready, s)
                for c in range(3):
                    last = nc.tensor.matmul(SETS[kb % 2][:, c * 512:(c + 1) * 512], keysT[n_par][:, kb * P:(kb + 1) * P],
                                            qrysT[n_par][:, c * 512:(c + 1) * 512], start=True, stop=True)
                last.then_inc(scores_ready, 1)

            def weighted(n, par, kb):
                if kb == 0:
                    pe.wait_ge(vhead_ready, n + 1)
                    pe.wait_ge(oacc_ready, n)
                pe.wait_ge(probs_ready, n * KEYB + (kb + 1))
                for g in range(QG):
                    last = nc.tensor.matmul(oacc[32 * g:32 * g + 32, 0:QW], vhead[par][:, kb, :],
                                            probs[kb % 3][:, g * QW:(g + 1) * QW], start=(kb == 0),
                                            stop=(kb == KEYB - 1), tile_position=(0, 32 * g))
                last.then_inc(probs_used, 1)

            def out_transpose(r, job):
                pe.wait_ge(tr_taken, job)
                pe.wait_ge(oacc_ready, r + 1)
                for c in range(3):
                    last = nc.tensor.transpose(b7[:, c * P:(c + 1) * P], o_acc[:, c * P:(c + 1) * P], ident[:])
                last.then_inc(tr_ready, 1)

            def t_transpose(r, par, job):
                pe.wait_ge(tr_taken, job)
                pe.wait_ge(t_ready, r + 1)
                nc.tensor.transpose(b7[:, 0:P], t_row[:, 0:P], ident[:])
                nc.tensor.transpose(b7[0:CB, P:2 * P], t_row[:, P:C], ident[:]).then_inc(tr_ready, 1)

            def logits(job):
                pe.wait_ge(tr_taken, job)
                nc.tensor.matmul(b7[:, 0:E], tT[:, 0:P], gatea_sb[:], start=True, stop=False)
                nc.tensor.matmul(b7[:, 0:E], tT[0:CB + 1, P:2 * P], gateb_sb[:], start=False, stop=True).then_inc(tr_ready, 1)

            def ranks(r, job):
                pe.wait_ge(tr_taken, job)
                pe.wait_ge(mask_ready, r + 1)
                nc.tensor.matmul(b7[:, 0:E], tri[:], mask[:], start=True, stop=False)
                nc.tensor.matmul(b7[:, 0:E], ones[:], seen[:], start=False, stop=True).then_inc(tr_ready, 1)

            def pe_head(n, r, par, first, last):
                base = 3 if first else tr_base(r)
                for kb in range(KEYB):
                    if kb + 1 < KEYB:
                        scores(par, kb + 1, n * KEYB + kb)
                    elif not last:
                        pe.wait_ge(tr_taken, base + (3 if first else 6))
                        scores(1 - par, 0, n * KEYB + kb)
                    weighted(n, par, kb)
                    if first:
                        if kb in (5, 7, 9):
                            stacks((kb - 5) // 2, n + 1, base + (kb - 5) // 2)
                    elif not last:
                        if kb == 1: out_transpose(r, base)
                        if kb == 5: stacks(0, n + 1, base + 1)
                        if kb == 6: t_transpose(r, 1 - par, base + 2)
                        if kb == 7: stacks(1, n + 1, base + 3)
                        if kb == 8: logits(base + 4)
                        if kb == 9: stacks(2, n + 1, base + 5)
                        if kb == 10: ranks(r, base + 6)
                    else:
                        if kb == 1: out_transpose(r, base)
                        if kb == 5: t_transpose(r, 1 - par, base + 1)
                        if kb == 7: logits(base + 2)
                        if kb == 9: ranks(r, base + 3)

            pe.wait_ge(acc_taken, TOK_ACC + NT)
            for g in range(3):
                stacks(g, 0, g)
            pe.wait_ge(tr_taken, 3)
            scores(0, 0, None)
            pe_head(0, None, 0, True, False)
            with pe.Fori(0, 5) as i:
                for p in (0, 1):
                    pe_head(i * 2 + (1 + p), i * 2 + p, 1 - p, False, False)
            pe_head(NT - 1, NT - 2, 1, False, True)
            base = tr_base(NT - 2) + 4
            out_transpose(NT - 1, base)
            t_transpose(NT - 1, 1, base + 1)
            logits(base + 2)
            ranks(NT - 1, base + 3)
            pe.wait_ge(tr_taken, base + 4)
            pe.wait_ge(slots_ready, NT)
            nc.tensor.matmul(b7[:, 0:E], ones[:], seen[:], start=True, stop=True).then_inc(tr_ready, 1)

            pe.wait_ge(w_in, 16 * 12)
            pe.wait_ge(plan_ready, 1)
            pe.wait_ge(tr_taken, base + 5)

            def x_transpose(j, r, n_loaded):
                pe.wait_ge(x_in[r], n_loaded)
                o = bank(7 * r)
                nc.tensor.transpose(o[:, 0:P], xt[r][:, 0:P], ident[:])
                nc.tensor.transpose(o[0:CB, P:2 * P], xt[r][:, P:C], ident[:]).then_inc(x_read, 1)

            def mlp1(j, r, wait):
                ex = pe.value_load(ej_i[0:1, bass.ds(j, 1)], min_val=0, max_val=E - 1)
                pe.wait_ge(xT_ready, j + 1)
                if wait:
                    pe.wait_ge(lin_ready, j - 1)
                for half in range(2):
                    o = bank(1 + 2 * half + r)[:, 0:FF]
                    nc.tensor.matmul(o, xtT[r][:, 0:P], w1a_sb[:, bass.ds(ex * 768 + half * FF, FF)], start=True, stop=False)
                    nc.tensor.matmul(o, xtT[r][0:CB + 1, P:2 * P], w1b_sb[0:CB + 1, bass.ds(ex * 768 + half * FF, FF)],
                                     start=False, stop=True).then_inc(h_done, 1)

            def mlp2(j, r, wait, b2_count):
                pe.wait_ge(actv_ready, j + 1)
                if wait:
                    pe.wait_ge(aT_ready, j)
                for c in range(3):
                    last = nc.tensor.transpose(bank(5)[:, c * P:(c + 1) * P], actv[r][:, c * P:(c + 1) * P], ident[:])
                last.then_inc(aT_psum, 1)
                ex = pe.value_load(ej_i[0:1, bass.ds(j, 1)], min_val=0, max_val=E - 1)
                if wait:
                    pe.wait_ge(y_sb, j)
                pe.wait_ge(b2_in[r], b2_count)
                o = bank(6)[:, 0:C]
                nc.tensor.matmul(o, ones[0:1, :], b2t[r], start=True, stop=False)
                pe.wait_ge(aT_ready, j + 1)
                for c in range(3):
                    last = nc.tensor.matmul(o, actT[r][:, c * P:(c + 1) * P], w2_sb[:, bass.ds((ex * 3 + c) * C, C)],
                                            start=False, stop=(c == 2))
                last.then_inc(y_psum, 1)

            pe.wait_ge(xT_ones, 2)
            x_transpose(0, 0, 16)
            x_transpose(1, 1, 16)
            mlp1(0, 0, False)
            mlp1(1, 1, False)
            mlp2(0, 0, False, 16)
            with pe.Fori(1, MT // 2) as i:
                x_transpose(i * 2, 0, i * 16 + 16)
                mlp1(i * 2, 0, True)
                mlp2(i * 2 - 1, 1, True, i * 16)
                x_transpose(i * 2 + 1, 1, i * 16 + 16)
                mlp1(i * 2 + 1, 1, True)
                mlp2(i * 2, 0, True, i * 16 + 16)
            mlp2(MT - 1, 1, True, 16 * (MT // 2))

        @block.scalar
        def _(act):
            acts = [0]

            def act_job():
                acts[0] += 1
                act.wait_ge(act_ready, acts[0])
                return bank(2 + (acts[0] - 1) % 2)

            act.wait_ge(small_in, 16 * 10)

            def y_copy(i, b):
                g, o = ((i % 2) * 4 + i // 2, (i % 2) * 4 + 2 + i // 2) if i < 2 * LAYERS else (8, 9)
                src = act_job()
                nc.scalar.activation(yT[:, b * NPIX:(b + 1) * NPIX], src[:, 0:NPIX], ACT.Identity,
                                     bias=cols_sb[:, o:o + 1], scale=cols_sb[:, g:g + 1]).then_inc(act_taken, 1)

            for l in range(LAYERS):
                for b in range(NB):
                    y_copy(2 * l, b)
                    for hp in range(2):
                        job = 2 * NB * l + 2 * b + hp
                        act.wait_ge(kmax_ready, job + 1)
                        for s in range(2):
                            h = 2 * hp + s
                            last = nc.scalar.activation(kT[:, h, b * NPIX:(b + 1) * NPIX],
                                                        bank(4 + job % 2)[:, s * NPIX:(s + 1) * NPIX], ACT.Exp,
                                                        bias=knmax[:, h, b:b + 1], accum_out=ksum[:, h, b:b + 1])
                        last.then_inc(kt_taken, 1)
                    for t in (2 * b, 2 * b + 1):
                        src = act_job()
                        nc.scalar.activation(v_tok[:, t, :], src, ACT.Identity).then_inc(act_taken, 1)
                        act.wait_ge(acc_taken, NT_IMG + l * (3 * NT_IMG + NB) + t + 1)
                        nc.scalar.activation(q_tok[:, t, :], q_tok[:, t, :], ACT.Exp).then_inc(qexp_ready, 1)
                for t in range(NT_IMG):
                    act.wait_ge(trk_ready, NT_IMG * l + t + 1)
                    nc.scalar.activation(k_tok[:, t, :], bank(7), ACT.Identity).then_inc(trk_taken, 1)
                for b in range(NB):
                    y_copy(2 * l + 1, b)
                    for hp in range(2):
                        src = act_job()
                        for s in range(2):
                            h = 2 * hp + s
                            last = nc.scalar.activation(mlp_hid[:, h, b * NPIX:(b + 1) * NPIX], src[:, s * NPIX:(s + 1) * NPIX],
                                                        ACT.Gelu, bias=cols_sb[:, 10 + 4 * l + h:11 + 4 * l + h])
                        last.then_inc(act_taken, 1)
            for b in range(NB):
                y_copy(2 * LAYERS, b)
            for t in range(NT):
                src = act_job()
                nc.scalar.activation(hnT[t % 2][:, 0:P], src[:, 0:P], ACT.Identity)
                nc.scalar.activation(hnT[t % 2][0:CB, P:2 * P], src[0:CB, P:2 * P], ACT.Identity).then_inc(act_taken, 1)

            SETS = [ps[:, 0:QS], ps[:, QS:2 * QS]]

            def act_head(n):
                for kb in range(KEYB):
                    act.wait_ge(scores_ready, n * KEYB + (kb + 1))
                    if not isinstance(n, int) or n * KEYB + kb >= 3:
                        act.wait_ge(probs_used, n * KEYB + kb - 2)
                    nc.scalar.activation(probs[kb % 3], SETS[kb % 2], ACT.Exp, scale=0.5).then_inc(probs_ready, 1)

            act_head(0)
            with act.Fori(1, NT) as i:
                act_head(i)

            act.wait_ge(wmax_ready, 1)
            nc.scalar.activation(wexp, wexp, ACT.Exp).then_inc(wexp_ready, 1)

            def x_copy(j, r):
                act.wait_ge(x_read, j + 1)
                o = bank(7 * r)
                nc.scalar.activation(xtT[r][:, 0:P], o[:, 0:P], ACT.Identity)
                nc.scalar.activation(xtT[r][0:CB, P:2 * P], o[0:CB, P:2 * P], ACT.Identity).then_inc(xT_ready, 1)

            def sigmoid(j, r):
                act.wait_ge(glu_ready, j + 1)
                nc.scalar.activation(sig[r], glu[r], ACT.Sigmoid, scale=1.702).then_inc(sig_ready, 1)

            def y_tile(j, r, count):
                act.wait_ge(y_psum, j + 1)
                if count is not None:
                    act.wait_ge(y_out[r], count)
                nc.scalar.activation(yt[r], bank(6)[:, 0:C], ACT.Identity).then_inc(y_sb, 1)
                act.wait_ge(y_sb, j + 1)
                act.dma_start(ys[bass.ds(j * P, P), :], yt[r]).then_inc(y_out[r], 16)

            x_copy(0, 0)
            x_copy(1, 1)
            sigmoid(0, 0)
            sigmoid(1, 1)
            y_tile(0, 0, None)
            x_copy(2, 0)
            sigmoid(2, 0)
            y_tile(1, 1, None)
            x_copy(3, 1)
            sigmoid(3, 1)
            y_tile(2, 0, 16)
            with act.Fori(2, MT // 2) as i:
                x_copy(i * 2, 0)
                sigmoid(i * 2, 0)
                y_tile(i * 2 - 1, 1, i * 16 - 16)
                x_copy(i * 2 + 1, 1)
                sigmoid(i * 2 + 1, 1)
                y_tile(i * 2, 0, i * 16)
            y_tile(MT - 1, 1, 16 * (MT // 2 - 1))
            for t in range(NT):
                act.wait_ge(g_used, t + 1)
                act.dma_start(out[t], h_res[:, t, :]).then_inc(final_out, 16)
            act.wait_ge(final_out, 16 * NT)

        @block.vector
        def _(dve):
            step = Chain(dve, dve_step)
            acc, lns = [0], [0]

            def acc_job():
                acc[0] += 1
                dve.wait_ge(acc_ready, acc[0])
                return bank((acc[0] - 1) % 2)

            def layer_norm(srcs, dsts):
                n = len(srcs)
                for s, x in enumerate(srcs):
                    step(nc.vector.bn_stats(stat[:, s, :], x))
                for s in range(n):
                    last = nc.vector.bn_aggr(mv[:, s, :], stat[:, s, :])
                last.then_inc(mv_ready, 1)
                lns[0] += 1
                dve.wait_ge(rstd_ready, lns[0])
                dve.wait_ge(mv_ready, lns[0])
                for s, (x, y) in enumerate(zip(srcs, dsts)):
                    last = nc.vector.tensor_scalar(y, x, mv[:, s, 0:1], rstd[:, s:s + 1], ALU.subtract, ALU.mult)
                last.then_inc(y_ready, 1)

            def image_norm(b):
                layer_norm([x_res[:, 2 * b + s, :] for s in range(2)], [x_nrm[:, 2 * b + s, :] for s in range(2)])

            for t in range(NT_IMG):
                src = acc_job()
                nc.vector.tensor_copy(x_res[:, t, :], src[:, 0:D]).then_inc(acc_taken, 1)
                dve.wait_ge(acc_taken, acc[0])
                if t % 2:
                    image_norm(t // 2)

            def residual(t):
                src = acc_job()
                nc.vector.tensor_tensor(x_res[:, t, :], src[:, 0:D], x_res[:, t, :], ALU.add).then_inc(acc_taken, 1)
                dve.wait_ge(acc_taken, acc[0])

            for l in range(LAYERS):
                def q_finish(t):
                    dve.wait_ge(qexp_ready, NT_IMG * l + t + 1)
                    step(nc.vector.reduce_sum(qsum[:, t, :], q_tok[:, t, :].rearrange("p (h d) -> p h d", h=8), AX.X))
                    nc.vector.reciprocal(qrec[:, t, :], qsum[:, t, :]).then_inc(qrec_ready, 1)

                for b in range(NB):
                    for hp in range(2):
                        job = 2 * NB * l + 2 * b + hp
                        dve.wait_ge(kt_ready, job + 1)
                        nc.vector.tensor_reduce(knmax[:, 2 * hp:2 * hp + 2, b],
                                                bank(4 + job % 2).rearrange("p (h n) -> p h n", h=2), AX.X, ALU.max,
                                                negate=True).then_inc(kmax_ready, 1)
                    for t in (2 * b, 2 * b + 1):
                        src = acc_job().rearrange("p (h d) -> p h d", h=8)
                        step(nc.vector.reduce_max(qmax[:, t, :], src, AX.X))
                        nc.vector.tensor_tensor(q_tok[:, t, :].rearrange("p (h d) -> p h d", h=8), src,
                                                qmax[:, t, :].unsqueeze(2).broadcast_to([P, 8, HD]),
                                                ALU.subtract).then_inc(acc_taken, 1)
                        if t:
                            q_finish(t - 1)
                q_finish(NT_IMG - 1)
                for b in range(NB):
                    for t in (2 * b, 2 * b + 1):
                        dve.wait_ge(trq_ready, NT_IMG * l + t + 1)
                        nc.vector.tensor_copy(qT[:, :, t * P:(t + 1) * P],
                                              bank(6).rearrange("p (h n) -> p h n", h=NPAIR)).then_inc(trq_taken, 1)
                    src = acc_job().rearrange("p (h n) -> p h n", h=NPAIR)
                    nc.vector.tensor_copy(ctx_bd[0:HD, b, :, 0:HD], src[0:HD, :, 0:HD])
                    nc.vector.tensor_copy(ctx_bd[HD:P, b, :, HD:P], src[HD:P, :, HD:P]).then_inc(acc_taken, 1)
                dve.wait_ge(kt_taken, 2 * NB * (l + 1))
                step(nc.vector.reciprocal(krec, ksum))
                step(nc.vector.tensor_scalar(krec8, krec, HD ** -0.5, None, ALU.mult))

                def ctx_w_copy(b):
                    dve.wait_ge(ctxw_ready, NB * l + b + 1)
                    nc.vector.tensor_tensor(ctx_w[:, b, :, :], bank(7).rearrange("p (h n) -> p h n", h=NPAIR),
                                            krec8[:, :, b:b + 1].broadcast_to([P, NPAIR, D]),
                                            ALU.mult).then_inc(ctxw_taken, 1)

                ctx_w_copy(0)
                for b in range(NB):
                    if b + 1 < NB:
                        ctx_w_copy(b + 1)
                    residual(2 * b)
                    residual(2 * b + 1)
                    image_norm(b)
                for b in range(NB):
                    residual(2 * b)
                    residual(2 * b + 1)
                    image_norm(b)

            for b in range(NB):
                for s in range(2):
                    src = acc_job()
                    nc.vector.tensor_copy(h_res[:, 3 * b + s, :], src[:, 0:C]).then_inc(acc_taken, 1)
            dve.wait_ge(acc_taken, acc[0])
            dve.wait_ge(small_in, 16 * 10)

            def qv_copy(t):
                src = acc_job()
                nc.vector.tensor_copy(qv[:, t, :], src[:, 0:2 * C]).then_inc(acc_taken, 1)

            for t in range(NT):
                layer_norm([h_res[:, t, :]], [h_nrm[t % 2]])
                if t:
                    qv_copy(t - 1)
            qv_copy(NT - 1)
            dve.wait_ge(acc_taken, acc[0])

            b7 = bank(7)
            b7h = bank(7).bitcast(f16)

            def heads(ap):
                return ap.rearrange("p (h d) -> p h d", h=NH)

            def per_head(ap):
                return ap.unsqueeze(2).broadcast_to([P, NH, DH])

            def prep(n):
                qh = qv[:, bass.ds(n, 1), 0:C].rearrange("p a c -> p (a c)")
                step(nc.vector.tensor_tensor(sq[:], qh, qh, ALU.mult))
                nc.vector.reduce_sum(ss[:], heads(sq[:]), AX.X).then_inc(ss_ready, 1)
                dve.wait_ge(nrm_ready, n + 1)
                step(nc.vector.tensor_scalar(nrmc[:], nrm[:], 1e-12, None, ALU.max))
                step(nc.vector.reciprocal(rn[:], nrmc[:]))
                step(nc.vector.tensor_tensor(heads(qn[:]), heads(qh), per_head(rn[:]), ALU.mult))
                nc.vector.tensor_copy(key_tok[:, :, 0:16], heads(qn[:]))
                step(nc.vector.tensor_tensor(sq[:], qn[:], qn[:], ALU.mult))
                nc.vector.tensor_tensor(key_tok[:, :, 32:48], heads(qn[:]), key_tok[:, :, 0:16], ALU.subtract)
                step(nc.vector.reduce_sum(aa[:], heads(sq[:]), AX.X))
                nc.vector.tensor_copy(key_tok[:, :, 16:32], key_tok[:, :, 0:16])
                nc.vector.tensor_copy(key_tok[:, :, 48:64], key_tok[:, :, 32:48])
                step(nc.vector.tensor_copy(key_tok[:, :, 64:65], aa[:].unsqueeze(2)))
                nc.vector.tensor_copy(qry_tok[:, :, 0:16], key_tok[:, :, 0:16])
                nc.vector.tensor_copy(qry_tok[:, :, 32:48], key_tok[:, :, 0:16])
                nc.vector.tensor_copy(qry_tok[:, :, 16:32], key_tok[:, :, 32:48])
                nc.vector.tensor_copy(qry_tok[:, :, 48:64], key_tok[:, :, 32:48])
                step(nc.vector.tensor_tensor(key_tok[:, :, 65:66], aa[:].unsqueeze(2), key_tok[:, :, 64:65], ALU.subtract))
                nc.vector.tensor_copy(qry_tok[:, :, 66:68], key_tok[:, :, 64:66]).then_inc(stack_ready, 1)

            def stack_copy(g, par, job):
                dve.wait_ge(tr_ready, job + 1)
                src = b7h[0:STK, :].rearrange("p (s n) -> p s n", s=8)
                kv = keysT[par].rearrange("p (t h) -> p h t", h=NH)
                qv_ = qrysT[par].rearrange("p (h t) -> p h t", h=NH)
                lo, hi = 8 * g, 8 * g + 8
                nk = max(0, min(hi, NH) - lo)
                if nk and nk < 8:
                    nc.vector.tensor_copy(kv[:, lo:lo + nk, :], src[:, 0:nk, :])
                if nk == 8:
                    nc.vector.tensor_copy(kv[:, lo:hi, :], src).then_inc(tr_taken, 1)
                else:
                    nc.vector.tensor_copy(qv_[:, lo + nk - NH:hi - NH, :], src[:, nk:8, :]).then_inc(tr_taken, 1)

            def sums_copy(r):
                dve.wait_ge(probs_used, r * KEYB + KEYB)
                nc.vector.tensor_copy(o_acc[:], bank(6)[:, 0:QW]).then_inc(oacc_ready, 1)

            def output(r, job):
                dve.wait_ge(tr_ready, job + 1)
                src = b7[:, 0:QW].rearrange("p (c g d) -> p c g d", c=3, g=QG)
                step(nc.vector.reciprocal(o_rec[:].unsqueeze(3), src[:, :, :, 16:17]))
                dst = o_nrm[:].rearrange("p (g c d) -> p c g d", g=QG, c=3)
                nc.vector.tensor_tensor(dst, src[:, :, :, 0:DH], o_rec[:].unsqueeze(3).broadcast_to([P, 3, QG, DH]),
                                        ALU.mult).then_inc(onrm_ready, 1)
                nc.vector.tensor_copy(bank_mark[:], ones[:, 0:1]).then_inc(tr_taken, 1)

            def norms(r, par):
                hr = h_res[:, bass.ds(r, 1), :].rearrange("p a c -> p (a c)")
                dve.wait_ge(h_ready, r + 1)
                step(nc.vector.bn_stats(stat[:, 0, :], hr))
                nc.vector.memset(bank_mark[:], 0.0)
                nc.vector.bn_aggr(mv[:, 0, :], stat[:, 0, :]).then_inc(lmv_ready, 1)
                dve.wait_ge(lrstd_ready, r + 1)
                dve.wait_ge(lmv_ready, r + 1)
                step(nc.vector.tensor_scalar(ln[:], hr, mv[:, 0, 0:1], rstd[:, 0:1], ALU.subtract, ALU.mult))
                step(nc.vector.tensor_tensor(sq[:], ln[:], ln[:], ALU.mult))
                nc.vector.reduce_sum(ms[:], sq[:], AX.X).then_inc(ms_ready, 1)
                dve.wait_ge(rms_ready, r + 1)
                dve.wait_ge(rows_out, r * (16 * TOPK) + 16)
                nc.vector.scalar_tensor_tensor(t_row[:], ln[:], rms[:], nscale_sb[:], ALU.mult,
                                               ALU.mult).then_inc(t_ready, 1)

            def tT_copy(job):
                dve.wait_ge(tr_ready, job + 1)
                nc.vector.tensor_copy(tT[:, 0:P], b7[:, 0:P])
                nc.vector.tensor_copy(tT[0:CB, P:2 * P], b7[0:CB, P:2 * P]).then_inc(tr_taken, 1)

            def choose(r, job):
                dve.wait_ge(tr_ready, job + 1)
                nc.vector.tensor_copy(logit[:], b7[:, 0:E]).then_inc(tr_taken, 1)
                held_wait(dve, tr_taken, job + 1)
                step(nc.vector.max(top8[:], logit[:]))
                nc.vector.tensor_copy(top_v[:, bass.ds(r, 1), :].rearrange("p a k -> p (a k)"), top8[:, 0:TOPK])
                step(nc.vector.max_index(top_i[:], top8[:], logit[:]))
                step(nc.vector.tensor_copy(top_f[:], top_i[:, 0:TOPK]))
                step(nc.vector.tensor_tensor(onehot[:], iota_e[:].unsqueeze(1).broadcast_to([P, TOPK, E]),
                                             top_f[:].unsqueeze(2).broadcast_to([P, TOPK, E]), ALU.is_equal))
                nc.vector.reduce_sum(mask[:], onehot[:].rearrange("p k e -> p e k"), AX.X).then_inc(mask_ready, 1)

            def place(r, par, job):
                dve.wait_ge(tr_ready, job + 1)
                nc.vector.tensor_tensor(slot_e[:], b7[:, 0:E], bucket0[:], ALU.add).then_inc(tr_taken, 1)
                dve.wait_ge(tr_taken, job + 1)
                step(nc.vector.tensor_tensor(slot_oh[:], onehot[:], slot_e[:].unsqueeze(1).broadcast_to([P, TOPK, E]), ALU.mult))
                step(nc.vector.tensor_tensor(seen[:], seen[:], mask[:], ALU.add))
                step(nc.vector.reduce_sum(slot_f[:], slot_oh[:], AX.X))
                nc.vector.tensor_copy(slot_all[:, bass.ds(r, 1), :].rearrange("p a k -> p (a k)"), slot_f[:])
                nc.vector.tensor_copy(top_all[:, bass.ds(r, 1), :].rearrange("p a k -> p (a k)"), top_f[:])
                nc.vector.tensor_copy(slot_u[:], slot_f[:]).then_inc(slots_ready, 1)

            def dve_head(n, r, par, first, last):
                base = 3 if first else tr_base(r)
                if not first:
                    sums_copy(r)
                    output(r, base)
                if not last:
                    prep(n + 1)
                if first:
                    for g in range(3):
                        stack_copy(g, 1 - par, base + g)
                elif not last:
                    norms(r, 1 - par)
                    stack_copy(0, 1 - par, base + 1)
                    tT_copy(base + 2)
                    stack_copy(1, 1 - par, base + 3)
                    choose(r, base + 4)
                    stack_copy(2, 1 - par, base + 5)
                    place(r, 1 - par, base + 6)
                else:
                    norms(r, 1 - par)
                    tT_copy(base + 1)
                    choose(r, base + 2)
                    place(r, 1 - par, base + 3)

            dve.wait_ge(consts_ready, NCONST + 2)
            prep(0)
            for g in range(3):
                stack_copy(g, 0, g)
            dve_head(0, None, 0, True, False)
            before = step.n
            with dve.Fori(0, 5) as i:
                for p in (0, 1):
                    step.rebase(i * (2 * DVE_STEPS) + (before + DVE_STEPS * p))
                    dve_head(i * 2 + (1 + p), i * 2 + p, 1 - p, False, False)
                    assert step.n == DVE_STEPS, step.n
            step.rebase(before + 10 * DVE_STEPS)
            dve_head(NT - 1, NT - 2, 1, False, True)
            base = tr_base(NT - 2) + 4
            sums_copy(NT - 1)
            output(NT - 1, base)
            norms(NT - 1, 1)
            tT_copy(base + 1)
            choose(NT - 1, base + 2)
            place(NT - 1, 1, base + 3)
            dve.wait_ge(slots_ready, NT)
            dve.wait_ge(tr_ready, base + 5)
            nc.vector.tensor_copy(cnt, b7[:, 0:E]).then_inc(tr_taken, 1)
            dve.wait_ge(tr_taken, base + 5)
            step(nc.vector.tensor_tensor(slot_e[:], cnt, bucket0[:], ALU.add))
            nc.vector.tensor_copy(pad0_i, slot_e[0:1, :]).then_inc(cnt_ready, 1)
            step(nc.vector.tensor_tensor(over, cnt.unsqueeze(2).broadcast_to([P, E, NT]),
                                         edges[:].unsqueeze(1).broadcast_to([P, E, NT]), ALU.is_gt))
            step(nc.vector.reduce_sum(tiles_e, over, AX.X))
            step(nc.vector.tensor_tensor_scan(ends, ones[:, 0:E], tiles_e, 0.0, ALU.mult, ALU.add))
            step(nc.vector.tensor_tensor(done_e, ends[0:1, :].unsqueeze(1).broadcast_to([1, MT, E]),
                                         iota_j[0:1, :].unsqueeze(2).broadcast_to([1, MT, E]), ALU.is_le))
            step(nc.vector.reduce_sum(ej, done_e, AX.X))
            step(nc.vector.tensor_tensor(done_t, done_e, tiles_e[0:1, :].unsqueeze(1).broadcast_to([1, MT, E]), ALU.mult))
            step(nc.vector.reduce_sum(sj, done_t, AX.X))
            step(nc.vector.tensor_tensor(tmpj, iota_j[0:1, :], sj, ALU.subtract))
            step(nc.vector.tensor_scalar(rowj, ej, float(BUCKET), None, ALU.mult))
            step(nc.vector.scalar_tensor_tensor(row_i, tmpj, float(P), rowj, ALU.mult, ALU.add))
            nc.vector.tensor_scalar(ej_i, ej, float(E - 1), None, ALU.min).then_inc(plan_ready, 1)
            nc.vector.tensor_tensor(wexp, top_v[:, :, 0:TOPK], top_v[:, :, 0:1].broadcast_to([P, NT, TOPK]),
                                    ALU.subtract).then_inc(wmax_ready, 1)
            dve.wait_ge(wexp_ready, 1)
            step(nc.vector.reduce_sum(wsum, wexp, AX.X))
            step(nc.vector.reciprocal(wrec, wsum))
            step(nc.vector.tensor_tensor(wgt, wexp, wrec.unsqueeze(2).broadcast_to([P, NT, TOPK]), ALU.mult))

            step(nc.vector.tensor_tensor(ends, ends, tiles_e, ALU.subtract))
            step(nc.vector.scalar_tensor_tensor(shift, ends, float(P), bucket0[:], ALU.mult, ALU.subtract))
            step(nc.vector.tensor_tensor(choice, iota_e[:].unsqueeze(1).broadcast_to([P, NT * TOPK, E]),
                                         top_all[:].rearrange("p t k -> p (t k)").unsqueeze(2).broadcast_to([P, NT * TOPK, E]),
                                         ALU.is_equal))
            step(nc.vector.tensor_tensor(choice, choice, shift.unsqueeze(1).broadcast_to([P, NT * TOPK, E]), ALU.mult))
            step(nc.vector.reduce_sum(wexp.rearrange("p t k -> p (t k)"), choice, AX.X))
            nc.vector.tensor_tensor(ys_row[:], slot_all[:], wexp, ALU.add).then_inc(place_ready, 1)

            for r in range(2):
                nc.vector.memset(xtT[r][CB:CB + 1, P:2 * P], 1.0).then_inc(xT_ones, 1)

            def clip(j, r):
                dve.wait_ge(h_done, j * 2 + 1)
                if not isinstance(j, int) or j >= 2:
                    dve.wait_ge(actv_ready, j - 1)
                nc.vector.tensor_scalar(glu[r], bank(1 + r)[:, 0:FF], 7.0, None, ALU.min).then_inc(glu_ready, 1)
                dve.wait_ge(h_done, j * 2 + 2)
                nc.vector.tensor_scalar(lin[r], bank(3 + r)[:, 0:FF], -7.0, 7.0, ALU.max, ALU.min).then_inc(lin_ready, 1)
                dve.wait_ge(lin_ready, j + 1)
                nc.vector.scalar_tensor_tensor(prod[r], lin[r], 1.0, glu[r], ALU.add, ALU.mult).then_inc(prod_ready, 1)

            def actT_copy(j, r):
                dve.wait_ge(aT_psum, j + 1)
                nc.vector.tensor_copy(actT[r], bank(5)[:, 0:FF]).then_inc(aT_ready, 1)

            clip(0, 0)
            clip(1, 1)
            actT_copy(0, 0)
            with dve.Fori(1, MT // 2) as i:
                clip(i * 2, 0)
                actT_copy(i * 2 - 1, 1)
                clip(i * 2 + 1, 1)
                actT_copy(i * 2, 0)
            actT_copy(MT - 1, 1)

            dve.wait_ge(base_ready, NT)
            for t in range(NT):
                dve.wait_ge(g_in[t % 3], 16 * TOPK * (t // 3 + 1))
                for k in range(TOPK):
                    ins = nc.vector.scalar_tensor_tensor(h_res[:, t, :], gath[t % 3][:, k, :], wgt[:, t, k:k + 1],
                                                         h_res[:, t, :], ALU.mult, ALU.add)
                    if k < TOPK - 1:
                        step(ins)
                    else:
                        ins.then_inc(g_used, 1)


def kernel(**inputs):
    import numpy as np
    import concourse.bacc as bacc
    from concourse import mybir
    from concourse.bass_utils import run_bass_kernel_spmd as run

    a = {k.replace("L0_", ""): np.asarray(v) for k, v in inputs.items()}
    cc = np.ascontiguousarray

    def fold(w, k):
        return cc(np.moveaxis(w.reshape((k, 128) + w.shape[1:]), 0, 1))

    x = a["x"].reshape(4, 32, 16, 8, 16, 8).transpose(0, 1, 3, 5, 2, 4)
    w1 = a["ffn_mlp1_w"].reshape(16, 384, 2, 192).transpose(3, 0, 2, 1).reshape(192, 16 * 768)
    b1 = a["ffn_mlp1_b"].reshape(16, 384, 2).transpose(0, 2, 1).reshape(1, 16 * 768)
    wqv = np.concatenate([a["attn_Wq"].T, a["attn_Wv"].T], 1)
    bqv = np.concatenate([a["attn_bq"], a["attn_bv"]])[None]
    arrays = {
        "patches": cc(x.reshape(4, 128, 16, 256)),
        "conv_w": cc(a["tok_conv_w"].reshape(128, 2048).T.reshape(128, 16, 128)),
        "cols": cc(np.concatenate([a["tok_ln1_g"], a["tok_ln1_b"], a["tok_ln2_g"], a["tok_ln2_b"],
                                   a["tok_lnf_g"][None], a["tok_lnf_b"][None],
                                   a["tok_ff1_b"].reshape(8, 128)], 0).T),
        "rows": cc(np.concatenate([a["tok_conv_b"], a["tok_out_b"].ravel(), a["tok_ff2_b"].ravel(),
                                   a["tok_head_b"]])[None]),
        "qkv_w": cc(a["tok_qkv_w"].transpose(1, 0, 2)),
        "out_w": cc(a["tok_out_w"].reshape(2, 4, 128, 128).transpose(2, 0, 1, 3)),
        "ff1_w": cc(a["tok_ff1_w"].transpose(1, 0, 2)),
        "ff2_w": cc(a["tok_ff2_w"].reshape(2, 4, 128, 128).transpose(2, 0, 1, 3)),
        "head_w": cc(a["tok_head_w"]),
        "txt": cc(a["txt"]),
        "wqv_a": cc(wqv[0:128]),
        "wqv_b": cc(np.concatenate([wqv[128:], bqv], 0)),
        "gate_a": cc(a["ffn_gate_w"].T[0:128]),
        "gate_b": cc(np.concatenate([a["ffn_gate_w"].T[128:], a["ffn_gate_b"][None]], 0)),
        "nscale": cc(a["ffn_norm_scale"][None]),
        "w1_a": cc(w1[0:128]),
        "w1_b": cc(np.concatenate([w1[128:], b1], 0)),
        "w2": cc(fold(a["ffn_mlp2_w"].transpose(2, 0, 1), 3).transpose(0, 2, 1, 3).reshape(128, 16 * 3 * 192)),
        "b2": cc(a["ffn_mlp2_b"]),
    }
    nc = bacc.Bacc("TRN2", target_bir_lowering=False, num_devices=1)
    args = [nc.dram_tensor(n, v.shape, mybir.dt.from_np(v.dtype), kind="ExternalInput").ap() for n, v in arrays.items()]
    f32 = mybir.dt.float32
    out = nc.dram_tensor("out", (12, 128, 192), f32, kind="ExternalOutput").ap()
    xs = nc.dram_tensor("expert_in", (SPARE + NSPARE * P, C), f32, kind="Internal").ap()
    ys = nc.dram_tensor("expert_out", (MT * P, C), f32, kind="Internal").ap()
    fusion_kernel(nc, *args, out, xs, ys)
    r = run(nc, [arrays], core_ids=[0])
    return r.results[0]["out"].reshape(4, 384, 192)
```

```python
import concourse.bass as bass
from concourse import mybir
from contextlib import ExitStack
import math

P = 128
NB, NPIX, D, KT = 4, 256, 128, 16
NT_IMG = NB * NPIX // P
LAYERS, INNER, HD, MLP = 2, 512, 64, 512
NPAIR = INNER // P
C, NH, DH = 192, 12, 16
NT = 12
KEYB = 12
QS = 1536
CB = C - P
QG = 4
QW = QS // QG
STK = 68
E, TOPK, FF = 16, 4, 384
BUCKET = QS + P
SPARE = E * BUCKET
MT = 64
NSPARE = MT - TOPK * NT
COMB = C
TOKEN = C + E
RW = C + E + 1
DUMP = NT * P
TOK_ACC = NT_IMG * 2 + LAYERS * (3 * NT_IMG + NB)


def fusion_kernel(nc, patches, conv_w, cols, rows, qkv_w, out_w, ff1_w, ff2_w, head_w, txt,
                  wqv_a, wqv_b, gate_a, gate_b, nscale, w1_a, w1_b, w2, b2, out, xs):
    f32, f16, i32, u32 = mybir.dt.float32, mybir.dt.float16, mybir.dt.int32, mybir.dt.uint32
    ALU, ACT, AX = mybir.AluOpType, mybir.ActivationFunctionType, mybir.AxisListType
    ctx = ExitStack()
    with ctx:
        def sb(name, shape, dt=f32):
            return ctx.enter_context(nc.sbuf_tensor(name, shape, dt))

        def sem(name):
            return ctx.enter_context(nc.semaphore(name))

        ps = ctx.enter_context(nc.psum_tensor("ps", [P, 8 * 512], f32))

        def bank(i):
            return ps[:, i * 512:(i + 1) * 512]

        big = sb("big", [P, E * 2 * 768 + E * 3 * C])
        at = [0]

        def carve(n):
            at[0] += n
            return big[:, at[0] - n:at[0]]

        patch_sb = [carve(KT * NPIX).rearrange("p (k n) -> p k n", k=KT) for _ in range(NB)]
        convw_sb = carve(KT * D).rearrange("p (k d) -> p k d", k=KT)
        qkvw_sb = carve(LAYERS * 3 * INNER).rearrange("p (l n) -> p l n", l=LAYERS)
        outw_sb = carve(LAYERS * NPAIR * D).rearrange("p (l k d) -> p l k d", l=LAYERS, k=NPAIR)
        ff1w_sb = carve(LAYERS * MLP).rearrange("p (l n) -> p l n", l=LAYERS)
        ff2w_sb = carve(LAYERS * 4 * D).rearrange("p (l k d) -> p l k d", l=LAYERS, k=4)
        k_tok = carve(NT_IMG * INNER).rearrange("p (t n) -> p t n", t=NT_IMG)
        mlp_hid = carve(4 * NT_IMG * P).rearrange("p (h n) -> p h n", h=4)
        yT = carve(NT_IMG * P)
        q_tok, v_tok, kT, qT = [big[:, i * KT * NPIX:(i + 1) * KT * NPIX] for i in range(4)]
        q_tok = q_tok.rearrange("p (t n) -> p t n", t=NT_IMG)
        v_tok = v_tok.rearrange("p (t n) -> p t n", t=NT_IMG)
        kT = kT.rearrange("p (h n) -> p h n", h=NPAIR)
        qT = qT.rearrange("p (h n) -> p h n", h=NPAIR)
        w1a_sb = big[:, 0:E * 768]
        w1b_sb = big[:, E * 768:2 * E * 768]
        w2_sb = big[:, 2 * E * 768:]

        mid = sb("mid", [P, 8448 + NH * STK])
        probs = [mid[:, i * QS:(i + 1) * QS] for i in range(3)]
        ab = mid[:, 3 * QS:5 * QS].bitcast(f16)
        keysT = [ab[0:STK, (2 * i) * QS:(2 * i + 1) * QS] for i in range(2)]
        qrysT = [ab[0:STK, (2 * i + 1) * QS:(2 * i + 2) * QS] for i in range(2)]
        vhead = [mid[:, 5 * QS + i * KEYB * 32:5 * QS + (i + 1) * KEYB * 32]
                 .rearrange("p (k d) -> p k d", k=KEYB) for i in range(2)]
        stk = mid[:, 5 * QS + 2 * KEYB * 32:5 * QS + 2 * KEYB * 32 + NH * STK].bitcast(f16)
        key_tok = stk[:, 0:NH * STK].rearrange("p (h c) -> p h c", h=NH)
        qry_tok = stk[:, NH * STK:2 * NH * STK].rearrange("p (h c) -> p h c", h=NH)
        x_res = mid[:, 0:1024].rearrange("p (t d) -> p t d", t=NT_IMG)
        x_nrm = mid[:, 1024:2048].rearrange("p (t d) -> p t d", t=NT_IMG)
        ctx_bd = mid[:, 2048:4096].rearrange("p (b k d) -> p b k d", b=NB, k=NPAIR)
        ctx_w = mid[:, 4096:6144].rearrange("p (b k d) -> p b k d", b=NB, k=NPAIR)
        wqva_sb = mid[:, 6144:6528]
        wqvb_sb = mid[0:CB + 1, 6528:6912]
        hnT = [mid[:, 6912 + 256 * i:7168 + 256 * i] for i in range(2)]
        h_nrm = [mid[:, 7424 + 192 * i:7616 + 192 * i] for i in range(2)]
        rows_sb = mid[0:1, 7808:7808 + 5 * D + C]
        headw_sb = mid[:, 8640:8640 + C]
        done_e = mid[0:1, 0:MT * E].rearrange("p (j e) -> p j e", j=MT)
        done_t = mid[0:1, MT * E:2 * MT * E].rearrange("p (j e) -> p j e", j=MT)
        over = mid[:, 2 * MT * E:2 * MT * E + E * NT].rearrange("p (e t) -> p e t", e=E)
        ej, sj, rowj, tmpj = [mid[0:1, 2304 + MT * i:2304 + MT * (i + 1)] for i in range(4)]
        combT = mid[0:E, 2560:2560 + NT * P]
        b2_sb = mid[0:E, 4096:4096 + C]
        iota_j = mid[0:1, 8448:8448 + MT]
        edges = mid[:, 8512:8512 + NT]
        xt = [mid[:, 6272 + i * RW:6272 + (i + 1) * RW] for i in range(2)]
        w_all = mid[:, 6720:6720 + MT]
        tok_all = mid[:, 6784:6784 + MT]
        tok_idx = [mid[:, 6848 + i:6849 + i].bitcast(u32) for i in range(2)]
        xtT = [mid[:, 384 + i * 256:640 + i * 256] for i in range(2)]
        glu = [mid[:, 896 + i * FF:1280 + i * FF] for i in range(2)]
        lin = [mid[:, 1664 + i * FF:2048 + i * FF] for i in range(2)]
        sig = [mid[:, 2432 + i * FF:2816 + i * FF] for i in range(2)]
        prod = [mid[:, 3200 + i * FF:3584 + i * FF] for i in range(2)]
        actv = [mid[:, 3968 + i * FF:4352 + i * FF] for i in range(2)]
        actT = [mid[:, 4736 + i * FF:5120 + i * FF] for i in range(2)]
        yt = [mid[:, 5504 + i * C:5696 + i * C] for i in range(2)]

        h_res = sb("h_res", [P, NT, C])
        qv = sb("qv", [P, NT, 2 * C])
        cols_sb = sb("cols_sb", [P, 18])
        ident = sb("ident", [P, P])
        ident16 = sb("ident16", [P, P], f16)
        ones = sb("ones", [P, P])
        tri = sb("tri", [P, P])
        zero_rows = sb("zero_rows", [P, RW])
        gatea_sb = sb("gatea_sb", [P, E])
        gateb_sb = sb("gateb_sb", [CB + 1, E])
        nscale_sb = sb("nscale_sb", [P, C])
        iota_e = sb("iota_e", [P, E])
        token_no = sb("token_no", [P, NT])
        bucket0 = sb("bucket0", [P, E])
        euler = sb("euler", [P, TOPK])
        phalf = sb("phalf", [P, NT])
        nhalf = sb("nhalf", [P, NT])
        stat = sb("stat", [P, 2, 6])
        mv = sb("mv", [P, 2, 2])
        vps = sb("vps", [P, 2])
        rstd = sb("rstd", [P, 2])
        sq = sb("sq", [P, C])
        qn = sb("qn", [P, C])
        cnt, tiles_e, ends = [qn[:, 16 * i:16 * i + 16] for i in range(3)]
        ss = sb("ss", [P, NH])
        nrm = sb("nrm", [P, NH])
        nrmc = sb("nrmc", [P, NH])
        rn = sb("rn", [P, NH])
        aa = sb("aa", [P, NH])
        o_acc = sb("o_acc", [P, QW])
        knmax, ksum, krec, krec8 = [o_acc[:, 16 * i:16 * i + 16].rearrange("p (h b) -> p h b", h=NPAIR) for i in range(4)]
        qmax, qsum, qrec = [o_acc[:, 64 * i:64 * i + 64].rearrange("p (t h) -> p t h", t=NT_IMG) for i in range(1, 4)]
        o_rec = sb("o_rec", [P, 3, QG])
        o_nrm = sb("o_nrm", [P, C])
        ej_i, row_i = [o_nrm[0:1, MT * i:MT * (i + 1)].bitcast(i32) for i in range(2)]
        pad0_i = o_nrm[0:1, 2 * MT:2 * MT + E].bitcast(i32)
        ln = sb("ln", [P, C])
        ms = sb("ms", [P, 1])
        mse = sb("mse", [P, 1])
        rms = sb("rms", [P, 1])
        t_row = sb("t_row", [P, RW])
        slot_u = sb("slot_u", [P, TOPK], u32)
        bank_mark = sb("bank_mark", [P, 1])
        tT = sb("tT", [P, 2 * P])
        logit = sb("logit", [P, E])
        top_i = sb("top_i", [P, 8], u32)
        top_f = sb("top_f", [P, TOPK])
        onehot = sb("onehot", [P, TOPK, E])
        mask = sb("mask", [P, E])
        seen = sb("seen", [P, E])
        slot_e = sb("slot_e", [P, E])
        slot_oh = sb("slot_oh", [P, TOPK, E])
        comb_all = sb("comb_all", [P, NT, E])
        gd = sb("gd", [P, TOPK])
        slot_f = gd
        wexp = sb("wexp", [P, TOPK])
        wsum = sb("wsum", [P, 1])
        wrec = sb("wrec", [P, 1])
        top8 = sb("top8", [P, 8])
        patch_in = [sem(f"patch_in{b}") for b in range(NB)]
        convw_in, rows_in, tokw_in = sem("convw_in"), sem("rows_in"), sem("tokw_in")
        small_in = sem("small_in")
        consts_ready = sem("consts_ready")
        pool_step = sem("pool_step")
        dve_step = sem("dve_step")
        acc_ready, acc_taken = sem("acc_ready"), sem("acc_taken")
        act_ready, act_taken = sem("act_ready"), sem("act_taken")
        kt_ready, kt_taken = sem("kt_ready"), sem("kt_taken")
        kmax_ready = sem("kmax_ready")
        trq_ready, trq_taken = sem("trq_ready"), sem("trq_taken")
        trk_ready, trk_taken = sem("trk_ready"), sem("trk_taken")
        ctxw_ready, ctxw_taken = sem("ctxw_ready"), sem("ctxw_taken")
        mv_ready, rstd_ready = sem("mv_ready"), sem("rstd_ready")
        y_ready = sem("y_ready")
        qexp_ready, qrec_ready, qnorm_ready = sem("qexp_ready"), sem("qrec_ready"), sem("qnorm_ready")
        w_in = sem("w_in")
        scores_ready, probs_ready, probs_used = sem("scores_ready"), sem("probs_ready"), sem("probs_used")
        stack_ready, tr_ready, tr_taken = sem("stack_ready"), sem("tr_ready"), sem("tr_taken")
        vhead_ready = sem("vhead_ready")
        ss_ready, nrm_ready = sem("ss_ready"), sem("nrm_ready")
        oacc_ready = sem("oacc_ready")
        onrm_ready, h_ready = sem("onrm_ready"), sem("h_ready")
        lmv_ready, lrstd_ready = sem("lmv_ready"), sem("lrstd_ready")
        ms_ready, rms_ready = sem("ms_ready"), sem("rms_ready")
        t_ready, mask_ready, slots_ready, rows_out = (sem("t_ready"), sem("mask_ready"), sem("slots_ready"),
                                                      sem("rows_out"))
        base_ready = sem("base_ready")
        plan_ready = sem("plan_ready")
        cnt_ready = sem("cnt_ready")
        pads_out = sem("pads_out")
        x_in, x_read = [sem("x_in0"), sem("x_in1")], sem("x_read")
        b2_in, xT_ones, x_copied = sem("b2_in"), sem("xT_ones"), sem("x_copied")
        xT_ready = sem("xT_ready")
        h_done, glu_ready, lin_ready, sig_ready = sem("h_done"), sem("glu_ready"), sem("lin_ready"), sem("sig_ready")
        prod_ready, actv_ready = sem("prod_ready"), sem("actv_ready")
        aT_psum, aT_ready = sem("aT_psum"), sem("aT_ready")
        y_psum, y_sb = sem("y_psum"), sem("y_sb")
        y_ready2, y_out = sem("y_ready2"), sem("y_out")
        gd_ready, wexp_ready, token_ready = sem("gd_ready"), sem("wexp_ready"), sem("token_ready")
        combT_psum, combT_ready = sem("combT_psum"), sem("combT_ready")
        bias_psum, bias_added = sem("bias_psum"), sem("bias_added")
        out_init, plan_consts = sem("out_init"), sem("plan_consts")

        NCONST = 18
        TR7 = 7

        def tr_base(r):
            return r * TR7 + 6

        def held_wait(eng, s, value):
            if not isinstance(value, int):
                value = eng.snap(value)
                eng.wait_ge(consts_ready, NCONST)
            eng.wait_ge(s, value)

        class Chain:
            def __init__(self, eng, s):
                self.eng, self.sem, self.base, self.n = eng, s, 0, 0

            def __call__(self, ins, held=False):
                self.n += 1
                ins.then_inc(self.sem, 1)
                (held_wait if held else type(self.eng).wait_ge)(self.eng, self.sem, self.base + self.n)

            def rebase(self, base):
                self.base, self.n = base, 0

        DVE_STEPS = 22
        POOL_STEPS = 2

        SP_PADS = 9

        def pad_bucket(eng, e):
            first = eng.value_load(pad0_i[0:1, e:e + 1], min_val=0, max_val=SPARE - P)
            eng.dma_start(xs[bass.ds(first, P), :], zero_rows[:]).then_inc(pads_out, 16)

        block = ctx.enter_context(nc.Block())

        @block.sync
        def _(sp):
            sp.dma_start(convw_sb, conv_w).then_inc(convw_in, 16)
            sp.dma_start(rows_sb, rows).then_inc(rows_in, 16)
            sp.dma_start(patch_sb[0], patches[0]).then_inc(patch_in[0], 16)
            sp.dma_start(cols_sb[:], cols).then_inc(small_in, 16)
            for b in range(1, NB):
                sp.dma_start(patch_sb[b], patches[b]).then_inc(patch_in[b], 16)
            for dst, src in ((qkvw_sb, qkv_w), (outw_sb, out_w), (ff1w_sb, ff1_w), (ff2w_sb, ff2_w),
                             (headw_sb, head_w)):
                sp.dma_start(dst, src).then_inc(tokw_in, 16)
            for dst, src in ((wqva_sb, wqv_a), (wqvb_sb, wqv_b), (gatea_sb[:], gate_a), (gateb_sb[:], gate_b),
                             (nscale_sb[:], nscale.broadcast_to([P, C]))):
                sp.dma_start(dst, src).then_inc(small_in, 16)
            for b in range(NB):
                sp.dma_start(h_res[:, 3 * b + 2, :], txt[b]).then_inc(small_in, 16)
            sp.wait_ge(acc_taken, TOK_ACC)
            for e in range(0, E, 4):
                sp.dma_start(w1a_sb[:, e * 768:(e + 4) * 768], w1_a[:, e * 768:(e + 4) * 768]).then_inc(w_in, 16)
                sp.dma_start(w1b_sb[0:CB + 1, e * 768:(e + 4) * 768], w1_b[:, e * 768:(e + 4) * 768]).then_inc(w_in, 16)
                sp.dma_start(w2_sb[:, e * 3 * C:(e + 4) * 3 * C], w2[:, e * 3 * C:(e + 4) * 3 * C]).then_inc(w_in, 16)
            sp.wait_ge(probs_used, NT * KEYB)
            sp.dma_start(b2_sb, b2).then_inc(b2_in, 16)
            sp.wait_ge(cnt_ready, 1)
            for e in range(SP_PADS):
                pad_bucket(sp, e)
            sp.wait_ge(pads_out, 16 * E)
            sp.wait_ge(rows_out, 16 * (TOPK * NT + 2))
            sp.wait_ge(plan_ready, 1)

            def load_rows(j, r, free=True):
                if free:
                    sp.wait_ge(x_read, j - 1)
                    sp.wait_ge(x_copied, j - 1)
                row = sp.value_load(row_i[0:1, bass.ds(j, 1)], min_val=0, max_val=SPARE + (NSPARE - 1) * P)
                sp.dma_start(xt[r], xs[bass.ds(row, P), :]).then_inc(x_in[r], 16)

            load_rows(0, 0, False)
            load_rows(1, 1, False)
            with sp.Fori(1, MT // 2) as i:
                for r in (0, 1):
                    load_rows(i * 2 + r, r)

        @block.gpsimd
        def _(pool):
            step = Chain(pool, pool_step)
            nc.gpsimd.memset(ident[:], 0.0).then_inc(consts_ready, 1)
            nc.gpsimd.memset(ident16[:], 0.0).then_inc(consts_ready, 1)
            nc.gpsimd.memset(ones[:], 1.0).then_inc(consts_ready, 1)
            pool.wait_ge(consts_ready, 3)
            nc.gpsimd.affine_select(out=ident[:], in_=ident[:], compare_op=ALU.not_equal, fill=1.0, base=0,
                                    pattern=[[-1, P]], channel_multiplier=1).then_inc(consts_ready, 1)
            nc.gpsimd.affine_select(out=ident16[:], in_=ident16[:], compare_op=ALU.not_equal, fill=1.0, base=0,
                                    pattern=[[-1, P]], channel_multiplier=1).then_inc(consts_ready, 1)
            nc.gpsimd.affine_select(out=tri[:], in_=ones[:], compare_op=ALU.is_gt, fill=0.0, base=0,
                                    pattern=[[1, P]], channel_multiplier=-1).then_inc(consts_ready, 1)
            nc.gpsimd.memset(zero_rows[:], 0.0).then_inc(consts_ready, 1)
            nc.gpsimd.memset(phalf[:], 0.5).then_inc(consts_ready, 1)
            nc.gpsimd.memset(nhalf[:], -0.5).then_inc(consts_ready, 1)
            nc.gpsimd.memset(mid[:, 2048:4096], 0.0).then_inc(consts_ready, 1)
            nc.gpsimd.memset(seen[:], 0.0).then_inc(consts_ready, 1)
            nc.gpsimd.memset(euler[:], math.e).then_inc(consts_ready, 1)
            for dst, pat, per_partition in ((iota_e, [[1, E]], 0), (bucket0, [[BUCKET, E]], 0), (token_no, [[P, NT]], 1)):
                nc.gpsimd.iota(dst[:], pattern=pat, base=0, channel_multiplier=per_partition,
                               allow_small_or_imprecise_dtypes=True).then_inc(consts_ready, 1)
            for i, dst in enumerate((hnT[0], hnT[1], tT)):
                pool.wait_ge(consts_ready, NCONST - 3 + i)
                nc.gpsimd.memset(dst[CB:CB + 1, P:2 * P], 1.0).then_inc(consts_ready, 1)
            pool.wait_ge(consts_ready, NCONST)
            step(nc.gpsimd.iota(zero_rows[:, TOKEN:RW].bitcast(u32), pattern=[[0, 1]], base=DUMP, channel_multiplier=1))
            pool.dma_start(xs[SPARE:SPARE + NSPARE * P, :].rearrange("(t p) c -> p t c", p=P),
                           zero_rows[:].unsqueeze(1).broadcast_to([P, NSPARE, RW])).then_inc(rows_out, 16)
            pool.dma_start(out[DUMP:DUMP + P, :], zero_rows[:, 0:C]).then_inc(rows_out, 16)

            def ln_rstd(i, n):
                pool.wait_ge(mv_ready, i + 1)
                step(nc.gpsimd.tensor_scalar(vps[:, 0:n], mv[:, 0:n, 1], 1e-5, None, ALU.add))
                nc.gpsimd.tensor_tensor(rstd[:, 0:n], vps[:, 0:n], nhalf[:, 0:n], ALU.pow).then_inc(rstd_ready, 1)

            for i in range(NB):
                ln_rstd(i, 2)
            for l in range(LAYERS):
                for t in range(NT_IMG):
                    pool.wait_ge(qrec_ready, NT_IMG * l + t + 1)
                    v = q_tok[:, t, :].rearrange("p (h d) -> p h d", h=8)
                    nc.gpsimd.tensor_tensor(v, v, qrec[:, t, :].unsqueeze(2).broadcast_to([P, 8, HD]),
                                            ALU.mult).then_inc(qnorm_ready, 1)
                for i in range(2 * NB):
                    ln_rstd(NB + 2 * NB * l + i, 2)
            for t in range(NT):
                ln_rstd(NB * (1 + 2 * LAYERS) + t, 1)

            pool.wait_ge(acc_taken, TOK_ACC + NT)
            nc.gpsimd.memset(key_tok[:, :, 66:68], -0.5).then_inc(consts_ready, 1)
            nc.gpsimd.memset(qry_tok[:, :, 64:66], -0.5).then_inc(consts_ready, 1)
            for r in range(2):
                step(nc.gpsimd.memset(vhead[r][:, :, 16:32], 0.0))
                step(nc.gpsimd.memset(vhead[r][:, :, 16:17], 1.0))

            def head_v(n, r):
                nc.gpsimd.tensor_copy(vhead[r][:, :, 0:DH], qv[:, :, bass.ds(n * DH + C, DH)]).then_inc(vhead_ready, 1)

            def norm_root(n):
                pool.wait_ge(ss_ready, n + 1)
                nc.gpsimd.tensor_tensor(nrm[:], ss[:], phalf[:, 0:NH], ALU.pow).then_inc(nrm_ready, 1)

            def route(r, par):
                pool.wait_ge(onrm_ready, r + 1)
                hr = h_res[:, bass.ds(r, 1), :].rearrange("p a c -> p (a c)")
                nc.gpsimd.tensor_tensor(hr, hr, o_nrm[:], ALU.add).then_inc(h_ready, 1)

            def route2(r, par):
                hr = h_res[:, bass.ds(r, 1), :].rearrange("p a c -> p (a c)")
                held_wait(pool, lmv_ready, r + 1)
                step(nc.gpsimd.tensor_scalar(vps[:, 0:1], mv[:, 0, 1:2], 1e-5, None, ALU.add))
                nc.gpsimd.tensor_tensor(rstd[:, 0:1], vps[:, 0:1], nhalf[:, 0:1], ALU.pow).then_inc(lrstd_ready, 1)
                held_wait(pool, ms_ready, r + 1)
                step(nc.gpsimd.tensor_scalar(mse[:], ms[:], 1.0 / C, 1e-5, ALU.mult, ALU.add))
                nc.gpsimd.tensor_tensor(rms[:], mse[:], nhalf[:, 0:1], ALU.pow).then_inc(rms_ready, 1)
                nc.gpsimd.tensor_tensor(hr, hr, ln[:], ALU.add).then_inc(base_ready, 1)

            def scatter(r, par):
                held_wait(pool, gd_ready, r + 1)
                nc.gpsimd.tensor_tensor(wexp[:], euler[:], gd[:], ALU.pow).then_inc(wexp_ready, 1)
                held_wait(pool, slots_ready, r + 1)
                for k in range(TOPK):
                    nc.gpsimd.indirect_dma_start(
                        xs[:, :], bass.IndirectOffsetOnAxis(ap=slot_u[:, k:k + 1], axis=0),
                        t_row[:], None).then_inc(rows_out, 16)

            def pool_head(n, r, par, first, last, prep2=True):
                if not first:
                    route(r, 1 - par)
                if not last:
                    if not first:
                        pool.wait_ge(oacc_ready, n)
                    head_v(n + 1, 1 - par)
                if not first:
                    route2(r, 1 - par)
                if not last and prep2:
                    norm_root(n + 2)
                if not first:
                    scatter(r, 1 - par)

            norm_root(0)
            head_v(0, 0)
            norm_root(1)
            pool_head(0, None, 0, True, False)
            before = step.n
            with pool.Fori(0, 4) as i:
                for p in (0, 1):
                    step.rebase(i * (2 * POOL_STEPS) + (before + POOL_STEPS * p))
                    pool_head(i * 2 + (1 + p), i * 2 + p, 1 - p, False, False)
                    assert step.n == POOL_STEPS, step.n
            step.rebase(before + 8 * POOL_STEPS)
            pool_head(NT - 3, NT - 4, 1, False, False)
            pool_head(NT - 2, NT - 3, 0, False, False, prep2=False)
            pool.wait_ge(tr_taken, tr_base(NT - 2))
            nc.gpsimd.iota(iota_j, pattern=[[1, MT]], base=0, channel_multiplier=0,
                           allow_small_or_imprecise_dtypes=True).then_inc(plan_consts, 1)
            pool.wait_ge(plan_consts, 1)
            nc.gpsimd.iota(edges, pattern=[[P, NT]], base=0, channel_multiplier=0,
                           allow_small_or_imprecise_dtypes=True).then_inc(plan_consts, 1)
            pool_head(NT - 1, NT - 2, 1, False, True)
            route(NT - 1, 1)
            route2(NT - 1, 1)
            scatter(NT - 1, 1)

            def expert(j, r, added=None):
                if added is not None:
                    pool.wait_ge(y_out, added * 16)
                    pool.wait_ge(y_psum, added + 1)
                pool.wait_ge(sig_ready, j + 1)
                pool.wait_ge(prod_ready, j + 1)
                nc.gpsimd.tensor_tensor(actv[r], prod[r], sig[r], ALU.mult).then_inc(actv_ready, 1)

            def add_rows(j, r):
                held_wait(pool, y_ready2, j + 1)
                nc.gpsimd.indirect_dma_start(
                    out[:, :], bass.IndirectOffsetOnAxis(ap=tok_idx[r], axis=0), yt[r], None,
                    compute_op=ALU.add).then_inc(y_out, 16)

            expert(0, 0)
            expert(1, 1)
            expert(2, 0)
            pool.wait_ge(out_init, 16)
            add_rows(0, 0)
            expert(3, 1, 1)
            add_rows(1, 1)
            with pool.Fori(1, MT // 2 - 1) as i:
                for r in (0, 1):
                    expert(i * 2 + (2 + r), r, i * 2 + r)
                    add_rows(i * 2 + r, r)
            pool.wait_ge(y_out, 16 * (MT - 2))
            add_rows(MT - 2, 0)
            pool.wait_ge(y_out, 16 * (MT - 1))
            add_rows(MT - 1, 1)
            pool.wait_ge(y_out, 16 * MT)

        @block.tensor
        def _(pe):
            acc, acts, kts = [0], [0], [0]

            def acc_job():
                if acc[0] >= 2:
                    pe.wait_ge(acc_taken, acc[0] - 1)
                acc[0] += 1
                return bank((acc[0] - 1) % 2)

            def act_job():
                if acts[0] >= 2:
                    pe.wait_ge(act_taken, acts[0] - 1)
                acts[0] += 1
                return bank(2 + (acts[0] - 1) % 2)

            def rows_bias(dst, off, n):
                nc.tensor.matmul(dst, ones[0:1, :], rows_sb[0:1, off:off + n], start=True, stop=False)

            pe.wait_ge(consts_ready, NCONST)
            pe.wait_ge(convw_in, 16)
            pe.wait_ge(rows_in, 16)
            for t in range(NT_IMG):
                if t % 2 == 0:
                    pe.wait_ge(patch_in[t // 2], 16)
                o = acc_job()[:, 0:D]
                rows_bias(o, 0, D)
                for k in range(KT):
                    last = nc.tensor.matmul(o, patch_sb[t // 2][:, k, (t % 2) * P:(t % 2) * P + P], convw_sb[:, k, :],
                                            start=False, stop=(k == KT - 1))
                last.then_inc(acc_ready, 1)
            pe.wait_ge(tokw_in, 16 * 5)
            pe.wait_ge(small_in, 16 * 10)

            def ln_transpose(i, b):
                pe.wait_ge(y_ready, NB * i + b + 1)
                o = act_job()
                for s in range(2):
                    last = nc.tensor.transpose(o[:, s * P:(s + 1) * P], x_nrm[:, 2 * b + s, :], ident[:])
                last.then_inc(act_ready, 1)

            for l in range(LAYERS):
                for b in range(NB):
                    ln_transpose(2 * l, b)
                    yb = yT[:, b * NPIX:(b + 1) * NPIX]
                    pe.wait_ge(act_taken, acts[0])
                    for hp in range(2):
                        if kts[0] >= 2:
                            pe.wait_ge(kt_taken, kts[0] - 1)
                        o = bank(4 + kts[0] % 2)
                        kts[0] += 1
                        for s in range(2):
                            h = 2 * hp + s
                            last = nc.tensor.matmul(o[:, s * NPIX:(s + 1) * NPIX],
                                                    qkvw_sb[:, l, INNER + h * P:INNER + (h + 1) * P], yb,
                                                    start=True, stop=True)
                        last.then_inc(kt_ready, 1)
                    for t in (2 * b, 2 * b + 1):
                        o = act_job()
                        nc.tensor.matmul(o, yT[:, t * P:(t + 1) * P], qkvw_sb[:, l, 2 * INNER:3 * INNER],
                                         start=True, stop=True).then_inc(act_ready, 1)
                        o = acc_job()
                        nc.tensor.matmul(o, yT[:, t * P:(t + 1) * P], qkvw_sb[:, l, 0:INNER],
                                         start=True, stop=True).then_inc(acc_ready, 1)
                for b in range(NB):
                    pe.wait_ge(kt_taken, 2 * NB * l + 2 * b + 2)
                    for t in (2 * b, 2 * b + 1):
                        pe.wait_ge(trk_taken, NT_IMG * l + t)
                        if l and t == 0:
                            pe.wait_ge(ctxw_taken, NB * l)
                        for h in range(NPAIR):
                            last = nc.tensor.transpose(bank(7)[:, h * P:(h + 1) * P], kT[:, h, t * P:(t + 1) * P], ident[:])
                        last.then_inc(trk_ready, 1)
                        pe.wait_ge(qnorm_ready, NT_IMG * l + t + 1)
                        pe.wait_ge(trq_taken, NT_IMG * l + t)
                        for h in range(NPAIR):
                            last = nc.tensor.transpose(bank(6)[:, h * P:(h + 1) * P], q_tok[:, t, h * P:(h + 1) * P], ident[:])
                        last.then_inc(trq_ready, 1)
                    pe.wait_ge(trk_taken, NT_IMG * l + 2 * b + 2)
                    pe.wait_ge(act_taken, acts[0])
                    o = acc_job()
                    for h in range(NPAIR):
                        for s in range(2):
                            last = nc.tensor.matmul(o[:, h * P:(h + 1) * P], v_tok[:, 2 * b + s, h * P:(h + 1) * P],
                                                    k_tok[:, 2 * b + s, h * P:(h + 1) * P], start=(s == 0), stop=(s == 1))
                    last.then_inc(acc_ready, 1)
                ctx_jobs = acc[0]

                def ctx_times_w(b):
                    pe.wait_ge(acc_taken, ctx_jobs - NB + b + 1)
                    pe.wait_ge(trk_taken, NT_IMG * (l + 1))
                    pe.wait_ge(ctxw_taken, NB * l + b)
                    for h in range(NPAIR):
                        last = nc.tensor.matmul(bank(7)[:, h * P:(h + 1) * P], ctx_bd[:, b, h, :], outw_sb[:, l, h, :],
                                                start=True, stop=True)
                    last.then_inc(ctxw_ready, 1)

                ctx_times_w(0)
                for b in range(NB):
                    if b + 1 < NB:
                        ctx_times_w(b + 1)
                    pe.wait_ge(ctxw_taken, NB * l + b + 1)
                    for t in (2 * b, 2 * b + 1):
                        pe.wait_ge(trq_taken, NT_IMG * l + t + 1)
                        o = acc_job()[:, 0:D]
                        rows_bias(o, D * (1 + l), D)
                        for h in range(NPAIR):
                            last = nc.tensor.matmul(o, qT[:, h, t * P:(t + 1) * P], ctx_w[:, b, h, :],
                                                    start=False, stop=(h == NPAIR - 1))
                        last.then_inc(acc_ready, 1)

                def ff2(b, hidden):
                    pe.wait_ge(act_taken, hidden)
                    for t in (2 * b, 2 * b + 1):
                        o = acc_job()[:, 0:D]
                        rows_bias(o, D * (3 + l), D)
                        for h in range(4):
                            last = nc.tensor.matmul(o, mlp_hid[:, h, t * P:(t + 1) * P], ff2w_sb[:, l, h, :],
                                                    start=False, stop=(h == 3))
                        last.then_inc(acc_ready, 1)

                for b in range(NB):
                    ln_transpose(2 * l + 1, b)
                    if b:
                        ff2(b - 1, acts[0] - 1)
                    pe.wait_ge(act_taken, acts[0])
                    for hp in range(2):
                        o = act_job()
                        for s in range(2):
                            h = 2 * hp + s
                            last = nc.tensor.matmul(o[:, s * NPIX:(s + 1) * NPIX], ff1w_sb[:, l, h * P:(h + 1) * P],
                                                    yT[:, b * NPIX:(b + 1) * NPIX], start=True, stop=True)
                        last.then_inc(act_ready, 1)
                ff2(NB - 1, acts[0])

            for b in range(NB):
                ln_transpose(2 * LAYERS, b)
                pe.wait_ge(act_taken, acts[0])
                for t in (2 * b, 2 * b + 1):
                    o = acc_job()[:, 0:C]
                    rows_bias(o, 5 * D, C)
                    nc.tensor.matmul(o, yT[:, t * P:(t + 1) * P], headw_sb, start=False, stop=True).then_inc(acc_ready, 1)
            assert acc[0] == TOK_ACC, acc[0]

            def h_transpose(t):
                pe.wait_ge(y_ready, NB * (2 * LAYERS + 1) + t + 1)
                o = act_job()
                nc.tensor.transpose(o[:, 0:P], h_nrm[t % 2][:, 0:P], ident[:])
                nc.tensor.transpose(o[0:CB, P:2 * P], h_nrm[t % 2][:, P:C], ident[:]).then_inc(act_ready, 1)

            h_transpose(0)
            for t in range(NT):
                if t + 1 < NT:
                    h_transpose(t + 1)
                pe.wait_ge(act_taken, acts[0] - (t + 1 < NT))
                o = acc_job()[:, 0:2 * C]
                nc.tensor.matmul(o, hnT[t % 2][:, 0:P], wqva_sb, start=True, stop=False)
                nc.tensor.matmul(o, hnT[t % 2][0:CB + 1, P:2 * P], wqvb_sb, start=False, stop=True).then_inc(acc_ready, 1)

            b7 = bank(7)
            b7h = bank(7).bitcast(f16)
            SETS = [ps[:, 0:QS], ps[:, QS:2 * QS]]
            oacc = bank(6)

            def stacks(g, n, job):
                pe.wait_ge(tr_taken, job)
                if g == 0:
                    pe.wait_ge(stack_ready, n + 1)
                for s in range(8):
                    k = 8 * g + s
                    src = key_tok[:, k, :] if k < NH else qry_tok[:, k - NH, :]
                    last = nc.tensor.transpose(b7h[0:STK, s * P:(s + 1) * P], src, ident16[:])
                last.then_inc(tr_ready, 1)

            def scores(n_par, kb, s):
                if s is not None:
                    pe.wait_ge(probs_ready, s)
                for c in range(3):
                    last = nc.tensor.matmul(SETS[kb % 2][:, c * 512:(c + 1) * 512], keysT[n_par][:, kb * P:(kb + 1) * P],
                                            qrysT[n_par][:, c * 512:(c + 1) * 512], start=True, stop=True)
                last.then_inc(scores_ready, 1)

            def weighted(n, par, kb):
                if kb == 0:
                    pe.wait_ge(vhead_ready, n + 1)
                    pe.wait_ge(oacc_ready, n)
                pe.wait_ge(probs_ready, n * KEYB + (kb + 1))
                for g in range(QG):
                    last = nc.tensor.matmul(oacc[32 * g:32 * g + 32, 0:QW], vhead[par][:, kb, :],
                                            probs[kb % 3][:, g * QW:(g + 1) * QW], start=(kb == 0),
                                            stop=(kb == KEYB - 1), tile_position=(0, 32 * g))
                last.then_inc(probs_used, 1)

            def out_transpose(r, job):
                pe.wait_ge(tr_taken, job)
                pe.wait_ge(oacc_ready, r + 1)
                for c in range(3):
                    last = nc.tensor.transpose(b7[:, c * P:(c + 1) * P], o_acc[:, c * P:(c + 1) * P], ident[:])
                last.then_inc(tr_ready, 1)

            def t_transpose(r, par, job):
                pe.wait_ge(tr_taken, job)
                pe.wait_ge(t_ready, r + 1)
                nc.tensor.transpose(b7[:, 0:P], t_row[:, 0:P], ident[:])
                nc.tensor.transpose(b7[0:CB, P:2 * P], t_row[:, P:C], ident[:]).then_inc(tr_ready, 1)

            def logits(job):
                pe.wait_ge(tr_taken, job)
                nc.tensor.matmul(b7[:, 0:E], tT[:, 0:P], gatea_sb[:], start=True, stop=False)
                nc.tensor.matmul(b7[:, 0:E], tT[0:CB + 1, P:2 * P], gateb_sb[:], start=False, stop=True).then_inc(tr_ready, 1)

            def ranks(r, job):
                pe.wait_ge(tr_taken, job)
                pe.wait_ge(mask_ready, r + 1)
                nc.tensor.matmul(b7[:, 0:E], tri[:], mask[:], start=True, stop=False)
                nc.tensor.matmul(b7[:, 0:E], ones[:], seen[:], start=False, stop=True).then_inc(tr_ready, 1)

            def pe_head(n, r, par, first, last):
                base = 3 if first else tr_base(r)
                for kb in range(KEYB):
                    if kb + 2 < KEYB:
                        scores(par, kb + 2, n * KEYB + (kb + 1))
                    elif not last:
                        if kb + 2 == KEYB:
                            pe.wait_ge(tr_taken, base + (3 if first else 4))
                        scores(1 - par, kb + 2 - KEYB, n * KEYB + (kb + 1))
                    weighted(n, par, kb)
                    if first:
                        if kb in (5, 7, 9):
                            stacks((kb - 5) // 2, n + 1, base + (kb - 5) // 2)
                    elif not last:
                        if kb == 1: out_transpose(r, base)
                        if kb == 2: stacks(0, n + 1, base + 1)
                        if kb == 3: stacks(1, n + 1, base + 2)
                        if kb == 4: stacks(2, n + 1, base + 3)
                        if kb == 6: t_transpose(r, 1 - par, base + 4)
                        if kb == 7: logits(base + 5)
                        if kb == 9: ranks(r, base + 6)
                    else:
                        if kb == 1: out_transpose(r, base)
                        if kb == 5: t_transpose(r, 1 - par, base + 1)
                        if kb == 7: logits(base + 2)
                        if kb == 9: ranks(r, base + 3)

            pe.wait_ge(acc_taken, TOK_ACC + NT)
            for g in range(3):
                stacks(g, 0, g)
            pe.wait_ge(tr_taken, 3)
            scores(0, 0, None)
            scores(0, 1, None)
            pe_head(0, None, 0, True, False)
            with pe.Fori(0, 4) as i:
                for p in (0, 1):
                    pe_head(i * 2 + (1 + p), i * 2 + p, 1 - p, False, False)
            pe_head(NT - 3, NT - 4, 1, False, False)
            pe_head(NT - 2, NT - 3, 0, False, False)
            pe_head(NT - 1, NT - 2, 1, False, True)
            base = tr_base(NT - 2) + 4
            out_transpose(NT - 1, base)
            t_transpose(NT - 1, 1, base + 1)
            logits(base + 2)
            ranks(NT - 1, base + 3)
            pe.wait_ge(tr_taken, base + 4)
            pe.wait_ge(slots_ready, NT)
            nc.tensor.matmul(b7[:, 0:E], ones[:], seen[:], start=True, stop=True).then_inc(tr_ready, 1)
            for t in range(NT):
                last = nc.tensor.transpose(ps[0:E, t * P:(t + 1) * P], comb_all[:, t, :], ident[:])
            last.then_inc(combT_psum, 1)
            pe.wait_ge(combT_ready, 1)
            pe.wait_ge(b2_in, 16)
            for t in range(NT):
                o = bank(t // 2)[:, (t % 2) * C:(t % 2) * C + C]
                nc.tensor.matmul(o, combT[:, t * P:(t + 1) * P], b2_sb, start=True, stop=True).then_inc(bias_psum, 1)

            pe.wait_ge(w_in, 16 * 12)
            pe.wait_ge(plan_ready, 1)
            pe.wait_ge(tr_taken, base + 5)
            pe.wait_ge(bias_added, NT // 2)

            def x_transpose(j, r, n_loaded):
                pe.wait_ge(x_in[r], n_loaded)
                o = bank(7 * r)
                nc.tensor.transpose(o[:, 0:P], xt[r][:, 0:P], ident[:])
                nc.tensor.transpose(o[0:CB, P:2 * P], xt[r][:, P:C], ident[:]).then_inc(x_read, 1)

            def mlp1(j, r, wait=True):
                ex = pe.value_load(ej_i[0:1, bass.ds(j, 1)], min_val=0, max_val=E - 1)
                pe.wait_ge(xT_ready, j + 1)
                if wait:
                    pe.wait_ge(lin_ready, j - 1)
                for half in range(2):
                    o = bank(1 + 2 * half + r)[:, 0:FF]
                    nc.tensor.matmul(o, xtT[r][:, 0:P], w1a_sb[:, bass.ds(ex * 768 + half * FF, FF)], start=True, stop=False)
                    nc.tensor.matmul(o, xtT[r][0:CB + 1, P:2 * P], w1b_sb[0:CB + 1, bass.ds(ex * 768 + half * FF, FF)],
                                     start=False, stop=True).then_inc(h_done, 1)

            def act_transpose(j, r, wait=True):
                pe.wait_ge(actv_ready, j + 1)
                if wait:
                    pe.wait_ge(aT_ready, j)
                for c in range(3):
                    last = nc.tensor.transpose(bank(5)[:, c * P:(c + 1) * P], actv[r][:, c * P:(c + 1) * P], ident[:])
                last.then_inc(aT_psum, 1)

            def mlp2(j, r, wait=True):
                ex = pe.value_load(ej_i[0:1, bass.ds(j, 1)], min_val=0, max_val=E - 1)
                pe.wait_ge(aT_ready, j + 1)
                if wait:
                    pe.wait_ge(y_sb, j)
                for c in range(3):
                    last = nc.tensor.matmul(bank(6)[:, 0:C], actT[r][:, c * P:(c + 1) * P],
                                            w2_sb[:, bass.ds((ex * 3 + c) * C, C)], start=(c == 0), stop=(c == 2))
                last.then_inc(y_psum, 1)

            pe.wait_ge(xT_ones, 2)
            x_transpose(0, 0, 16)
            x_transpose(1, 1, 16)
            mlp1(0, 0, False)
            x_transpose(2, 0, 32)
            mlp1(1, 1, False)
            act_transpose(0, 0, False)
            x_transpose(3, 1, 32)
            mlp1(2, 0)
            mlp2(0, 0, False)
            act_transpose(1, 1)
            x_transpose(4, 0, 48)
            mlp1(3, 1)
            mlp2(1, 1)
            act_transpose(2, 0)
            with pe.Fori(2, MT // 2 - 1) as i:
                x_transpose(i * 2 + 1, 1, i * 16 + 16)
                mlp1(i * 2, 0)
                mlp2(i * 2 - 2, 0)
                act_transpose(i * 2 - 1, 1)
                x_transpose(i * 2 + 2, 0, i * 16 + 32)
                mlp1(i * 2 + 1, 1)
                mlp2(i * 2 - 1, 1)
                act_transpose(i * 2, 0)
            x_transpose(MT - 1, 1, 16 * (MT // 2))
            mlp1(MT - 2, 0)
            mlp2(MT - 4, 0)
            act_transpose(MT - 3, 1)
            mlp1(MT - 1, 1)
            mlp2(MT - 3, 1)
            act_transpose(MT - 2, 0)
            mlp2(MT - 2, 0)
            act_transpose(MT - 1, 1)
            mlp2(MT - 1, 1)

        @block.scalar
        def _(act):
            acts = [0]

            def act_job():
                acts[0] += 1
                act.wait_ge(act_ready, acts[0])
                return bank(2 + (acts[0] - 1) % 2)

            act.wait_ge(small_in, 16 * 10)

            def y_copy(i, b):
                g, o = ((i % 2) * 4 + i // 2, (i % 2) * 4 + 2 + i // 2) if i < 2 * LAYERS else (8, 9)
                src = act_job()
                nc.scalar.activation(yT[:, b * NPIX:(b + 1) * NPIX], src[:, 0:NPIX], ACT.Identity,
                                     bias=cols_sb[:, o:o + 1], scale=cols_sb[:, g:g + 1]).then_inc(act_taken, 1)

            for l in range(LAYERS):
                for b in range(NB):
                    y_copy(2 * l, b)
                    for hp in range(2):
                        job = 2 * NB * l + 2 * b + hp
                        act.wait_ge(kmax_ready, job + 1)
                        for s in range(2):
                            h = 2 * hp + s
                            last = nc.scalar.activation(kT[:, h, b * NPIX:(b + 1) * NPIX],
                                                        bank(4 + job % 2)[:, s * NPIX:(s + 1) * NPIX], ACT.Exp,
                                                        bias=knmax[:, h, b:b + 1], accum_out=ksum[:, h, b:b + 1])
                        last.then_inc(kt_taken, 1)
                    for t in (2 * b, 2 * b + 1):
                        src = act_job()
                        nc.scalar.activation(v_tok[:, t, :], src, ACT.Identity).then_inc(act_taken, 1)
                        act.wait_ge(acc_taken, NT_IMG + l * (3 * NT_IMG + NB) + t + 1)
                        nc.scalar.activation(q_tok[:, t, :], q_tok[:, t, :], ACT.Exp).then_inc(qexp_ready, 1)
                for t in range(NT_IMG):
                    act.wait_ge(trk_ready, NT_IMG * l + t + 1)
                    nc.scalar.activation(k_tok[:, t, :], bank(7), ACT.Identity).then_inc(trk_taken, 1)
                for b in range(NB):
                    y_copy(2 * l + 1, b)
                    for hp in range(2):
                        src = act_job()
                        for s in range(2):
                            h = 2 * hp + s
                            last = nc.scalar.activation(mlp_hid[:, h, b * NPIX:(b + 1) * NPIX], src[:, s * NPIX:(s + 1) * NPIX],
                                                        ACT.Gelu, bias=cols_sb[:, 10 + 4 * l + h:11 + 4 * l + h])
                        last.then_inc(act_taken, 1)
            for b in range(NB):
                y_copy(2 * LAYERS, b)
            for t in range(NT):
                src = act_job()
                nc.scalar.activation(hnT[t % 2][:, 0:P], src[:, 0:P], ACT.Identity)
                nc.scalar.activation(hnT[t % 2][0:CB, P:2 * P], src[0:CB, P:2 * P], ACT.Identity).then_inc(act_taken, 1)

            SETS = [ps[:, 0:QS], ps[:, QS:2 * QS]]

            def act_head(n):
                for kb in range(KEYB):
                    act.wait_ge(scores_ready, n * KEYB + (kb + 1))
                    if not isinstance(n, int) or n * KEYB + kb >= 3:
                        act.wait_ge(probs_used, n * KEYB + kb - 2)
                    nc.scalar.activation(probs[kb % 3], SETS[kb % 2], ACT.Exp, scale=0.5).then_inc(probs_ready, 1)

            act_head(0)
            with act.Fori(1, NT) as i:
                act_head(i)

            act.wait_ge(combT_psum, 1)
            nc.scalar.activation(combT, ps[0:E, 0:NT * P], ACT.Identity).then_inc(combT_ready, 1)
            act.wait_ge(cnt_ready, 1)
            for e in range(SP_PADS, E):
                pad_bucket(act, e)
            act.wait_ge(plan_ready, 1)

            def x_copy(j, r):
                ex = act.value_load(ej_i[0:1, bass.ds(j, 1)], min_val=0, max_val=E - 1)
                act.wait_ge(x_read, j + 1)
                o = bank(7 * r)
                nc.scalar.activation(xtT[r][:, 0:P], o[:, 0:P], ACT.Identity)
                nc.scalar.activation(xtT[r][0:CB, P:2 * P], o[0:CB, P:2 * P], ACT.Identity).then_inc(xT_ready, 1)
                nc.scalar.activation(w_all[:, bass.ds(j, 1)], xt[r][:, bass.ds(ex + COMB, 1)], ACT.Identity)
                nc.scalar.activation(tok_all[:, bass.ds(j, 1)], xt[r][:, TOKEN:RW].bitcast(u32),
                                     ACT.Identity).then_inc(x_copied, 1)

            def sigmoid(j, r):
                act.wait_ge(glu_ready, j + 1)
                nc.scalar.activation(sig[r], glu[r], ACT.Sigmoid, scale=1.702).then_inc(sig_ready, 1)

            def y_tile(j, r, wait=True):
                act.wait_ge(y_psum, j + 1)
                if wait:
                    act.wait_ge(y_out, j * 16 - 16)
                act.wait_ge(x_copied, j + 1)
                nc.scalar.activation(yt[r], bank(6)[:, 0:C], ACT.Identity, scale=w_all[:, bass.ds(j, 1)]).then_inc(y_sb, 1)
                nc.scalar.activation(tok_idx[r], tok_all[:, bass.ds(j, 1)], ACT.Identity).then_inc(y_ready2, 1)

            act.wait_ge(bias_added, NT // 2)
            act.dma_start(out[0:DUMP, :].rearrange("(t p) c -> p t c", p=P), h_res[:]).then_inc(out_init, 16)
            x_copy(0, 0)
            x_copy(1, 1)
            sigmoid(0, 0)
            x_copy(2, 0)
            sigmoid(1, 1)
            x_copy(3, 1)
            sigmoid(2, 0)
            y_tile(0, 0, False)
            x_copy(4, 0)
            sigmoid(3, 1)
            y_tile(1, 1, False)
            with act.Fori(2, MT // 2 - 1) as i:
                x_copy(i * 2 + 1, 1)
                sigmoid(i * 2, 0)
                y_tile(i * 2 - 2, 0)
                x_copy(i * 2 + 2, 0)
                sigmoid(i * 2 + 1, 1)
                y_tile(i * 2 - 1, 1)
            x_copy(MT - 1, 1)
            sigmoid(MT - 2, 0)
            y_tile(MT - 4, 0)
            sigmoid(MT - 1, 1)
            y_tile(MT - 3, 1)
            y_tile(MT - 2, 0)
            y_tile(MT - 1, 1)

        @block.vector
        def _(dve):
            step = Chain(dve, dve_step)
            acc, lns = [0], [0]

            def acc_job():
                acc[0] += 1
                dve.wait_ge(acc_ready, acc[0])
                return bank((acc[0] - 1) % 2)

            def layer_norm(srcs, dsts):
                n = len(srcs)
                for s, x in enumerate(srcs):
                    step(nc.vector.bn_stats(stat[:, s, :], x))
                for s in range(n):
                    last = nc.vector.bn_aggr(mv[:, s, :], stat[:, s, :])
                last.then_inc(mv_ready, 1)
                lns[0] += 1
                dve.wait_ge(rstd_ready, lns[0])
                dve.wait_ge(mv_ready, lns[0])
                for s, (x, y) in enumerate(zip(srcs, dsts)):
                    last = nc.vector.tensor_scalar(y, x, mv[:, s, 0:1], rstd[:, s:s + 1], ALU.subtract, ALU.mult)
                last.then_inc(y_ready, 1)

            def image_norm(b):
                layer_norm([x_res[:, 2 * b + s, :] for s in range(2)], [x_nrm[:, 2 * b + s, :] for s in range(2)])

            for t in range(NT_IMG):
                src = acc_job()
                nc.vector.tensor_copy(x_res[:, t, :], src[:, 0:D]).then_inc(acc_taken, 1)
                dve.wait_ge(acc_taken, acc[0])
                if t % 2:
                    image_norm(t // 2)

            def residual(t):
                src = acc_job()
                nc.vector.tensor_tensor(x_res[:, t, :], src[:, 0:D], x_res[:, t, :], ALU.add).then_inc(acc_taken, 1)
                dve.wait_ge(acc_taken, acc[0])

            for l in range(LAYERS):
                def q_finish(t):
                    dve.wait_ge(qexp_ready, NT_IMG * l + t + 1)
                    step(nc.vector.reduce_sum(qsum[:, t, :], q_tok[:, t, :].rearrange("p (h d) -> p h d", h=8), AX.X))
                    nc.vector.reciprocal(qrec[:, t, :], qsum[:, t, :]).then_inc(qrec_ready, 1)

                for b in range(NB):
                    for hp in range(2):
                        job = 2 * NB * l + 2 * b + hp
                        dve.wait_ge(kt_ready, job + 1)
                        nc.vector.tensor_reduce(knmax[:, 2 * hp:2 * hp + 2, b],
                                                bank(4 + job % 2).rearrange("p (h n) -> p h n", h=2), AX.X, ALU.max,
                                                negate=True).then_inc(kmax_ready, 1)
                    for t in (2 * b, 2 * b + 1):
                        src = acc_job().rearrange("p (h d) -> p h d", h=8)
                        step(nc.vector.reduce_max(qmax[:, t, :], src, AX.X))
                        nc.vector.tensor_tensor(q_tok[:, t, :].rearrange("p (h d) -> p h d", h=8), src,
                                                qmax[:, t, :].unsqueeze(2).broadcast_to([P, 8, HD]),
                                                ALU.subtract).then_inc(acc_taken, 1)
                        if t:
                            q_finish(t - 1)
                q_finish(NT_IMG - 1)
                for b in range(NB):
                    for t in (2 * b, 2 * b + 1):
                        dve.wait_ge(trq_ready, NT_IMG * l + t + 1)
                        nc.vector.tensor_copy(qT[:, :, t * P:(t + 1) * P],
                                              bank(6).rearrange("p (h n) -> p h n", h=NPAIR)).then_inc(trq_taken, 1)
                    src = acc_job().rearrange("p (h n) -> p h n", h=NPAIR)
                    nc.vector.tensor_copy(ctx_bd[0:HD, b, :, 0:HD], src[0:HD, :, 0:HD])
                    nc.vector.tensor_copy(ctx_bd[HD:P, b, :, HD:P], src[HD:P, :, HD:P]).then_inc(acc_taken, 1)
                dve.wait_ge(kt_taken, 2 * NB * (l + 1))
                step(nc.vector.reciprocal(krec, ksum))
                step(nc.vector.tensor_scalar(krec8, krec, HD ** -0.5, None, ALU.mult))

                def ctx_w_copy(b):
                    dve.wait_ge(ctxw_ready, NB * l + b + 1)
                    nc.vector.tensor_tensor(ctx_w[:, b, :, :], bank(7).rearrange("p (h n) -> p h n", h=NPAIR),
                                            krec8[:, :, b:b + 1].broadcast_to([P, NPAIR, D]),
                                            ALU.mult).then_inc(ctxw_taken, 1)

                ctx_w_copy(0)
                for b in range(NB):
                    if b + 1 < NB:
                        ctx_w_copy(b + 1)
                    residual(2 * b)
                    residual(2 * b + 1)
                    image_norm(b)
                for b in range(NB):
                    residual(2 * b)
                    residual(2 * b + 1)
                    image_norm(b)

            for b in range(NB):
                for s in range(2):
                    src = acc_job()
                    nc.vector.tensor_copy(h_res[:, 3 * b + s, :], src[:, 0:C]).then_inc(acc_taken, 1)
            dve.wait_ge(acc_taken, acc[0])
            dve.wait_ge(small_in, 16 * 10)

            def qv_copy(t):
                src = acc_job()
                nc.vector.tensor_copy(qv[:, t, :], src[:, 0:2 * C]).then_inc(acc_taken, 1)

            for t in range(NT):
                layer_norm([h_res[:, t, :]], [h_nrm[t % 2]])
                if t:
                    qv_copy(t - 1)
            qv_copy(NT - 1)
            dve.wait_ge(acc_taken, acc[0])

            b7 = bank(7)
            b7h = bank(7).bitcast(f16)

            def heads(ap):
                return ap.rearrange("p (h d) -> p h d", h=NH)

            def per_head(ap):
                return ap.unsqueeze(2).broadcast_to([P, NH, DH])

            def prep_squares(n):
                qh = qv[:, bass.ds(n, 1), 0:C].rearrange("p a c -> p (a c)")
                step(nc.vector.tensor_tensor(sq[:], qh, qh, ALU.mult))
                nc.vector.reduce_sum(ss[:], heads(sq[:]), AX.X).then_inc(ss_ready, 1)

            def prep(n):
                qh = qv[:, bass.ds(n, 1), 0:C].rearrange("p a c -> p (a c)")
                dve.wait_ge(nrm_ready, n + 1)
                step(nc.vector.tensor_scalar(nrmc[:], nrm[:], 1e-12, None, ALU.max))
                step(nc.vector.reciprocal(rn[:], nrmc[:]))
                step(nc.vector.tensor_tensor(heads(qn[:]), heads(qh), per_head(rn[:]), ALU.mult))
                nc.vector.tensor_copy(key_tok[:, :, 0:16], heads(qn[:]))
                step(nc.vector.tensor_tensor(sq[:], qn[:], qn[:], ALU.mult))
                nc.vector.tensor_tensor(key_tok[:, :, 32:48], heads(qn[:]), key_tok[:, :, 0:16], ALU.subtract)
                step(nc.vector.reduce_sum(aa[:], heads(sq[:]), AX.X))
                nc.vector.tensor_copy(key_tok[:, :, 16:32], key_tok[:, :, 0:16])
                nc.vector.tensor_copy(key_tok[:, :, 48:64], key_tok[:, :, 32:48])
                step(nc.vector.tensor_copy(key_tok[:, :, 64:65], aa[:].unsqueeze(2)))
                nc.vector.tensor_copy(qry_tok[:, :, 0:16], key_tok[:, :, 0:16])
                nc.vector.tensor_copy(qry_tok[:, :, 32:48], key_tok[:, :, 0:16])
                nc.vector.tensor_copy(qry_tok[:, :, 16:32], key_tok[:, :, 32:48])
                nc.vector.tensor_copy(qry_tok[:, :, 48:64], key_tok[:, :, 32:48])
                step(nc.vector.tensor_tensor(key_tok[:, :, 65:66], aa[:].unsqueeze(2), key_tok[:, :, 64:65], ALU.subtract))
                nc.vector.tensor_copy(qry_tok[:, :, 66:68], key_tok[:, :, 64:66]).then_inc(stack_ready, 1)

            def stack_copy(g, par, job):
                dve.wait_ge(tr_ready, job + 1)
                src = b7h[0:STK, :].rearrange("p (s n) -> p s n", s=8)
                kv = keysT[par].rearrange("p (t h) -> p h t", h=NH)
                qv_ = qrysT[par].rearrange("p (h t) -> p h t", h=NH)
                lo, hi = 8 * g, 8 * g + 8
                nk = max(0, min(hi, NH) - lo)
                if nk and nk < 8:
                    nc.vector.tensor_copy(kv[:, lo:lo + nk, :], src[:, 0:nk, :])
                if nk == 8:
                    nc.vector.tensor_copy(kv[:, lo:hi, :], src).then_inc(tr_taken, 1)
                else:
                    nc.vector.tensor_copy(qv_[:, lo + nk - NH:hi - NH, :], src[:, nk:8, :]).then_inc(tr_taken, 1)

            def sums_copy(r):
                dve.wait_ge(probs_used, r * KEYB + KEYB)
                nc.vector.tensor_copy(o_acc[:], bank(6)[:, 0:QW]).then_inc(oacc_ready, 1)

            def output(r, job):
                dve.wait_ge(tr_ready, job + 1)
                src = b7[:, 0:QW].rearrange("p (c g d) -> p c g d", c=3, g=QG)
                step(nc.vector.reciprocal(o_rec[:].unsqueeze(3), src[:, :, :, 16:17]))
                dst = o_nrm[:].rearrange("p (g c d) -> p c g d", g=QG, c=3)
                nc.vector.tensor_tensor(dst, src[:, :, :, 0:DH], o_rec[:].unsqueeze(3).broadcast_to([P, 3, QG, DH]),
                                        ALU.mult).then_inc(onrm_ready, 1)
                nc.vector.tensor_copy(bank_mark[:], ones[:, 0:1]).then_inc(tr_taken, 1)

            def norm_stats(r, par):
                hr = h_res[:, bass.ds(r, 1), :].rearrange("p a c -> p (a c)")
                dve.wait_ge(h_ready, r + 1)
                step(nc.vector.bn_stats(stat[:, 0, :], hr))
                nc.vector.memset(bank_mark[:], 0.0)
                nc.vector.bn_aggr(mv[:, 0, :], stat[:, 0, :]).then_inc(lmv_ready, 1)

            def norm_square(r, par):
                hr = h_res[:, bass.ds(r, 1), :].rearrange("p a c -> p (a c)")
                dve.wait_ge(lrstd_ready, r + 1)
                dve.wait_ge(lmv_ready, r + 1)
                step(nc.vector.tensor_scalar(ln[:], hr, mv[:, 0, 0:1], rstd[:, 0:1], ALU.subtract, ALU.mult))
                step(nc.vector.tensor_tensor(sq[:], ln[:], ln[:], ALU.mult))
                nc.vector.reduce_sum(ms[:], sq[:], AX.X).then_inc(ms_ready, 1)

            def norm_rows(r, par):
                dve.wait_ge(rms_ready, r + 1)
                dve.wait_ge(rows_out, r * (16 * TOPK) + 32)
                nc.vector.scalar_tensor_tensor(t_row[:, 0:C], ln[:], rms[:], nscale_sb[:], ALU.mult,
                                               ALU.mult).then_inc(t_ready, 1)
                nc.vector.tensor_copy(t_row[:, TOKEN:RW].bitcast(u32), token_no[:, bass.ds(r, 1)])

            def tT_copy(job):
                dve.wait_ge(tr_ready, job + 1)
                nc.vector.tensor_copy(tT[:, 0:P], b7[:, 0:P])
                nc.vector.tensor_copy(tT[0:CB, P:2 * P], b7[0:CB, P:2 * P]).then_inc(tr_taken, 1)

            def choose(r, job):
                dve.wait_ge(tr_ready, job + 1)
                nc.vector.tensor_copy(logit[:], b7[:, 0:E]).then_inc(tr_taken, 1)
                held_wait(dve, tr_taken, job + 1)
                step(nc.vector.max(top8[:], logit[:]))
                nc.vector.tensor_scalar(gd[:], top8[:, 0:TOPK], top8[:, 0:1], None, ALU.subtract).then_inc(gd_ready, 1)
                step(nc.vector.max_index(top_i[:], top8[:], logit[:]))
                step(nc.vector.tensor_copy(top_f[:], top_i[:, 0:TOPK]))
                step(nc.vector.tensor_tensor(onehot[:], iota_e[:].unsqueeze(1).broadcast_to([P, TOPK, E]),
                                             top_f[:].unsqueeze(2).broadcast_to([P, TOPK, E]), ALU.is_equal))
                nc.vector.reduce_sum(mask[:], onehot[:].rearrange("p k e -> p e k"), AX.X).then_inc(mask_ready, 1)

            def place(r, par, job):
                dve.wait_ge(tr_ready, job + 1)
                nc.vector.tensor_tensor(slot_e[:], b7[:, 0:E], bucket0[:], ALU.add).then_inc(tr_taken, 1)
                dve.wait_ge(tr_taken, job + 1)
                step(nc.vector.tensor_tensor(slot_oh[:], onehot[:], slot_e[:].unsqueeze(1).broadcast_to([P, TOPK, E]), ALU.mult))
                step(nc.vector.tensor_tensor(seen[:], seen[:], mask[:], ALU.add))
                step(nc.vector.reduce_sum(slot_f[:], slot_oh[:], AX.X))
                nc.vector.tensor_copy(slot_u[:], slot_f[:]).then_inc(slots_ready, 1)

            def weigh(r):
                comb = comb_all[:, bass.ds(r, 1), :].rearrange("p a e -> p (a e)")
                dve.wait_ge(wexp_ready, r + 1)
                nc.vector.tensor_tensor(slot_oh[:], onehot[:], wexp[:].unsqueeze(2).broadcast_to([P, TOPK, E]), ALU.mult)
                step(nc.vector.reduce_sum(wsum[:], wexp[:], AX.X))
                nc.vector.reduce_sum(slot_e[:], slot_oh[:].rearrange("p k e -> p e k"), AX.X)
                step(nc.vector.reciprocal(wrec[:], wsum[:]))
                nc.vector.tensor_scalar(t_row[:, COMB:TOKEN], slot_e[:], wrec[:], None, ALU.mult)
                step(nc.vector.tensor_scalar(comb, slot_e[:], wrec[:], None, ALU.mult))

            def dve_head(n, r, par, first, last, prep2=True):
                base = 3 if first else tr_base(r)
                if not first:
                    sums_copy(r)
                    output(r, base)
                if first:
                    for g in range(3):
                        stack_copy(g, 1 - par, base + g)
                elif not last:
                    stack_copy(0, 1 - par, base + 1)
                    norm_stats(r, 1 - par)
                    stack_copy(1, 1 - par, base + 2)
                    norm_square(r, 1 - par)
                    stack_copy(2, 1 - par, base + 3)
                    norm_rows(r, 1 - par)
                    if prep2:
                        prep_squares(n + 2)
                    tT_copy(base + 4)
                    choose(r, base + 5)
                    weigh(r)
                    place(r, 1 - par, base + 6)
                else:
                    norm_stats(r, 1 - par)
                    norm_square(r, 1 - par)
                    norm_rows(r, 1 - par)
                    tT_copy(base + 1)
                    choose(r, base + 2)
                    weigh(r)
                    place(r, 1 - par, base + 3)
                if first:
                    prep_squares(n + 2)
                if not last and prep2:
                    prep(n + 2)

            dve.wait_ge(consts_ready, NCONST + 2)
            prep_squares(0)
            prep(0)
            for g in range(3):
                stack_copy(g, 0, g)
            prep_squares(1)
            prep(1)
            dve_head(0, None, 0, True, False)
            before = step.n
            with dve.Fori(0, 4) as i:
                for p in (0, 1):
                    step.rebase(i * (2 * DVE_STEPS) + (before + DVE_STEPS * p))
                    dve_head(i * 2 + (1 + p), i * 2 + p, 1 - p, False, False)
                    assert step.n == DVE_STEPS, step.n
            step.rebase(before + 8 * DVE_STEPS)
            dve_head(NT - 3, NT - 4, 1, False, False)
            dve_head(NT - 2, NT - 3, 0, False, False, prep2=False)
            dve_head(NT - 1, NT - 2, 1, False, True)
            base = tr_base(NT - 2) + 4
            sums_copy(NT - 1)
            output(NT - 1, base)
            norm_stats(NT - 1, 1)
            norm_square(NT - 1, 1)
            norm_rows(NT - 1, 1)
            tT_copy(base + 1)
            choose(NT - 1, base + 2)
            weigh(NT - 1)
            place(NT - 1, 1, base + 3)
            dve.wait_ge(slots_ready, NT)
            dve.wait_ge(tr_ready, base + 5)
            nc.vector.tensor_copy(cnt, b7[:, 0:E]).then_inc(tr_taken, 1)
            dve.wait_ge(tr_taken, base + 5)
            step(nc.vector.tensor_tensor(slot_e[:], cnt, bucket0[:], ALU.add))
            nc.vector.tensor_copy(pad0_i, slot_e[0:1, :]).then_inc(cnt_ready, 1)
            dve.wait_ge(plan_consts, 2)
            step(nc.vector.tensor_tensor(over, cnt.unsqueeze(2).broadcast_to([P, E, NT]),
                                         edges.unsqueeze(1).broadcast_to([P, E, NT]), ALU.is_gt))
            step(nc.vector.reduce_sum(tiles_e, over, AX.X))
            step(nc.vector.tensor_tensor_scan(ends, ones[:, 0:E], tiles_e, 0.0, ALU.mult, ALU.add))
            step(nc.vector.tensor_tensor(done_e, ends[0:1, :].unsqueeze(1).broadcast_to([1, MT, E]),
                                         iota_j.unsqueeze(2).broadcast_to([1, MT, E]), ALU.is_le))
            step(nc.vector.reduce_sum(ej, done_e, AX.X))
            step(nc.vector.tensor_tensor(done_t, done_e, tiles_e[0:1, :].unsqueeze(1).broadcast_to([1, MT, E]), ALU.mult))
            step(nc.vector.reduce_sum(sj, done_t, AX.X))
            step(nc.vector.tensor_tensor(tmpj, iota_j, sj, ALU.subtract))
            step(nc.vector.tensor_scalar(rowj, ej, float(BUCKET), None, ALU.mult))
            step(nc.vector.scalar_tensor_tensor(row_i, tmpj, float(P), rowj, ALU.mult, ALU.add))
            nc.vector.tensor_scalar(ej_i, ej, float(E - 1), None, ALU.min).then_inc(plan_ready, 1)
            dve.wait_ge(base_ready, NT)
            for t in range(0, NT, 2):
                dve.wait_ge(bias_psum, t + 2)
                pair = h_res[:, t:t + 2, :].rearrange("p t c -> p (t c)")
                nc.vector.tensor_tensor(pair, pair, bank(t // 2)[:, 0:2 * C], ALU.add).then_inc(bias_added, 1)

            for r in range(2):
                nc.vector.memset(xtT[r][CB:CB + 1, P:2 * P], 1.0).then_inc(xT_ones, 1)

            def clip(j, r):
                dve.wait_ge(h_done, j * 2 + 1)
                if not isinstance(j, int) or j >= 2:
                    dve.wait_ge(actv_ready, j - 1)
                nc.vector.tensor_scalar(glu[r], bank(1 + r)[:, 0:FF], 7.0, None, ALU.min).then_inc(glu_ready, 1)
                dve.wait_ge(h_done, j * 2 + 2)
                nc.vector.tensor_scalar(lin[r], bank(3 + r)[:, 0:FF], -7.0, 7.0, ALU.max, ALU.min).then_inc(lin_ready, 1)
                dve.wait_ge(lin_ready, j + 1)
                nc.vector.scalar_tensor_tensor(prod[r], lin[r], 1.0, glu[r], ALU.add, ALU.mult).then_inc(prod_ready, 1)

            def actT_copy(j, r):
                dve.wait_ge(aT_psum, j + 1)
                nc.vector.tensor_copy(actT[r], bank(5)[:, 0:FF]).then_inc(aT_ready, 1)

            clip(0, 0)
            clip(1, 1)
            actT_copy(0, 0)
            clip(2, 0)
            actT_copy(1, 1)
            clip(3, 1)
            actT_copy(2, 0)
            with dve.Fori(2, MT // 2) as i:
                clip(i * 2, 0)
                actT_copy(i * 2 - 1, 1)
                clip(i * 2 + 1, 1)
                actT_copy(i * 2, 0)
            actT_copy(MT - 1, 1)


def kernel(**inputs):
    import numpy as np
    import concourse.bacc as bacc
    from concourse import mybir
    from concourse.bass_utils import run_bass_kernel_spmd as run

    a = {k.replace("L0_", ""): np.asarray(v) for k, v in inputs.items()}
    cc = np.ascontiguousarray

    def fold(w, k):
        return cc(np.moveaxis(w.reshape((k, 128) + w.shape[1:]), 0, 1))

    x = a["x"].reshape(4, 32, 16, 8, 16, 8).transpose(0, 1, 3, 5, 2, 4)
    w1 = a["ffn_mlp1_w"].reshape(16, 384, 2, 192).transpose(3, 0, 2, 1).reshape(192, 16 * 768)
    b1 = a["ffn_mlp1_b"].reshape(16, 384, 2).transpose(0, 2, 1).reshape(1, 16 * 768)
    wqv = np.concatenate([a["attn_Wq"].T, a["attn_Wv"].T], 1)
    bqv = np.concatenate([a["attn_bq"], a["attn_bv"]])[None]
    arrays = {
        "patches": cc(x.reshape(4, 128, 16, 256)),
        "conv_w": cc(a["tok_conv_w"].reshape(128, 2048).T.reshape(128, 16, 128)),
        "cols": cc(np.concatenate([a["tok_ln1_g"], a["tok_ln1_b"], a["tok_ln2_g"], a["tok_ln2_b"],
                                   a["tok_lnf_g"][None], a["tok_lnf_b"][None],
                                   a["tok_ff1_b"].reshape(8, 128)], 0).T),
        "rows": cc(np.concatenate([a["tok_conv_b"], a["tok_out_b"].ravel(), a["tok_ff2_b"].ravel(),
                                   a["tok_head_b"]])[None]),
        "qkv_w": cc(a["tok_qkv_w"].transpose(1, 0, 2)),
        "out_w": cc(a["tok_out_w"].reshape(2, 4, 128, 128).transpose(2, 0, 1, 3)),
        "ff1_w": cc(a["tok_ff1_w"].transpose(1, 0, 2)),
        "ff2_w": cc(a["tok_ff2_w"].reshape(2, 4, 128, 128).transpose(2, 0, 1, 3)),
        "head_w": cc(a["tok_head_w"]),
        "txt": cc(a["txt"]),
        "wqv_a": cc(wqv[0:128]),
        "wqv_b": cc(np.concatenate([wqv[128:], bqv], 0)),
        "gate_a": cc(a["ffn_gate_w"].T[0:128]),
        "gate_b": cc(np.concatenate([a["ffn_gate_w"].T[128:], a["ffn_gate_b"][None]], 0)),
        "nscale": cc(a["ffn_norm_scale"][None]),
        "w1_a": cc(w1[0:128]),
        "w1_b": cc(np.concatenate([w1[128:], b1], 0)),
        "w2": cc(fold(a["ffn_mlp2_w"].transpose(2, 0, 1), 3).transpose(0, 2, 1, 3).reshape(128, 16 * 3 * 192)),
        "b2": cc(a["ffn_mlp2_b"]),
    }
    nc = bacc.Bacc("TRN2", target_bir_lowering=False, num_devices=1)
    args = [nc.dram_tensor(n, v.shape, mybir.dt.from_np(v.dtype), kind="ExternalInput").ap() for n, v in arrays.items()]
    f32 = mybir.dt.float32
    out = nc.dram_tensor("out", (DUMP + P, C), f32, kind="ExternalOutput").ap()
    xs = nc.dram_tensor("expert_in", (SPARE + NSPARE * P, RW), f32, kind="Internal").ap()
    fusion_kernel(nc, *args, out, xs)
    r = run(nc, [arrays], core_ids=[0])
    return r.results[0]["out"][0:DUMP].reshape(4, 384, 192)
```

```python
import concourse.bass as bass
from concourse import mybir
from contextlib import ExitStack
import math

P = 128
NB, NPIX, D, KT = 4, 256, 128, 16
NT_IMG = NB * NPIX // P
LAYERS, INNER, HD, MLP = 2, 512, 64, 512
NPAIR = INNER // P
C, NH, DH = 192, 12, 16
NT = 12
KEYB = 12
QS = 1536
CB = C - P
QG = 4
QW = QS // QG
STK = 52
STKW = 68
ROW2 = 64
E, TOPK, FF = 16, 4, 384
BUCKET = QS + P
BIAS_BANK = (3, 4, 5, 0, 1, 2)
SPARE = E * BUCKET
MT = (TOPK * QS - E) // P + E
NSPARE = MT - TOPK * NT
COMB = C
TOKEN = C + E
RW = C + E + 1
DUMP = NT * P

LANE = [("conv", 0)]
for _l in range(LAYERS):
    LANE += [(_s, _l) for _s in ("T", "A", "Q", "B", "K", "W", "C", "T", "D1", "D2")]
LANE += [("T", LAYERS), ("H", 0), ("PT", 0), ("PP", 0)]
FIRST_LANE = LANE + [("S0", 0), ("S1", 0), ("S2", 0)]
TEXT_LANE = [("N", 0), ("PT", 0), ("PP", 0)]


def schedule():
    lanes = [(len(LANE) - 5 + i, TEXT_LANE, None, (6 * i + 2, 6 * i + 5)) for i in range(2)]
    lanes += [(b, LANE if b else FIRST_LANE, b, (3 * b, 3 * b + 1)) for b in range(NB)]
    return [(*lane[slot - start], b, tiles) for slot in range(len(LANE) + NB - 1)
            for start, lane, b, tiles in lanes if 0 <= slot - start < len(lane)]


NORMS = ("conv", "C", "D2", "H", "N")
ACC_JOBS = {"conv": 2, "A": 2, "K": 1, "C": 2, "D2": 2, "H": 2, "PP": 2}
ACT_JOBS = {"T": 1, "A": 2, "D1": 2, "PT": 1}
TOK_ACC = sum(ACC_JOBS.get(_s, 0) for _s, *_ in schedule())


def fusion_kernel(nc, patches, conv_w, cols, rows, qkv_w, out_w, ff1_w, ff2_w, head_w, txt,
                  wqv_a, wqv_b, gate_a, gate_b, nscale, w1_a, w1_b, w2, b2, out, xs):
    f32, f16, i32, u32 = mybir.dt.float32, mybir.dt.float16, mybir.dt.int32, mybir.dt.uint32
    ALU, ACT, AX = mybir.AluOpType, mybir.ActivationFunctionType, mybir.AxisListType
    ctx = ExitStack()
    with ctx:
        def sb(name, shape, dt=f32):
            return ctx.enter_context(nc.sbuf_tensor(name, shape, dt))

        def sem(name):
            return ctx.enter_context(nc.semaphore(name))

        ps = ctx.enter_context(nc.psum_tensor("ps", [P, 8 * 512], f32))

        def bank(i):
            return ps[:, i * 512:(i + 1) * 512]

        big = sb("big", [P, E * 2 * 768 + E * 3 * C])
        at = [0]

        def carve(n):
            at[0] += n
            return big[:, at[0] - n:at[0]]

        patch_sb = [carve(KT * NPIX).rearrange("p (k n) -> p k n", k=KT) for _ in range(NB)]
        convw_sb = carve(KT * D).rearrange("p (k d) -> p k d", k=KT)
        qkvw_sb = carve(LAYERS * 3 * INNER).rearrange("p (l n) -> p l n", l=LAYERS)
        outw_sb = carve(LAYERS * NPAIR * D).rearrange("p (l k d) -> p l k d", l=LAYERS, k=NPAIR)
        ff1w_sb = carve(LAYERS * MLP).rearrange("p (l n) -> p l n", l=LAYERS)
        ff2w_sb = carve(LAYERS * 4 * D).rearrange("p (l k d) -> p l k d", l=LAYERS, k=4)
        k_tok = carve(NT_IMG * INNER).rearrange("p (t n) -> p t n", t=NT_IMG)
        mlp_hid = carve(4 * NT_IMG * P).rearrange("p (h n) -> p h n", h=4)
        yT = carve(NT_IMG * P)
        image_sb = [big[:, b * KT * NPIX:(b + 1) * KT * NPIX].rearrange("p (i n) -> p i n", i=4) for b in range(NB)]
        q_tok, v_tok = [[image_sb[t // 2][:, i, (t % 2) * INNER:(t % 2 + 1) * INNER] for t in range(NT_IMG)]
                        for i in range(2)]
        kT, qT = [[image_sb[b][:, i, :].rearrange("p (h n) -> p h n", h=NPAIR) for b in range(NB)] for i in (2, 3)]
        w1a_sb = big[:, 0:E * 768]
        w1b_sb = big[:, E * 768:2 * E * 768]
        w2_sb = big[:, 2 * E * 768:]

        mid = sb("mid", [P, 8448 + NH * STKW])
        probs = [mid[:, i * QS:(i + 1) * QS] for i in range(3)]
        ab = mid[:, 3 * QS:5 * QS].bitcast(f16)
        keysT, keysT2 = [[ab[p0:p0 + STK, (2 * i) * QS:(2 * i + 1) * QS] for i in range(2)] for p0 in (0, ROW2)]
        qrysT, qrysT2 = [[ab[p0:p0 + STK, (2 * i + 1) * QS:(2 * i + 2) * QS] for i in range(2)] for p0 in (0, ROW2)]
        vhead = [mid[:, 5 * QS + i * KEYB * 32:5 * QS + (i + 1) * KEYB * 32]
                 .rearrange("p (k d) -> p k d", k=KEYB) for i in range(2)]
        stk = mid[:, 5 * QS + 2 * KEYB * 32:5 * QS + 2 * KEYB * 32 + NH * STKW].bitcast(f16)
        key_tok = stk[:, 0:NH * STKW].rearrange("p (h c) -> p h c", h=NH)
        qry_tok = stk[:, NH * STKW:2 * NH * STKW].rearrange("p (h c) -> p h c", h=NH)
        x_res = mid[:, 0:1024].rearrange("p (t d) -> p t d", t=NT_IMG)
        x_nrm = mid[:, 1024:2048].rearrange("p (t d) -> p t d", t=NT_IMG)
        ctx_bd = mid[:, 2048:4096].rearrange("p (b k d) -> p b k d", b=NB, k=NPAIR)
        ctx_w = mid[:, 4096:6144].rearrange("p (b k d) -> p b k d", b=NB, k=NPAIR)
        wqva_sb = mid[:, 6144:6528]
        wqvb_sb = mid[0:CB + 1, 6528:6912]
        hnT_both = mid[:, 6912:7424].rearrange("p (s n) -> p s n", s=2)
        hnT = [hnT_both[:, s, :] for s in range(2)]
        h_nrm = [mid[:, 7424 + 192 * i:7616 + 192 * i] for i in range(2)]
        rows_sb = mid[:, 7808:7808 + 5 * D]
        done_e, done_t = [mid[:, E * i:E * (i + 1)] for i in range(2)]
        over = mid[:, 128:128 + E * NT].rearrange("p (e t) -> p e t", e=E)
        ej, sj, rowj, tmpj = [mid[:, 64 + i:65 + i] for i in range(4)]
        plan_cols = mid[:, 72:74]
        combT = mid[0:E, 2560:2560 + NT * P]
        b2_sb = mid[0:E, 8560:8560 + C]
        edges = mid[:, 8512:8512 + NT]
        xt = [mid[:, 6272 + i * RW:6272 + (i + 1) * RW] for i in range(2)]
        w_all = mid[:, 6720:6720 + MT]
        tok_all = mid[:, 6784:6784 + MT]
        tok_idx = [mid[:, 6848 + i:6849 + i].bitcast(u32) for i in range(2)]
        xtT = [mid[:, 384 + i * 256:640 + i * 256] for i in range(2)]
        glu = [mid[:, 896 + i * FF:1280 + i * FF] for i in range(2)]
        lin = [mid[:, 1664 + i * FF:2048 + i * FF] for i in range(2)]
        sig = [mid[:, 2432 + i * FF:2816 + i * FF] for i in range(2)]
        prod = [mid[:, 3200 + i * FF:3584 + i * FF] for i in range(2)]
        actv = [mid[:, 3968 + i * FF:4352 + i * FF] for i in range(2)]
        actT = [mid[:, 4736 + i * FF:5120 + i * FF] for i in range(2)]
        yt = [mid[:, 5504 + i * C:5696 + i * C] for i in range(2)]

        h_res = sb("h_res", [P, NT, C])
        qv = sb("qv", [P, NT, 2 * C])
        cols_sb = sb("cols_sb", [P, 18])
        ident = sb("ident", [P, P])
        ident16 = sb("ident16", [P, P], f16)
        ones = sb("ones", [P, P])
        tri = sb("tri", [P, P])
        zero_rows = sb("zero_rows", [P, RW])
        gatea_sb = sb("gatea_sb", [P, E])
        gateb_sb = sb("gateb_sb", [CB + 1, E])
        nscale_sb = sb("nscale_sb", [P, C])
        iota_e = sb("iota_e", [P, E])
        token_no = sb("token_no", [P, NT])
        bucket0 = sb("bucket0", [P, E])
        euler = sb("euler", [P, TOPK])
        phalf = sb("phalf", [P, NT])
        nhalf = sb("nhalf", [P, NT])
        stat = sb("stat", [P, 2, 6])
        mv = sb("mv", [P, 2, 2])
        vps = sb("vps", [P, 2])
        rstd = sb("rstd", [P, 2])
        sq = sb("sq", [P, C])
        qn = sb("qn", [P, C])
        cnt, tiles_e, ends = [qn[:, 16 * i:16 * i + 16] for i in range(3)]
        ss = sb("ss", [P, NH])
        nrm = sb("nrm", [P, NH])
        nrmc = sb("nrmc", [P, NH])
        rn = sb("rn", [P, NH])
        aa = sb("aa", [P, NH])
        o_acc = sb("o_acc", [P, QW])
        knmax, ksum, krec, krec8 = [o_acc[:, 16 * i:16 * i + 16].rearrange("p (h b) -> p h b", h=NPAIR) for i in range(4)]
        qmax, qsum, qrec = [o_acc[:, 64 * i:64 * i + 64].rearrange("p (t h) -> p t h", t=NT_IMG) for i in range(1, 4)]
        o_rec = sb("o_rec", [P, 3, QG])
        o_nrm = sb("o_nrm", [P, C])
        headw_sb = o_nrm[:]
        ej_i, row_i = [o_nrm[0:1, MT * i:MT * (i + 1)].bitcast(i32) for i in range(2)]
        pad0_i = mid[0:1, 8528:8528 + E].bitcast(i32)
        ln = sb("ln", [P, C])
        headb_sb = ln[:]
        ms = sb("ms", [P, 1])
        mse = sb("mse", [P, 1])
        rms = sb("rms", [P, 1])
        t_row = sb("t_row", [P, RW])
        slot_u = sb("slot_u", [P, TOPK], u32)
        bank_mark = sb("bank_mark", [P, 1])
        tT = sb("tT", [P, 2 * P])
        logit = sb("logit", [P, E])
        top_i = sb("top_i", [P, 8], u32)
        top_f = sb("top_f", [P, TOPK])
        onehot = sb("onehot", [P, TOPK, E])
        mask = sb("mask", [P, E])
        seen = sb("seen", [P, E])
        slot_e = sb("slot_e", [P, E])
        slot_oh = sb("slot_oh", [P, TOPK, E])
        comb_all = sb("comb_all", [P, NT, E])
        gd = sb("gd", [P, TOPK])
        slot_f = gd
        wexp = sb("wexp", [P, TOPK])
        wsum = sb("wsum", [P, 1])
        wrec = sb("wrec", [P, 1])
        top8 = sb("top8", [P, 8])
        convw_in, patch0_in = [[sem(f"{name}{q}") for q in range(4)] for name in ("convw_in", "patch0_in")]
        patch_in = [None] + [sem(f"patch_in{b}") for b in range(1, NB)]
        rows_in, tokw_in = sem("rows_in"), sem("tokw_in")
        small_in, cols_in, qkvw_in, headb_in = sem("small_in"), sem("cols_in"), sem("qkvw_in"), sem("headb_in")
        xbias_ready = sem("xbias_ready")
        consts_ready = sem("consts_ready")
        pool_step = sem("pool_step")
        dve_step = sem("dve_step")
        acc_ready, acc_taken = sem("acc_ready"), sem("acc_taken")
        act_ready, act_taken = sem("act_ready"), sem("act_taken")
        kt_ready, kt_taken = sem("kt_ready"), sem("kt_taken")
        kmax_ready = sem("kmax_ready")
        trq_ready, trq_taken = sem("trq_ready"), sem("trq_taken")
        trk_ready, trk_taken = sem("trk_ready"), sem("trk_taken")
        ctxw_ready, ctxw_taken = sem("ctxw_ready"), sem("ctxw_taken")
        mv_ready, rstd_ready = sem("mv_ready"), sem("rstd_ready")
        y_ready = sem("y_ready")
        qexp_ready, qrec_ready, qnorm_ready = sem("qexp_ready"), sem("qrec_ready"), sem("qnorm_ready")
        w_in = sem("w_in")
        scores_ready, probs_ready, probs_used = sem("scores_ready"), sem("probs_ready"), sem("probs_used")
        stack_ready, tr_ready, tr_taken = sem("stack_ready"), sem("tr_ready"), sem("tr_taken")
        vhead_ready = sem("vhead_ready")
        ss_ready, nrm_ready = sem("ss_ready"), sem("nrm_ready")
        oacc_ready = sem("oacc_ready")
        onrm_ready, h_ready = sem("onrm_ready"), sem("h_ready")
        lmv_ready, lrstd_ready = sem("lmv_ready"), sem("lrstd_ready")
        ms_ready, rms_ready = sem("ms_ready"), sem("rms_ready")
        t_ready, mask_ready, slots_ready, rows_out = (sem("t_ready"), sem("mask_ready"), sem("slots_ready"),
                                                      sem("rows_out"))
        base_ready = sem("base_ready")
        plan_cols_ready, plan_ready = sem("plan_cols_ready"), sem("plan_ready")
        cnt_ready = sem("cnt_ready")
        pads_out = sem("pads_out")
        x_in, x_read = [sem("x_in0"), sem("x_in1")], sem("x_read")
        b2_in, xT_ones, x_copied = sem("b2_in"), sem("xT_ones"), sem("x_copied")
        xT_ready = sem("xT_ready")
        h_done, glu_ready, lin_ready, sig_ready = sem("h_done"), sem("glu_ready"), sem("lin_ready"), sem("sig_ready")
        prod_ready, actv_ready = sem("prod_ready"), sem("actv_ready")
        aT_psum, aT_ready = sem("aT_psum"), sem("aT_ready")
        y_psum, y_sb = sem("y_psum"), sem("y_sb")
        y_ready2, y_out = sem("y_ready2"), sem("y_out")
        gd_ready, wexp_ready, token_ready = sem("gd_ready"), sem("wexp_ready"), sem("token_ready")
        combT_psum, combT_ready = sem("combT_psum"), sem("combT_ready")
        bias_psum, bias_added = sem("bias_psum"), sem("bias_added")
        out_init, plan_consts = sem("out_init"), sem("plan_consts")

        NCONST = 18
        TR7 = 7

        def tr_base(r):
            return r * TR7 + 6

        def held_wait(eng, s, value):
            if not isinstance(value, int):
                value = eng.snap(value)
                eng.wait_ge(consts_ready, NCONST)
            eng.wait_ge(s, value)

        class Chain:
            def __init__(self, eng, s):
                self.eng, self.sem, self.base, self.n = eng, s, 0, 0

            def __call__(self, ins, held=False):
                self.n += 1
                ins.then_inc(self.sem, 1)
                (held_wait if held else type(self.eng).wait_ge)(self.eng, self.sem, self.base + self.n)

            def rebase(self, base):
                self.base, self.n = base, 0

        DVE_STEPS = 22
        POOL_STEPS = 2

        SP_PADS, ACT_PADS = range(0, 10), range(10, E)

        def pad_bucket(eng, e):
            first = eng.value_load(pad0_i[0:1, e:e + 1], min_val=0, max_val=SPARE - 2 * P)
            eng.dma_start(xs[bass.ds(first, 2 * P), :].rearrange("(t p) c -> p t c", p=P),
                          zero_rows[:].unsqueeze(1).broadcast_to([P, 2, RW])).then_inc(pads_out, 16)

        block = ctx.enter_context(nc.Block())

        @block.sync
        def _(sp):
            for k in range(0, KT, KT // 4):
                ks = slice(k, k + KT // 4)
                sp.dma_start(convw_sb[:, ks, :], conv_w[:, ks, :]).then_inc(convw_in[k * 4 // KT], 16)
                sp.dma_start(patch_sb[0][:, ks, :], patches[0][:, ks, :]).then_inc(patch0_in[k * 4 // KT], 16)
            for dst, src, s in ((rows_sb, rows[:, 0:5 * D].broadcast_to([P, 5 * D]), rows_in), (cols_sb[:], cols, cols_in),
                                (patch_sb[1], patches[1], patch_in[1]), (qkvw_sb, qkv_w, qkvw_in),
                                (patch_sb[2], patches[2], patch_in[2]), (outw_sb, out_w, tokw_in),
                                (patch_sb[3], patches[3], patch_in[3]), (ff1w_sb, ff1_w, tokw_in),
                                (ff2w_sb, ff2_w, tokw_in), (headw_sb, head_w, tokw_in),
                                (headb_sb, rows[:, 5 * D:5 * D + C].broadcast_to([P, C]), headb_in)):
                sp.dma_start(dst, src).then_inc(s, 16)
            for dst, src in ((wqva_sb, wqv_a), (wqvb_sb, wqv_b), (gatea_sb[:], gate_a), (gateb_sb[:], gate_b),
                             (nscale_sb[:], nscale.broadcast_to([P, C]))):
                sp.dma_start(dst, src).then_inc(small_in, 16)
            for b in range(NB):
                sp.dma_start(h_res[:, 3 * b + 2, :], txt[b]).then_inc(small_in, 16)
            sp.wait_ge(acc_taken, TOK_ACC)
            for e in range(0, E, 4):
                sp.dma_start(w1a_sb[:, e * 768:(e + 4) * 768], w1_a[:, e * 768:(e + 4) * 768]).then_inc(w_in, 16)
                sp.dma_start(w1b_sb[0:CB + 1, e * 768:(e + 4) * 768], w1_b[:, e * 768:(e + 4) * 768]).then_inc(w_in, 16)
                sp.dma_start(w2_sb[:, e * 3 * C:(e + 4) * 3 * C], w2[:, e * 3 * C:(e + 4) * 3 * C]).then_inc(w_in, 16)
            sp.wait_ge(cnt_ready, 1)
            sp.dma_start(b2_sb, b2).then_inc(b2_in, 16)
            for e in SP_PADS:
                pad_bucket(sp, e)
            sp.wait_ge(rows_out, 16 * (TOPK * NT + 2))
            sp.wait_ge(plan_ready, 1)

            def load_rows(j, r, free=True):
                if free:
                    sp.wait_ge(x_read, j - 1)
                    sp.wait_ge(x_copied, j - 1)
                row = sp.value_load(row_i[0:1, bass.ds(j, 1)], min_val=0, max_val=SPARE + (NSPARE - 1) * P)
                sp.dma_start(xt[r], xs[bass.ds(row, P), :]).then_inc(x_in[r], 16)

            load_rows(0, 0, False)
            load_rows(1, 1, False)
            with sp.Fori(1, MT // 2) as i:
                for r in (0, 1):
                    load_rows(i * 2 + r, r)
            load_rows(MT - 1, 0)

        @block.gpsimd
        def _(pool):
            step = Chain(pool, pool_step)
            nc.gpsimd.memset(ident[:], 0.0).then_inc(consts_ready, 1)
            nc.gpsimd.memset(ident16[:], 0.0).then_inc(consts_ready, 1)
            nc.gpsimd.memset(ones[:], 1.0).then_inc(consts_ready, 1)
            pool.wait_ge(consts_ready, 3)
            nc.gpsimd.affine_select(out=ident[:], in_=ident[:], compare_op=ALU.not_equal, fill=1.0, base=0,
                                    pattern=[[-1, P]], channel_multiplier=1).then_inc(consts_ready, 1)
            nc.gpsimd.affine_select(out=ident16[:], in_=ident16[:], compare_op=ALU.not_equal, fill=1.0, base=0,
                                    pattern=[[-1, P]], channel_multiplier=1).then_inc(consts_ready, 1)
            nc.gpsimd.affine_select(out=tri[:], in_=ones[:], compare_op=ALU.is_gt, fill=0.0, base=0,
                                    pattern=[[1, P]], channel_multiplier=-1).then_inc(consts_ready, 1)
            nc.gpsimd.memset(zero_rows[:], 0.0).then_inc(consts_ready, 1)
            nc.gpsimd.memset(phalf[:], 0.5).then_inc(consts_ready, 1)
            nc.gpsimd.memset(nhalf[:], -0.5).then_inc(consts_ready, 1)
            nc.gpsimd.memset(mid[:, 2048:4096], 0.0).then_inc(consts_ready, 1)
            nc.gpsimd.memset(seen[:], 0.0).then_inc(consts_ready, 1)
            nc.gpsimd.memset(euler[:], math.e).then_inc(consts_ready, 1)
            for dst, pat, per_partition in ((iota_e, [[1, E]], 0), (bucket0, [[BUCKET, E]], 0), (token_no, [[P, NT]], 1)):
                nc.gpsimd.iota(dst[:], pattern=pat, base=0, channel_multiplier=per_partition,
                               allow_small_or_imprecise_dtypes=True).then_inc(consts_ready, 1)
            for i, dst in enumerate((hnT[0], hnT[1], tT)):
                pool.wait_ge(consts_ready, NCONST - 3 + i)
                nc.gpsimd.memset(dst[CB:CB + 1, P:2 * P], 1.0).then_inc(consts_ready, 1)
            pool.wait_ge(consts_ready, NCONST)
            step(nc.gpsimd.iota(zero_rows[:, TOKEN:RW].bitcast(u32), pattern=[[0, 1]], base=DUMP, channel_multiplier=1))
            pool.dma_start(xs[SPARE:SPARE + NSPARE * P, :].rearrange("(t p) c -> p t c", p=P),
                           zero_rows[:].unsqueeze(1).broadcast_to([P, NSPARE, RW])).then_inc(rows_out, 16)
            pool.dma_start(out[DUMP:DUMP + P, :], zero_rows[:, 0:C]).then_inc(rows_out, 16)

            t_norm, before_attention = {}, [True] * NB
            pool.wait_ge(rows_in, 16)

            def ln_rstd(i, n):
                pool.wait_ge(mv_ready, i + 1)
                step(nc.gpsimd.tensor_scalar(vps[:, 0:n], mv[:, 0:n, 1], 1e-5, None, ALU.add))
                nc.gpsimd.tensor_tensor(rstd[:, 0:n], vps[:, 0:n], nhalf[:, 0:n], ALU.pow).then_inc(rstd_ready, 1)

            def norm_root(n):
                pool.wait_ge(ss_ready, n + 1)
                nc.gpsimd.tensor_tensor(nrm[:], ss[:], phalf[:, 0:NH], ALU.pow).then_inc(nrm_ready, 1)

            norms, qs = 0, 0
            for stage, l, b, _ in schedule():
                if stage == "S0":
                    nc.gpsimd.memset(key_tok[:, :, 50:52], -0.5).then_inc(consts_ready, 1)
                    for part in (key_tok, qry_tok):
                        nc.gpsimd.memset(part[:, :, STK:STKW], 0.0).then_inc(consts_ready, 1)
                    nc.gpsimd.memset(qry_tok[:, :, 48:50], -0.5).then_inc(consts_ready, 1)
                    norm_root(0)
                if stage == "S1":
                    norm_root(1)
                if stage == "T" and l < LAYERS:
                    pool.wait_ge(y_ready, t_norm[b])
                    off = D * (1 + l) if before_attention[b] else D * (3 + l)
                    before_attention[b] = not before_attention[b]
                    x = x_res[:, 2 * b:2 * b + 2, :]
                    nc.gpsimd.tensor_tensor(x, x, rows_sb[:, off:off + D].unsqueeze(1).broadcast_to([P, 2, D]),
                                            ALU.add).then_inc(xbias_ready, 1)
                if stage == "Q":
                    for t in (2 * b, 2 * b + 1):
                        qs += 1
                        pool.wait_ge(qrec_ready, qs)
                        v = q_tok[t].rearrange("p (h d) -> p h d", h=8)
                        nc.gpsimd.tensor_tensor(v, v, qrec[:, t, :].unsqueeze(2).broadcast_to([P, 8, HD]),
                                                ALU.mult).then_inc(qnorm_ready, 1)
                if stage in NORMS:
                    ln_rstd(norms, 2)
                    norms += 1
                    t_norm[b] = norms

            pool.wait_ge(acc_taken, TOK_ACC)
            for r in range(2):
                step(nc.gpsimd.memset(vhead[r][:, :, 16:32], 0.0))
                step(nc.gpsimd.memset(vhead[r][:, :, 16:17], 1.0))

            def head_v(n, r):
                nc.gpsimd.tensor_copy(vhead[r][:, :, 0:DH], qv[:, :, bass.ds(n * DH + C, DH)]).then_inc(vhead_ready, 1)

            def route(r, par):
                pool.wait_ge(onrm_ready, r + 1)
                hr = h_res[:, bass.ds(r, 1), :].rearrange("p a c -> p (a c)")
                nc.gpsimd.tensor_tensor(hr, hr, o_nrm[:], ALU.add).then_inc(h_ready, 1)

            def route2(r, par):
                hr = h_res[:, bass.ds(r, 1), :].rearrange("p a c -> p (a c)")
                held_wait(pool, lmv_ready, r + 1)
                step(nc.gpsimd.tensor_scalar(vps[:, 0:1], mv[:, 0, 1:2], 1e-5, None, ALU.add))
                nc.gpsimd.tensor_tensor(rstd[:, 0:1], vps[:, 0:1], nhalf[:, 0:1], ALU.pow).then_inc(lrstd_ready, 1)
                held_wait(pool, ms_ready, r + 1)
                step(nc.gpsimd.tensor_scalar(mse[:], ms[:], 1.0 / C, 1e-5, ALU.mult, ALU.add))
                nc.gpsimd.tensor_tensor(rms[:], mse[:], nhalf[:, 0:1], ALU.pow).then_inc(rms_ready, 1)
                nc.gpsimd.tensor_tensor(hr, hr, ln[:], ALU.add).then_inc(base_ready, 1)

            def scatter(r, par):
                held_wait(pool, gd_ready, r + 1)
                nc.gpsimd.tensor_tensor(wexp[:], euler[:], gd[:], ALU.pow).then_inc(wexp_ready, 1)
                if isinstance(r, int) and r == NT - 1:
                    pool.wait_ge(pads_out, 16 * E)
                held_wait(pool, slots_ready, r + 1)
                for k in range(TOPK):
                    nc.gpsimd.indirect_dma_start(
                        xs[:, :], bass.IndirectOffsetOnAxis(ap=slot_u[:, k:k + 1], axis=0),
                        t_row[:], None).then_inc(rows_out, 16)

            def pool_head(n, r, par, first, last, prep2=True):
                if not first:
                    route(r, 1 - par)
                if not last:
                    if not first:
                        pool.wait_ge(oacc_ready, n)
                    head_v(n + 1, 1 - par)
                if not first:
                    route2(r, 1 - par)
                if not last and prep2:
                    norm_root(n + 2)
                if not first:
                    scatter(r, 1 - par)

            head_v(0, 0)
            pool_head(0, None, 0, True, False)
            before = step.n
            with pool.Fori(0, 4) as i:
                for p in (0, 1):
                    step.rebase(i * (2 * POOL_STEPS) + (before + POOL_STEPS * p))
                    pool_head(i * 2 + (1 + p), i * 2 + p, 1 - p, False, False)
                    assert step.n == POOL_STEPS, step.n
            step.rebase(before + 8 * POOL_STEPS)
            pool_head(NT - 3, NT - 4, 1, False, False)
            pool_head(NT - 2, NT - 3, 0, False, False, prep2=False)
            pool.wait_ge(tr_taken, tr_base(NT - 2))
            nc.gpsimd.iota(edges, pattern=[[P, NT]], base=0, channel_multiplier=0,
                           allow_small_or_imprecise_dtypes=True).then_inc(plan_consts, 1)
            pool_head(NT - 1, NT - 2, 1, False, True)
            route(NT - 1, 1)
            route2(NT - 1, 1)
            scatter(NT - 1, 1)

            def expert(j, r, added=None):
                if added is not None:
                    pool.wait_ge(y_out, added * 16)
                    pool.wait_ge(y_psum, added + 1)
                pool.wait_ge(sig_ready, j + 1)
                pool.wait_ge(prod_ready, j + 1)
                nc.gpsimd.tensor_tensor(actv[r], prod[r], sig[r], ALU.mult).then_inc(actv_ready, 1)

            def add_rows(j, r):
                held_wait(pool, y_ready2, j + 1)
                nc.gpsimd.indirect_dma_start(
                    out[:, :], bass.IndirectOffsetOnAxis(ap=tok_idx[r], axis=0), yt[r], None,
                    compute_op=ALU.add).then_inc(y_out, 16)

            expert(0, 0)
            expert(1, 1)
            expert(2, 0)
            pool.wait_ge(out_init, 16)
            add_rows(0, 0)
            expert(3, 1, 1)
            add_rows(1, 1)
            with pool.Fori(1, MT // 2 - 1) as i:
                for r in (0, 1):
                    expert(i * 2 + (2 + r), r, i * 2 + r)
                    add_rows(i * 2 + r, r)
            expert(MT - 1, 0, MT - 3)
            add_rows(MT - 3, 0)
            pool.wait_ge(y_out, 16 * (MT - 2))
            add_rows(MT - 2, 1)
            pool.wait_ge(y_out, 16 * (MT - 1))
            add_rows(MT - 1, 0)
            pool.wait_ge(y_out, 16 * MT)

        @block.tensor
        def _(pe):
            acc, acts, kts = [0], [0], [0]

            def acc_job():
                if acc[0] >= 2:
                    pe.wait_ge(acc_taken, acc[0] - 1)
                acc[0] += 1
                return bank((acc[0] - 1) % 2)

            def act_job():
                if acts[0] >= 2:
                    pe.wait_ge(act_taken, acts[0] - 1)
                acts[0] += 1
                return bank(2 + (acts[0] - 1) % 2)

            b7 = bank(7)
            b7h = bank(7).bitcast(f16)

            def stacks(g, n, job):
                if not isinstance(job, int) or job:
                    pe.wait_ge(tr_taken, job)
                if g == 0:
                    pe.wait_ge(stack_ready, n + 1)
                for s in range(8):
                    k = 8 * g + s
                    src = key_tok[:, k, :] if k < NH else qry_tok[:, k - NH, :]
                    last = nc.tensor.transpose(b7h[0:STKW, s * P:(s + 1) * P], src, ident16[:])
                last.then_inc(tr_ready, 1)

            pe.wait_ge(consts_ready, NCONST)
            trks, trqs, ctxws = 0, 0, 0
            norms, qs = 0, 0
            norm_of, t_job, kt_of, v_job, trk_of, trq_of, ctx_job, ctxw_of, hid_job, pt_of = ({} for _ in range(10))
            for stage, l, b, tiles in schedule():
                mine = (2 * b, 2 * b + 1) if b is not None else ()
                if stage == "conv" and b == 0:
                    tile = [acc_job()[:, 0:D] for s in range(2)]
                    for k in range(KT):
                        if k * 4 % KT == 0:
                            pe.wait_ge(convw_in[k * 4 // KT], 16)
                            pe.wait_ge(patch0_in[k * 4 // KT], 16)
                        for s in range(2):
                            last = nc.tensor.matmul(tile[s], patch_sb[b][:, k, s * P:s * P + P], convw_sb[:, k, :],
                                                    start=(k == 0), stop=(k == KT - 1))
                            if k == KT - 1:
                                last.then_inc(acc_ready, 1)
                if stage == "conv" and b:
                    pe.wait_ge(patch_in[b], 16)
                    for s in range(2):
                        o = acc_job()[:, 0:D]
                        for k in range(KT):
                            last = nc.tensor.matmul(o, patch_sb[b][:, k, s * P:s * P + P], convw_sb[:, k, :],
                                                    start=(k == 0), stop=(k == KT - 1))
                        last.then_inc(acc_ready, 1)
                if stage == "T":
                    pe.wait_ge(y_ready, norm_of[b])
                    o = act_job()
                    for s in range(2):
                        last = nc.tensor.transpose(o[:, s * P:(s + 1) * P], x_nrm[:, 2 * b + s, :], ident[:])
                    last.then_inc(act_ready, 1)
                    t_job[b] = acts[0]
                if stage == "A":
                    if b == 0 and l == 0:
                        pe.wait_ge(qkvw_in, 16)
                    pe.wait_ge(act_taken, t_job[b])
                    for hp in range(2):
                        if kts[0] >= 2:
                            pe.wait_ge(kt_taken, kts[0] - 1)
                        o = bank(4 + kts[0] % 2)
                        kts[0] += 1
                        for s in range(2):
                            h = 2 * hp + s
                            last = nc.tensor.matmul(o[:, s * NPIX:(s + 1) * NPIX],
                                                    qkvw_sb[:, l, INNER + h * P:INNER + (h + 1) * P],
                                                    yT[:, b * NPIX:(b + 1) * NPIX], start=True, stop=True)
                        last.then_inc(kt_ready, 1)
                    kt_of[b] = kts[0]
                    for t in mine:
                        o = act_job()
                        nc.tensor.matmul(o, yT[:, t * P:(t + 1) * P], qkvw_sb[:, l, 2 * INNER:3 * INNER],
                                         start=True, stop=True).then_inc(act_ready, 1)
                        o = acc_job()
                        nc.tensor.matmul(o, yT[:, t * P:(t + 1) * P], qkvw_sb[:, l, 0:INNER],
                                         start=True, stop=True).then_inc(acc_ready, 1)
                    v_job[b] = acts[0]
                if stage == "B":
                    pe.wait_ge(kt_taken, kt_of[b])
                    for t in mine:
                        if trks:
                            pe.wait_ge(trk_taken, trks)
                        if ctxws:
                            pe.wait_ge(ctxw_taken, ctxws)
                        for h in range(NPAIR):
                            last = nc.tensor.transpose(bank(7)[:, h * P:(h + 1) * P], kT[b][:, h, (t % 2) * P:(t % 2 + 1) * P],
                                                       ident[:])
                        last.then_inc(trk_ready, 1)
                        trks += 1
                        qs += 1
                        pe.wait_ge(qnorm_ready, qs)
                        if trqs:
                            pe.wait_ge(trq_taken, trqs)
                        for h in range(NPAIR):
                            last = nc.tensor.transpose(bank(6)[:, h * P:(h + 1) * P], q_tok[t][:, h * P:(h + 1) * P], ident[:])
                        last.then_inc(trq_ready, 1)
                        trqs += 1
                    trq_of[b] = trqs
                    trk_of[b] = trks
                if stage == "W":
                    pe.wait_ge(tokw_in, 16 * 4)
                    pe.wait_ge(acc_taken, ctx_job[b])
                    pe.wait_ge(trk_taken, trks)
                    if ctxws:
                        pe.wait_ge(ctxw_taken, ctxws)
                    for h in range(NPAIR):
                        last = nc.tensor.matmul(bank(7)[:, h * P:(h + 1) * P], ctx_bd[:, b, h, :], outw_sb[:, l, h, :],
                                                start=True, stop=True)
                    last.then_inc(ctxw_ready, 1)
                    ctxws += 1
                    ctxw_of[b] = ctxws
                if stage == "K":
                    pe.wait_ge(trk_taken, trk_of[b])
                    pe.wait_ge(act_taken, v_job[b])
                    o = acc_job()
                    for h in range(NPAIR):
                        for s in range(2):
                            last = nc.tensor.matmul(o[:, h * P:(h + 1) * P], v_tok[2 * b + s][:, h * P:(h + 1) * P],
                                                    k_tok[:, 2 * b + s, h * P:(h + 1) * P], start=(s == 0), stop=(s == 1))
                    last.then_inc(acc_ready, 1)
                    ctx_job[b] = acc[0]
                if stage == "C":
                    pe.wait_ge(ctxw_taken, ctxw_of[b])
                    pe.wait_ge(trq_taken, trq_of[b])
                    for s in range(2):
                        o = acc_job()[:, 0:D]
                        for h in range(NPAIR):
                            last = nc.tensor.matmul(o, qT[b][:, h, s * P:(s + 1) * P], ctx_w[:, b, h, :],
                                                    start=(h == 0), stop=(h == NPAIR - 1))
                        last.then_inc(acc_ready, 1)
                if stage == "D1":
                    pe.wait_ge(act_taken, t_job[b])
                    for hp in range(2):
                        o = act_job()
                        for s in range(2):
                            h = 2 * hp + s
                            last = nc.tensor.matmul(o[:, s * NPIX:(s + 1) * NPIX], ff1w_sb[:, l, h * P:(h + 1) * P],
                                                    yT[:, b * NPIX:(b + 1) * NPIX], start=True, stop=True)
                        last.then_inc(act_ready, 1)
                    hid_job[b] = acts[0]
                if stage == "D2":
                    pe.wait_ge(act_taken, hid_job[b])
                    for t in mine:
                        o = acc_job()[:, 0:D]
                        for h in range(4):
                            last = nc.tensor.matmul(o, mlp_hid[:, h, t * P:(t + 1) * P], ff2w_sb[:, l, h, :],
                                                    start=(h == 0), stop=(h == 3))
                        last.then_inc(acc_ready, 1)
                if stage == "H":
                    pe.wait_ge(act_taken, t_job[b])
                    for t in mine:
                        o = acc_job()[:, 0:C]
                        nc.tensor.matmul(o, yT[:, t * P:(t + 1) * P], headw_sb, start=True, stop=True).then_inc(acc_ready, 1)
                if stage == "PT":
                    pe.wait_ge(y_ready, norm_of[tiles])
                    o = act_job()
                    for s in range(2):
                        nc.tensor.transpose(o[:, s * 256:s * 256 + P], h_nrm[s][:, 0:P], ident[:])
                        last = nc.tensor.transpose(o[0:CB, s * 256 + P:s * 256 + 2 * P], h_nrm[s][:, P:C], ident[:])
                    last.then_inc(act_ready, 1)
                    pt_of[tiles] = acts[0]
                if stage == "PP":
                    pe.wait_ge(small_in, 16 * 9)
                    pe.wait_ge(act_taken, pt_of[tiles])
                    for s in range(2):
                        o = acc_job()[:, 0:2 * C]
                        nc.tensor.matmul(o, hnT[s][:, 0:P], wqva_sb, start=True, stop=False)
                        nc.tensor.matmul(o, hnT[s][0:CB + 1, P:2 * P], wqvb_sb, start=False, stop=True).then_inc(acc_ready, 1)
                if stage == "S2":
                    pe.wait_ge(trk_taken, trks)
                    pe.wait_ge(ctxw_taken, ctxws)
                    for g in range(3):
                        stacks(g, 0, g)
                if stage in NORMS:
                    norms += 1
                    norm_of[b] = norm_of[tiles] = norms

            SETS = [ps[:, 0:QS], ps[:, QS:2 * QS]]
            oacc = bank(6)

            def scores(n_par, kb, s):
                if s is not None:
                    pe.wait_ge(probs_ready, s)
                for c, keys, qrys, row in ((0, keysT, qrysT, 0), (1, keysT2, qrysT2, ROW2), (2, keysT, qrysT, 0)):
                    last = nc.tensor.matmul(SETS[kb % 2][:, c * 512:(c + 1) * 512], keys[n_par][:, kb * P:(kb + 1) * P],
                                            qrys[n_par][:, c * 512:(c + 1) * 512], start=True, stop=True,
                                            tile_position=(row, 0))
                last.then_inc(scores_ready, 1)

            def weighted(n, par, kb):
                if kb == 0:
                    pe.wait_ge(vhead_ready, n + 1)
                    pe.wait_ge(oacc_ready, n)
                pe.wait_ge(probs_ready, n * KEYB + (kb + 1))
                for g in range(QG):
                    last = nc.tensor.matmul(oacc[32 * g:32 * g + 32, 0:QW], vhead[par][:, kb, :],
                                            probs[kb % 3][:, g * QW:(g + 1) * QW], start=(kb == 0),
                                            stop=(kb == KEYB - 1), tile_position=(0, 32 * g))
                last.then_inc(probs_used, 1)

            def out_transpose(r, job):
                pe.wait_ge(tr_taken, job)
                pe.wait_ge(oacc_ready, r + 1)
                for c in range(3):
                    last = nc.tensor.transpose(b7[:, c * P:(c + 1) * P], o_acc[:, c * P:(c + 1) * P], ident[:])
                last.then_inc(tr_ready, 1)

            def t_transpose(r, par, job):
                pe.wait_ge(tr_taken, job)
                pe.wait_ge(t_ready, r + 1)
                nc.tensor.transpose(b7[:, 0:P], t_row[:, 0:P], ident[:])
                nc.tensor.transpose(b7[0:CB, P:2 * P], t_row[:, P:C], ident[:]).then_inc(tr_ready, 1)

            def logits(job):
                pe.wait_ge(tr_taken, job)
                nc.tensor.matmul(b7[:, 0:E], tT[:, 0:P], gatea_sb[:], start=True, stop=False)
                nc.tensor.matmul(b7[:, 0:E], tT[0:CB + 1, P:2 * P], gateb_sb[:], start=False, stop=True).then_inc(tr_ready, 1)

            def ranks(r, job):
                pe.wait_ge(tr_taken, job)
                pe.wait_ge(mask_ready, r + 1)
                nc.tensor.matmul(b7[:, 0:E], tri[:], mask[:], start=True, stop=False)
                nc.tensor.matmul(b7[:, 0:E], ones[:], seen[:], start=False, stop=True).then_inc(tr_ready, 1)

            def counts(tiles, job):
                pe.wait_ge(tr_taken, job)
                pe.wait_ge(slots_ready, tiles)
                nc.tensor.matmul(b7[:, 0:E], ones[:], seen[:], start=True, stop=True).then_inc(tr_ready, 1)

            def pe_head(n, r, par, first, last):
                base = 3 if first else tr_base(r)
                for kb in range(KEYB):
                    if kb + 2 < KEYB:
                        scores(par, kb + 2, n * KEYB + (kb + 1))
                    elif not last:
                        if kb + 2 == KEYB:
                            pe.wait_ge(tr_taken, base + (3 if first else 4))
                        scores(1 - par, kb + 2 - KEYB, n * KEYB + (kb + 1))
                    weighted(n, par, kb)
                    if first:
                        if kb in (5, 7, 9):
                            stacks((kb - 5) // 2, n + 1, base + (kb - 5) // 2)
                    elif not last:
                        if kb == 1: out_transpose(r, base)
                        if kb == 2: stacks(0, n + 1, base + 1)
                        if kb == 4: stacks(1, n + 1, base + 2)
                        if kb == 5: stacks(2, n + 1, base + 3)
                        if kb == 7: t_transpose(r, 1 - par, base + 4)
                        if kb == 8: logits(base + 5)
                        if kb == 10: ranks(r, base + 6)
                    else:
                        if kb == 1: out_transpose(r, base)
                        if kb == 4: t_transpose(r, 1 - par, base + 1)
                        if kb == 5: logits(base + 2)
                        if kb == 6: ranks(r, base + 3)
                        if kb == 7: counts(NT - 1, base + 4)

            pe.wait_ge(acc_taken, TOK_ACC)
            pe.wait_ge(tr_taken, 3)
            scores(0, 0, None)
            scores(0, 1, None)
            pe_head(0, None, 0, True, False)
            with pe.Fori(0, 4) as i:
                for p in (0, 1):
                    pe_head(i * 2 + (1 + p), i * 2 + p, 1 - p, False, False)
            pe_head(NT - 3, NT - 4, 1, False, False)
            pe_head(NT - 2, NT - 3, 0, False, False)
            pe_head(NT - 1, NT - 2, 1, False, True)
            base = tr_base(NT - 2) + 5
            out_transpose(NT - 1, base)
            for t in range(NT - 1):
                last = nc.tensor.transpose(ps[0:E, t * P:(t + 1) * P], comb_all[:, t, :], ident[:])
            last.then_inc(combT_psum, 1)

            def weighted_bias(pair):
                for s in range(2):
                    t = 2 * pair + s
                    last = nc.tensor.matmul(bank(BIAS_BANK[pair])[:, s * C:s * C + C], combT[:, t * P:(t + 1) * P], b2_sb,
                                            start=True, stop=True)
                last.then_inc(bias_psum, 1)

            pe.wait_ge(combT_ready, 1)
            pe.wait_ge(b2_in, 16)
            weighted_bias(0)
            weighted_bias(1)
            t_transpose(NT - 1, 1, base + 1)
            logits(base + 2)
            weighted_bias(2)
            ranks(NT - 1, base + 3)
            weighted_bias(3)
            counts(NT, base + 4)
            nc.tensor.transpose(ps[0:E, (NT - 1) * P:NT * P], comb_all[:, NT - 1, :], ident[:]).then_inc(combT_psum, 1)
            weighted_bias(4)
            pe.wait_ge(combT_ready, 2)
            weighted_bias(5)
            pe.wait_ge(tr_taken, base + 5)
            pe.wait_ge(plan_cols_ready, 1)
            for c in range(2):
                last = nc.tensor.matmul(b7[0:1, c * P:(c + 1) * P], plan_cols[:, c:c + 1], ident[:], start=True, stop=True)
            last.then_inc(tr_ready, 1)
            pe.wait_ge(w_in, 16 * 12)
            pe.wait_ge(plan_ready, 1)
            pe.wait_ge(tr_taken, base + 6)
            pe.wait_ge(bias_added, NT // 2)

            def x_transpose(j, r, n_loaded):
                pe.wait_ge(x_in[r], n_loaded)
                o = bank(7 * r)
                nc.tensor.transpose(o[:, 0:P], xt[r][:, 0:P], ident[:])
                nc.tensor.transpose(o[0:CB, P:2 * P], xt[r][:, P:C], ident[:]).then_inc(x_read, 1)

            def mlp1(j, r, wait=True):
                ex = pe.value_load(ej_i[0:1, bass.ds(j, 1)], min_val=0, max_val=E - 1)
                pe.wait_ge(xT_ready, j + 1)
                if wait:
                    pe.wait_ge(lin_ready, j - 1)
                for half in range(2):
                    o = bank(1 + 2 * half + r)[:, 0:FF]
                    nc.tensor.matmul(o, xtT[r][:, 0:P], w1a_sb[:, bass.ds(ex * 768 + half * FF, FF)], start=True, stop=False)
                    nc.tensor.matmul(o, xtT[r][0:CB + 1, P:2 * P], w1b_sb[0:CB + 1, bass.ds(ex * 768 + half * FF, FF)],
                                     start=False, stop=True).then_inc(h_done, 1)

            def act_transpose(j, r, wait=True):
                pe.wait_ge(actv_ready, j + 1)
                if wait:
                    pe.wait_ge(aT_ready, j)
                for c in range(3):
                    last = nc.tensor.transpose(bank(5)[:, c * P:(c + 1) * P], actv[r][:, c * P:(c + 1) * P], ident[:])
                last.then_inc(aT_psum, 1)

            def mlp2(j, r, wait=True):
                ex = pe.value_load(ej_i[0:1, bass.ds(j, 1)], min_val=0, max_val=E - 1)
                pe.wait_ge(aT_ready, j + 1)
                if wait:
                    pe.wait_ge(y_sb, j)
                for c in range(3):
                    last = nc.tensor.matmul(bank(6)[:, 0:C], actT[r][:, c * P:(c + 1) * P],
                                            w2_sb[:, bass.ds((ex * 3 + c) * C, C)], start=(c == 0), stop=(c == 2))
                last.then_inc(y_psum, 1)

            pe.wait_ge(xT_ones, 2)
            x_transpose(0, 0, 16)
            x_transpose(1, 1, 16)
            mlp1(0, 0, False)
            x_transpose(2, 0, 32)
            mlp1(1, 1, False)
            act_transpose(0, 0, False)
            x_transpose(3, 1, 32)
            mlp1(2, 0)
            mlp2(0, 0, False)
            act_transpose(1, 1)
            x_transpose(4, 0, 48)
            mlp1(3, 1)
            mlp2(1, 1)
            act_transpose(2, 0)
            with pe.Fori(2, MT // 2 - 1) as i:
                x_transpose(i * 2 + 1, 1, i * 16 + 16)
                mlp1(i * 2, 0)
                mlp2(i * 2 - 2, 0)
                act_transpose(i * 2 - 1, 1)
                x_transpose(i * 2 + 2, 0, i * 16 + 32)
                mlp1(i * 2 + 1, 1)
                mlp2(i * 2 - 1, 1)
                act_transpose(i * 2, 0)
            x_transpose(MT - 2, 1, 16 * (MT // 2))
            mlp1(MT - 3, 0)
            mlp2(MT - 5, 0)
            act_transpose(MT - 4, 1)
            x_transpose(MT - 1, 0, 16 * (MT // 2 + 1))
            mlp1(MT - 2, 1)
            mlp2(MT - 4, 1)
            act_transpose(MT - 3, 0)
            mlp1(MT - 1, 0)
            mlp2(MT - 3, 0)
            act_transpose(MT - 2, 1)
            mlp2(MT - 2, 1)
            act_transpose(MT - 1, 0)
            mlp2(MT - 1, 0)

        @block.scalar
        def _(act):
            acts = [0]

            def act_job():
                acts[0] += 1
                act.wait_ge(act_ready, acts[0])
                return bank(2 + (acts[0] - 1) % 2)

            act.wait_ge(cols_in, 16)
            kts, trks, acc, half = 0, 0, 0, {}
            for stage, l, b, tiles in schedule():
                if stage == "T":
                    i = half.get(b, 0)
                    half[b] = i + 1
                    g, o = ((i % 2) * 4 + l, (i % 2) * 4 + 2 + l) if l < LAYERS else (8, 9)
                    src = act_job()
                    nc.scalar.activation(yT[:, b * NPIX:(b + 1) * NPIX], src[:, 0:NPIX], ACT.Identity,
                                         bias=cols_sb[:, o:o + 1], scale=cols_sb[:, g:g + 1]).then_inc(act_taken, 1)
                if stage == "A":
                    for hp in range(2):
                        act.wait_ge(kmax_ready, kts + 1)
                        for s in range(2):
                            h = 2 * hp + s
                            last = nc.scalar.activation(kT[b][:, h, :], bank(4 + kts % 2)[:, s * NPIX:(s + 1) * NPIX], ACT.Exp,
                                                        bias=knmax[:, h, b:b + 1], accum_out=ksum[:, h, b:b + 1])
                        last.then_inc(kt_taken, 1)
                        kts += 1
                    for t in (2 * b, 2 * b + 1):
                        src = act_job()
                        nc.scalar.activation(v_tok[t], src, ACT.Identity).then_inc(act_taken, 1)
                    for s in range(2):
                        act.wait_ge(acc_taken, acc + s + 1)
                        nc.scalar.activation(q_tok[2 * b + s], q_tok[2 * b + s], ACT.Exp).then_inc(qexp_ready, 1)
                if stage == "B":
                    for t in (2 * b, 2 * b + 1):
                        trks += 1
                        act.wait_ge(trk_ready, trks)
                        nc.scalar.activation(k_tok[:, t, :], bank(7), ACT.Identity).then_inc(trk_taken, 1)
                if stage == "D1":
                    for hp in range(2):
                        src = act_job()
                        for s in range(2):
                            h = 2 * hp + s
                            last = nc.scalar.activation(mlp_hid[:, h, b * NPIX:(b + 1) * NPIX], src[:, s * NPIX:(s + 1) * NPIX],
                                                        ACT.Gelu, bias=cols_sb[:, 10 + 4 * l + h:11 + 4 * l + h])
                        last.then_inc(act_taken, 1)
                if stage == "PT":
                    src = act_job().rearrange("p (s n) -> p s n", s=2)
                    nc.scalar.activation(hnT_both[:, :, 0:P], src[:, :, 0:P], ACT.Identity)
                    nc.scalar.activation(hnT_both[0:CB, :, P:2 * P], src[0:CB, :, P:2 * P], ACT.Identity).then_inc(act_taken, 1)
                acc += ACC_JOBS.get(stage, 0)

            SETS = [ps[:, 0:QS], ps[:, QS:2 * QS]]

            def act_head(n):
                for kb in range(KEYB):
                    act.wait_ge(scores_ready, n * KEYB + (kb + 1))
                    if not isinstance(n, int) or n * KEYB + kb >= 3:
                        act.wait_ge(probs_used, n * KEYB + kb - 2)
                    nc.scalar.activation(probs[kb % 3], SETS[kb % 2], ACT.Exp, scale=0.5).then_inc(probs_ready, 1)
                    if kb == 0 and not (isinstance(n, int) and n == 0):
                        sums_copy(n)

            def sums_copy(n):
                act.wait_ge(probs_used, n * KEYB)
                nc.scalar.activation(o_acc[:], bank(6)[:, 0:QW], ACT.Identity).then_inc(oacc_ready, 1)

            act_head(0)
            with act.Fori(1, NT) as i:
                act_head(i)
            sums_copy(NT)

            for i, cols_ in enumerate((slice(0, (NT - 1) * P), slice((NT - 1) * P, NT * P))):
                act.wait_ge(combT_psum, i + 1)
                nc.scalar.activation(combT[:, cols_], ps[0:E, cols_], ACT.Identity).then_inc(combT_ready, 1)
                if i == 0:
                    act.wait_ge(cnt_ready, 1)
                    for e in ACT_PADS:
                        pad_bucket(act, e)
            act.wait_ge(plan_ready, 1)

            def x_copy(j, r):
                ex = act.value_load(ej_i[0:1, bass.ds(j, 1)], min_val=0, max_val=E - 1)
                act.wait_ge(x_read, j + 1)
                o = bank(7 * r)
                nc.scalar.activation(xtT[r][:, 0:P], o[:, 0:P], ACT.Identity)
                nc.scalar.activation(xtT[r][0:CB, P:2 * P], o[0:CB, P:2 * P], ACT.Identity).then_inc(xT_ready, 1)
                nc.scalar.activation(w_all[:, bass.ds(j, 1)], xt[r][:, bass.ds(ex + COMB, 1)], ACT.Identity)
                nc.scalar.activation(tok_all[:, bass.ds(j, 1)], xt[r][:, TOKEN:RW].bitcast(u32),
                                     ACT.Identity).then_inc(x_copied, 1)

            def sigmoid(j, r):
                act.wait_ge(glu_ready, j + 1)
                nc.scalar.activation(sig[r], glu[r], ACT.Sigmoid, scale=1.702).then_inc(sig_ready, 1)

            def y_tile(j, r, wait=True):
                act.wait_ge(y_psum, j + 1)
                if wait:
                    act.wait_ge(y_out, j * 16 - 16)
                act.wait_ge(x_copied, j + 1)
                nc.scalar.activation(yt[r], bank(6)[:, 0:C], ACT.Identity, scale=w_all[:, bass.ds(j, 1)]).then_inc(y_sb, 1)
                nc.scalar.activation(tok_idx[r], tok_all[:, bass.ds(j, 1)], ACT.Identity).then_inc(y_ready2, 1)

            x_copy(0, 0)
            x_copy(1, 1)
            sigmoid(0, 0)
            x_copy(2, 0)
            act.wait_ge(bias_added, NT // 2)
            act.dma_start(out[0:DUMP, :].rearrange("(t p) c -> p t c", p=P), h_res[:]).then_inc(out_init, 16)
            sigmoid(1, 1)
            x_copy(3, 1)
            sigmoid(2, 0)
            y_tile(0, 0, False)
            x_copy(4, 0)
            sigmoid(3, 1)
            y_tile(1, 1, False)
            with act.Fori(2, MT // 2 - 1) as i:
                x_copy(i * 2 + 1, 1)
                sigmoid(i * 2, 0)
                y_tile(i * 2 - 2, 0)
                x_copy(i * 2 + 2, 0)
                sigmoid(i * 2 + 1, 1)
                y_tile(i * 2 - 1, 1)
            x_copy(MT - 2, 1)
            sigmoid(MT - 3, 0)
            y_tile(MT - 5, 0)
            x_copy(MT - 1, 0)
            sigmoid(MT - 2, 1)
            y_tile(MT - 4, 1)
            sigmoid(MT - 1, 0)
            y_tile(MT - 3, 0)
            y_tile(MT - 2, 1)
            y_tile(MT - 1, 0)

        @block.vector
        def _(dve):
            step = Chain(dve, dve_step)
            acc, lns = [0], [0]

            def acc_job():
                acc[0] += 1
                dve.wait_ge(acc_ready, acc[0])
                return bank((acc[0] - 1) % 2)

            def layer_norm(srcs, dsts):
                n = len(srcs)
                for s, x in enumerate(srcs):
                    step(nc.vector.bn_stats(stat[:, s, :], x))
                for s in range(n):
                    last = nc.vector.bn_aggr(mv[:, s, :], stat[:, s, :])
                last.then_inc(mv_ready, 1)
                lns[0] += 1
                dve.wait_ge(rstd_ready, lns[0])
                dve.wait_ge(mv_ready, lns[0])
                for s, (x, y) in enumerate(zip(srcs, dsts)):
                    last = nc.vector.tensor_scalar(y, x, mv[:, s, 0:1], rstd[:, s:s + 1], ALU.subtract, ALU.mult)
                last.then_inc(y_ready, 1)

            def image_norm(b):
                layer_norm([x_res[:, 2 * b + s, :] for s in range(2)], [x_nrm[:, 2 * b + s, :] for s in range(2)])

            b7 = bank(7)
            b7h = bank(7).bitcast(f16)

            def heads(ap):
                return ap.rearrange("p (h d) -> p h d", h=NH)

            def per_head(ap):
                return ap.unsqueeze(2).broadcast_to([P, NH, DH])

            def prep_squares(n):
                qh = qv[:, bass.ds(n, 1), 0:C].rearrange("p a c -> p (a c)")
                step(nc.vector.tensor_tensor(sq[:], qh, qh, ALU.mult))
                nc.vector.reduce_sum(ss[:], heads(sq[:]), AX.X).then_inc(ss_ready, 1)

            def prep(n):
                qh = qv[:, bass.ds(n, 1), 0:C].rearrange("p a c -> p (a c)")
                dve.wait_ge(nrm_ready, n + 1)
                step(nc.vector.tensor_scalar(nrmc[:], nrm[:], 1e-12, None, ALU.max))
                step(nc.vector.reciprocal(rn[:], nrmc[:]))
                step(nc.vector.tensor_tensor(heads(qn[:]), heads(qh), per_head(rn[:]), ALU.mult))
                nc.vector.tensor_copy(key_tok[:, :, 0:16], heads(qn[:]))
                step(nc.vector.tensor_tensor(sq[:], qn[:], qn[:], ALU.mult))
                nc.vector.tensor_tensor(key_tok[:, :, 32:48], heads(qn[:]), key_tok[:, :, 0:16], ALU.subtract)
                step(nc.vector.reduce_sum(aa[:], heads(sq[:]), AX.X))
                nc.vector.tensor_copy(key_tok[:, :, 16:32], key_tok[:, :, 0:16])
                step(nc.vector.tensor_copy(key_tok[:, :, 48:49], aa[:].unsqueeze(2)))
                nc.vector.tensor_copy(qry_tok[:, :, 0:16], key_tok[:, :, 0:16])
                nc.vector.tensor_copy(qry_tok[:, :, 32:48], key_tok[:, :, 0:16])
                nc.vector.tensor_copy(qry_tok[:, :, 16:32], key_tok[:, :, 32:48])
                step(nc.vector.tensor_tensor(key_tok[:, :, 49:50], aa[:].unsqueeze(2), key_tok[:, :, 48:49], ALU.subtract))
                nc.vector.tensor_copy(qry_tok[:, :, 50:52], key_tok[:, :, 48:50]).then_inc(stack_ready, 1)

            def stack_copy(g, par, job):
                dve.wait_ge(tr_ready, job + 1)
                src = b7h[0:STK, :].rearrange("p (s n) -> p s n", s=8)
                def heads_of(t, order):
                    return t[par].rearrange(order, h=NH)

                lo, hi = 8 * g, 8 * g + 8
                nk = max(0, min(hi, NH) - lo)
                copies = []
                if nk:
                    copies += [(heads_of(t, "p (t h) -> p h t")[:, lo:lo + nk, :], src[:, 0:nk, :]) for t in (keysT, keysT2)]
                if nk < 8:
                    copies += [(heads_of(qrysT, "p (h t) -> p h t")[:, lo + nk - NH:hi - NH, :], src[:, nk:8, :])]
                if g == 2:
                    copies += [(heads_of(qrysT2, "p (h t) -> p h t")[:, 4:8, :], src[:, 0:4, :])]
                for dst, part in copies:
                    last = nc.vector.tensor_copy(dst, part)
                last.then_inc(tr_taken, 1)

            dve.wait_ge(rows_in, 16)
            kts, qs, trqs, ctxws, biases, acts, pt_job = 0, 0, 0, 0, 0, 0, 0
            kt_of, bias_of = {}, {}
            for stage, l, b, tiles in schedule():
                mine = (2 * b, 2 * b + 1) if b is not None else ()
                if stage == "conv":
                    for t in mine:
                        src = acc_job()
                        nc.vector.tensor_tensor(x_res[:, t, :], src[:, 0:D], rows_sb[:, 0:D], ALU.add).then_inc(acc_taken, 1)
                    dve.wait_ge(acc_taken, acc[0])
                    image_norm(b)
                if stage == "T" and l < LAYERS:
                    biases += 1
                    bias_of[b] = biases
                if stage == "A":
                    for hp in range(2):
                        kts += 1
                        dve.wait_ge(kt_ready, kts)
                        nc.vector.tensor_reduce(knmax[:, 2 * hp:2 * hp + 2, b],
                                                bank(4 + (kts - 1) % 2).rearrange("p (h n) -> p h n", h=2), AX.X, ALU.max,
                                                negate=True).then_inc(kmax_ready, 1)
                    kt_of[b] = kts
                    for t in mine:
                        src = acc_job().rearrange("p (h d) -> p h d", h=8)
                        step(nc.vector.reduce_max(qmax[:, t, :], src, AX.X))
                        nc.vector.tensor_tensor(q_tok[t].rearrange("p (h d) -> p h d", h=8), src,
                                                qmax[:, t, :].unsqueeze(2).broadcast_to([P, 8, HD]),
                                                ALU.subtract).then_inc(acc_taken, 1)
                if stage == "Q":
                    for t in mine:
                        qs += 1
                        dve.wait_ge(qexp_ready, qs)
                        step(nc.vector.reduce_sum(qsum[:, t, :], q_tok[t].rearrange("p (h d) -> p h d", h=8), AX.X))
                        nc.vector.reciprocal(qrec[:, t, :], qsum[:, t, :]).then_inc(qrec_ready, 1)
                if stage == "B":
                    for s in range(2):
                        trqs += 1
                        dve.wait_ge(trq_ready, trqs)
                        nc.vector.tensor_copy(qT[b][:, :, s * P:(s + 1) * P],
                                              bank(6).rearrange("p (h n) -> p h n", h=NPAIR)).then_inc(trq_taken, 1)
                if stage == "K":
                    src = acc_job().rearrange("p (h n) -> p h n", h=NPAIR)
                    nc.vector.tensor_copy(ctx_bd[0:HD, b, :, 0:HD], src[0:HD, :, 0:HD])
                    nc.vector.tensor_copy(ctx_bd[HD:P, b, :, HD:P], src[HD:P, :, HD:P]).then_inc(acc_taken, 1)
                    dve.wait_ge(kt_taken, kt_of[b])
                    step(nc.vector.reciprocal(krec[:, :, b:b + 1], ksum[:, :, b:b + 1]))
                    step(nc.vector.tensor_scalar(krec8[:, :, b:b + 1], krec[:, :, b:b + 1], HD ** -0.5, None, ALU.mult))
                if stage == "W":
                    ctxws += 1
                    dve.wait_ge(ctxw_ready, ctxws)
                    nc.vector.tensor_tensor(ctx_w[:, b, :, :], bank(7).rearrange("p (h n) -> p h n", h=NPAIR),
                                            krec8[:, :, b:b + 1].broadcast_to([P, NPAIR, D]),
                                            ALU.mult).then_inc(ctxw_taken, 1)
                if stage in ("C", "D2"):
                    dve.wait_ge(xbias_ready, bias_of[b])
                    for t in mine:
                        src = acc_job()
                        nc.vector.tensor_tensor(x_res[:, t, :], src[:, 0:D], x_res[:, t, :], ALU.add).then_inc(acc_taken, 1)
                    dve.wait_ge(acc_taken, acc[0])
                    image_norm(b)
                if stage == "H":
                    dve.wait_ge(headb_in, 16)
                    for t in tiles:
                        src = acc_job()
                        nc.vector.tensor_tensor(h_res[:, t, :], src[:, 0:C], headb_sb, ALU.add).then_inc(acc_taken, 1)
                    dve.wait_ge(acc_taken, acc[0])
                if stage == "N":
                    dve.wait_ge(small_in, 16 * 9)
                if stage in ("H", "N"):
                    if pt_job:
                        dve.wait_ge(act_ready, pt_job)
                    layer_norm([h_res[:, t, :] for t in tiles], h_nrm)
                acts += ACT_JOBS.get(stage, 0)
                if stage == "PT":
                    pt_job = acts
                if stage == "PP":
                    for t in tiles:
                        src = acc_job()
                        nc.vector.tensor_copy(qv[:, t, :], src[:, 0:2 * C]).then_inc(acc_taken, 1)
                if stage == "S0":
                    dve.wait_ge(acc_taken, acc[0])
                    prep_squares(0)
                if stage == "S1":
                    dve.wait_ge(consts_ready, NCONST + 4)
                    prep(0)
                    prep_squares(1)
                if stage == "S2":
                    for g in range(3):
                        stack_copy(g, 0, g)
            prep(1)
            assert acc[0] == TOK_ACC, acc[0]
            dve.wait_ge(acc_taken, acc[0])

            def output(r, job):
                dve.wait_ge(tr_ready, job + 1)
                src = b7[:, 0:QW].rearrange("p (c g d) -> p c g d", c=3, g=QG)
                step(nc.vector.reciprocal(o_rec[:].unsqueeze(3), src[:, :, :, 16:17]))
                dst = o_nrm[:].rearrange("p (g c d) -> p c g d", g=QG, c=3)
                nc.vector.tensor_tensor(dst, src[:, :, :, 0:DH], o_rec[:].unsqueeze(3).broadcast_to([P, 3, QG, DH]),
                                        ALU.mult).then_inc(onrm_ready, 1)
                nc.vector.tensor_copy(bank_mark[:], ones[:, 0:1]).then_inc(tr_taken, 1)

            def norm_stats(r, par):
                hr = h_res[:, bass.ds(r, 1), :].rearrange("p a c -> p (a c)")
                dve.wait_ge(h_ready, r + 1)
                step(nc.vector.bn_stats(stat[:, 0, :], hr))
                nc.vector.memset(bank_mark[:], 0.0)
                nc.vector.bn_aggr(mv[:, 0, :], stat[:, 0, :]).then_inc(lmv_ready, 1)

            def norm_square(r, par):
                hr = h_res[:, bass.ds(r, 1), :].rearrange("p a c -> p (a c)")
                dve.wait_ge(lrstd_ready, r + 1)
                dve.wait_ge(lmv_ready, r + 1)
                step(nc.vector.tensor_scalar(ln[:], hr, mv[:, 0, 0:1], rstd[:, 0:1], ALU.subtract, ALU.mult))
                step(nc.vector.tensor_tensor(sq[:], ln[:], ln[:], ALU.mult))
                nc.vector.reduce_sum(ms[:], sq[:], AX.X).then_inc(ms_ready, 1)

            def norm_rows(r, par):
                dve.wait_ge(rms_ready, r + 1)
                dve.wait_ge(rows_out, r * (16 * TOPK) + 32)
                nc.vector.scalar_tensor_tensor(t_row[:, 0:C], ln[:], rms[:], nscale_sb[:], ALU.mult,
                                               ALU.mult).then_inc(t_ready, 1)
                nc.vector.tensor_copy(t_row[:, TOKEN:RW].bitcast(u32), token_no[:, bass.ds(r, 1)])

            def tT_copy(job):
                dve.wait_ge(tr_ready, job + 1)
                nc.vector.tensor_copy(tT[:, 0:P], b7[:, 0:P])
                nc.vector.tensor_copy(tT[0:CB, P:2 * P], b7[0:CB, P:2 * P]).then_inc(tr_taken, 1)

            def choose(r, job):
                dve.wait_ge(tr_ready, job + 1)
                nc.vector.tensor_copy(logit[:], b7[:, 0:E]).then_inc(tr_taken, 1)
                held_wait(dve, tr_taken, job + 1)
                step(nc.vector.max(top8[:], logit[:]))
                nc.vector.tensor_scalar(gd[:], top8[:, 0:TOPK], top8[:, 0:1], None, ALU.subtract).then_inc(gd_ready, 1)
                step(nc.vector.max_index(top_i[:], top8[:], logit[:]))
                step(nc.vector.tensor_copy(top_f[:], top_i[:, 0:TOPK]))
                step(nc.vector.tensor_tensor(onehot[:], iota_e[:].unsqueeze(1).broadcast_to([P, TOPK, E]),
                                             top_f[:].unsqueeze(2).broadcast_to([P, TOPK, E]), ALU.is_equal))
                nc.vector.reduce_sum(mask[:], onehot[:].rearrange("p k e -> p e k"), AX.X).then_inc(mask_ready, 1)

            def place(r, par, job):
                dve.wait_ge(tr_ready, job + 1)
                nc.vector.tensor_tensor(slot_e[:], b7[:, 0:E], bucket0[:], ALU.add).then_inc(tr_taken, 1)
                dve.wait_ge(tr_taken, job + 1)
                step(nc.vector.tensor_tensor(slot_oh[:], onehot[:], slot_e[:].unsqueeze(1).broadcast_to([P, TOPK, E]), ALU.mult))
                step(nc.vector.tensor_tensor(seen[:], seen[:], mask[:], ALU.add))
                step(nc.vector.reduce_sum(slot_f[:], slot_oh[:], AX.X))
                nc.vector.tensor_copy(slot_u[:], slot_f[:]).then_inc(slots_ready, 1)

            def weigh(r):
                comb = comb_all[:, bass.ds(r, 1), :].rearrange("p a e -> p (a e)")
                dve.wait_ge(wexp_ready, r + 1)
                nc.vector.tensor_tensor(slot_oh[:], onehot[:], wexp[:].unsqueeze(2).broadcast_to([P, TOPK, E]), ALU.mult)
                step(nc.vector.reduce_sum(wsum[:], wexp[:], AX.X))
                nc.vector.reduce_sum(slot_e[:], slot_oh[:].rearrange("p k e -> p e k"), AX.X)
                step(nc.vector.reciprocal(wrec[:], wsum[:]))
                nc.vector.tensor_scalar(t_row[:, COMB:TOKEN], slot_e[:], wrec[:], None, ALU.mult)
                step(nc.vector.tensor_scalar(comb, slot_e[:], wrec[:], None, ALU.mult))

            def dve_head(n, r, par, first, last, prep2=True):
                base = 3 if first else tr_base(r)
                if not first:
                    output(r, base)
                if first:
                    for g in range(3):
                        stack_copy(g, 1 - par, base + g)
                elif not last:
                    stack_copy(0, 1 - par, base + 1)
                    norm_stats(r, 1 - par)
                    stack_copy(1, 1 - par, base + 2)
                    norm_square(r, 1 - par)
                    stack_copy(2, 1 - par, base + 3)
                    norm_rows(r, 1 - par)
                    if prep2:
                        prep_squares(n + 2)
                    tT_copy(base + 4)
                    choose(r, base + 5)
                    weigh(r)
                    place(r, 1 - par, base + 6)
                else:
                    norm_stats(r, 1 - par)
                    norm_square(r, 1 - par)
                    norm_rows(r, 1 - par)
                    tT_copy(base + 1)
                    choose(r, base + 2)
                    weigh(r)
                    place(r, 1 - par, base + 3)
                    dve.wait_ge(slots_ready, NT - 1)
                    dve.wait_ge(tr_ready, base + 5)
                    nc.vector.tensor_tensor(slot_e[:], b7[:, 0:E], bucket0[:], ALU.add).then_inc(tr_taken, 1)
                    dve.wait_ge(tr_taken, base + 5)
                    nc.vector.tensor_copy(pad0_i, slot_e[0:1, :]).then_inc(cnt_ready, 1)
                if first:
                    prep_squares(n + 2)
                if not last and prep2:
                    prep(n + 2)

            dve_head(0, None, 0, True, False)
            before = step.n
            with dve.Fori(0, 4) as i:
                for p in (0, 1):
                    step.rebase(i * (2 * DVE_STEPS) + (before + DVE_STEPS * p))
                    dve_head(i * 2 + (1 + p), i * 2 + p, 1 - p, False, False)
                    assert step.n == DVE_STEPS, step.n
            step.rebase(before + 8 * DVE_STEPS)
            dve_head(NT - 3, NT - 4, 1, False, False)
            dve_head(NT - 2, NT - 3, 0, False, False, prep2=False)
            dve_head(NT - 1, NT - 2, 1, False, True)
            base = tr_base(NT - 2) + 5
            output(NT - 1, base)
            norm_stats(NT - 1, 1)
            norm_square(NT - 1, 1)
            norm_rows(NT - 1, 1)
            tT_copy(base + 1)
            choose(NT - 1, base + 2)
            weigh(NT - 1)
            place(NT - 1, 1, base + 3)
            dve.wait_ge(slots_ready, NT)
            dve.wait_ge(tr_ready, base + 5)
            nc.vector.tensor_copy(cnt, b7[:, 0:E]).then_inc(tr_taken, 1)
            dve.wait_ge(tr_taken, base + 5)
            dve.wait_ge(plan_consts, 1)
            step(nc.vector.tensor_tensor(over, cnt.unsqueeze(2).broadcast_to([P, E, NT]),
                                         edges.unsqueeze(1).broadcast_to([P, E, NT]), ALU.is_gt))
            step(nc.vector.reduce_sum(tiles_e, over, AX.X))
            step(nc.vector.tensor_tensor_scan(ends, ones[:, 0:E], tiles_e, 0.0, ALU.mult, ALU.add))
            step(nc.vector.tensor_scalar(done_e, ends, token_no[:, 0:1], None, ALU.is_le))
            step(nc.vector.reduce_sum(ej, done_e, AX.X))
            step(nc.vector.tensor_tensor(done_t, done_e, tiles_e, ALU.mult))
            step(nc.vector.reduce_sum(sj, done_t, AX.X))
            step(nc.vector.tensor_tensor(tmpj, token_no[:, 0:1], sj, ALU.subtract))
            step(nc.vector.tensor_scalar(rowj, ej, float(BUCKET), None, ALU.mult))
            nc.vector.tensor_scalar(plan_cols[:, 0:1], ej, float(E - 1), None, ALU.min)
            nc.vector.scalar_tensor_tensor(plan_cols[:, 1:2], tmpj, float(P), rowj, ALU.mult,
                                           ALU.add).then_inc(plan_cols_ready, 1)
            dve.wait_ge(tr_ready, base + 6)
            nc.vector.tensor_copy(ej_i, b7[0:1, 0:MT])
            nc.vector.tensor_copy(row_i, b7[0:1, P:P + MT]).then_inc(tr_taken, 1)
            dve.wait_ge(tr_taken, base + 6)
            nc.vector.tensor_copy(bank_mark[:], ones[:, 0:1]).then_inc(plan_ready, 1)
            dve.wait_ge(base_ready, NT)
            for t in range(0, NT, 2):
                dve.wait_ge(bias_psum, t // 2 + 1)
                pair = h_res[:, t:t + 2, :].rearrange("p t c -> p (t c)")
                nc.vector.tensor_tensor(pair, pair, bank(BIAS_BANK[t // 2])[:, 0:2 * C], ALU.add).then_inc(bias_added, 1)

            for r in range(2):
                nc.vector.memset(xtT[r][CB:CB + 1, P:2 * P], 1.0).then_inc(xT_ones, 1)

            def clip(j, r):
                dve.wait_ge(h_done, j * 2 + 1)
                if not isinstance(j, int) or j >= 2:
                    dve.wait_ge(actv_ready, j - 1)
                nc.vector.tensor_scalar(glu[r], bank(1 + r)[:, 0:FF], 7.0, None, ALU.min).then_inc(glu_ready, 1)
                dve.wait_ge(h_done, j * 2 + 2)
                nc.vector.tensor_scalar(lin[r], bank(3 + r)[:, 0:FF], -7.0, 7.0, ALU.max, ALU.min).then_inc(lin_ready, 1)
                dve.wait_ge(lin_ready, j + 1)
                nc.vector.scalar_tensor_tensor(prod[r], lin[r], 1.0, glu[r], ALU.add, ALU.mult).then_inc(prod_ready, 1)

            def actT_copy(j, r):
                dve.wait_ge(aT_psum, j + 1)
                nc.vector.tensor_copy(actT[r], bank(5)[:, 0:FF]).then_inc(aT_ready, 1)

            clip(0, 0)
            clip(1, 1)
            actT_copy(0, 0)
            clip(2, 0)
            actT_copy(1, 1)
            clip(3, 1)
            actT_copy(2, 0)
            with dve.Fori(2, MT // 2) as i:
                clip(i * 2, 0)
                actT_copy(i * 2 - 1, 1)
                clip(i * 2 + 1, 1)
                actT_copy(i * 2, 0)
            clip(MT - 1, 0)
            actT_copy(MT - 2, 1)
            actT_copy(MT - 1, 0)


def kernel(**inputs):
    import numpy as np
    import concourse.bacc as bacc
    from concourse import mybir
    from concourse.bass_utils import run_bass_kernel_spmd as run

    a = {k.replace("L0_", ""): np.asarray(v) for k, v in inputs.items()}
    cc = np.ascontiguousarray

    def fold(w, k):
        return cc(np.moveaxis(w.reshape((k, 128) + w.shape[1:]), 0, 1))

    x = a["x"].reshape(4, 32, 16, 8, 16, 8).transpose(0, 1, 3, 5, 2, 4)
    w1 = a["ffn_mlp1_w"].reshape(16, 384, 2, 192).transpose(3, 0, 2, 1).reshape(192, 16 * 768)
    b1 = a["ffn_mlp1_b"].reshape(16, 384, 2).transpose(0, 2, 1).reshape(1, 16 * 768)
    wqv = np.concatenate([a["attn_Wq"].T, a["attn_Wv"].T], 1)
    bqv = np.concatenate([a["attn_bq"], a["attn_bv"]])[None]
    arrays = {
        "patches": cc(x.reshape(4, 128, 16, 256)),
        "conv_w": cc(a["tok_conv_w"].reshape(128, 2048).T.reshape(128, 16, 128)),
        "cols": cc(np.concatenate([a["tok_ln1_g"], a["tok_ln1_b"], a["tok_ln2_g"], a["tok_ln2_b"],
                                   a["tok_lnf_g"][None], a["tok_lnf_b"][None],
                                   a["tok_ff1_b"].reshape(8, 128)], 0).T),
        "rows": cc(np.concatenate([a["tok_conv_b"], a["tok_out_b"].ravel(), a["tok_ff2_b"].ravel(),
                                   a["tok_head_b"]])[None]),
        "qkv_w": cc(a["tok_qkv_w"].transpose(1, 0, 2)),
        "out_w": cc(a["tok_out_w"].reshape(2, 4, 128, 128).transpose(2, 0, 1, 3)),
        "ff1_w": cc(a["tok_ff1_w"].transpose(1, 0, 2)),
        "ff2_w": cc(a["tok_ff2_w"].reshape(2, 4, 128, 128).transpose(2, 0, 1, 3)),
        "head_w": cc(a["tok_head_w"]),
        "txt": cc(a["txt"]),
        "wqv_a": cc(wqv[0:128]),
        "wqv_b": cc(np.concatenate([wqv[128:], bqv], 0)),
        "gate_a": cc(a["ffn_gate_w"].T[0:128]),
        "gate_b": cc(np.concatenate([a["ffn_gate_w"].T[128:], a["ffn_gate_b"][None]], 0)),
        "nscale": cc(a["ffn_norm_scale"][None]),
        "w1_a": cc(w1[0:128]),
        "w1_b": cc(np.concatenate([w1[128:], b1], 0)),
        "w2": cc(fold(a["ffn_mlp2_w"].transpose(2, 0, 1), 3).transpose(0, 2, 1, 3).reshape(128, 16 * 3 * 192)),
        "b2": cc(a["ffn_mlp2_b"]),
    }
    nc = bacc.Bacc("TRN2", target_bir_lowering=False, num_devices=1)
    args = [nc.dram_tensor(n, v.shape, mybir.dt.from_np(v.dtype), kind="ExternalInput").ap() for n, v in arrays.items()]
    f32 = mybir.dt.float32
    out = nc.dram_tensor("out", (DUMP + P, C), f32, kind="ExternalOutput").ap()
    xs = nc.dram_tensor("expert_in", (SPARE + NSPARE * P, RW), f32, kind="Internal").ap()
    fusion_kernel(nc, *args, out, xs)
    r = run(nc, [arrays], core_ids=[0])
    return r.results[0]["out"][0:DUMP].reshape(4, 384, 192)
```
